# Optimizing a Trainium2 kernel written in Bass

```python
import numpy as np
import jax
import jax.numpy as jnp

def _softmax(x, axis=-1):
    return jax.nn.softmax(x, axis=axis)

def _gelu(x):
    return jax.nn.gelu(x, approximate=True)

def _silu(x):
    return jax.nn.silu(x)

def _sigmoid(x):
    return jax.nn.sigmoid(x)

def _layernorm(x, axis=-1, eps=1e-05):
    m = jnp.mean(x, axis=axis, keepdims=True)
    v = jnp.var(x, axis=axis, keepdims=True)
    return (x - m) / jnp.sqrt(v + eps)

def _scatter_add(tgt, idx, src, axis=0):
    return tgt.at[idx].add(src)

def _segment_sum(src, seg, n):
    return jax.ops.segment_sum(src, seg, n)
kernel_name = 'mk_decoder_preln_d4_seqx_r8_24058e'

def setup_inputs(seed: int=0):
    np.random.seed(seed)
    _w = jnp.asarray

    def _rec_inputs():
        import jax
        import jax.numpy as jnp
        _rk = jax.random.key(seed)
        x = -0.0002928 + 1 * jax.random.normal(jax.random.fold_in(_rk, 1), (8, 256, 128), jnp.float32)
        _lenS = 256 - jax.random.randint(jax.random.fold_in(_rk, 7), (8,), 0, max(1, 256 // 4) + 1, jnp.int32)
        _lenS2 = 256 - jax.random.randint(jax.random.fold_in(_rk, 8), (8,), 0, max(1, 256 // 4) + 1, jnp.int32)
        _ctx_1024P = jax.random.normal(jax.random.fold_in(_rk, 11), (8, 16, 128), jnp.float32)
        _ctx_1024c = jax.random.dirichlet(jax.random.fold_in(_rk, 511), 0.3 * jnp.ones((16,), jnp.float32), (8, 256))
        _ctx_1024t = jnp.einsum('bsk,bkd->bsd', _ctx_1024c, _ctx_1024P)
        _ctx_1024t = _ctx_1024t * jax.lax.rsqrt(jnp.mean(jnp.square(_ctx_1024t)) + 1e-12) * 0.953939
        ctx_1024 = -1.39393e-06 + 0.999914 * (_ctx_1024t + 0.3 * jax.random.normal(jax.random.fold_in(_rk, 611), (8, 256, 128), jnp.float32))
        _validS = jnp.arange(256)[None, :] < _lenS[:, None]
        _validS2 = jnp.arange(256)[None, :] < _lenS2[:, None]
        _causal = jnp.tril(jnp.ones((256, 256), dtype=bool))
        mask_Bx1xSxS2_ik1 = jnp.where(jnp.broadcast_to(_validS2[:, None, None, :], (8, 1, 256, 256)), 1, 0).astype(jnp.int32)
        return (x, ctx_1024, mask_Bx1xSxS2_ik1)
    x, ctx_1024, mask_Bx1xSxS2_ik1 = _rec_inputs()

    def _L0_attn_setup():
        import jax, jax.numpy as jnp
        import numpy as np
        B, T, D_MODEL, N_HEADS = (2, 256, 128, 16)
        HEAD_DIM = D_MODEL // N_HEADS
        CODE_SIZE = HEAD_DIM // 4
        key = jax.random.key(seed)
        k1, k2, k3, k4 = jax.random.split(key, 4)
        x = jax.random.normal(k1, (B, T, D_MODEL), dtype=jnp.float32)
        w_qkv = jax.random.normal(k2, (3 * D_MODEL, D_MODEL), dtype=jnp.float32) / np.sqrt(D_MODEL)
        w_out = jax.random.normal(k3, (D_MODEL, D_MODEL), dtype=jnp.float32) / np.sqrt(D_MODEL)
        fc_code = jax.random.normal(k4, (1, N_HEADS, CODE_SIZE, HEAD_DIM), dtype=jnp.float32)
        return {'x': x, 'w_qkv': w_qkv, 'w_out': w_out, 'fc_code': fc_code}
    _L0_attn_all = _L0_attn_setup()
    _L0_attn_in = {k: v for k, v in _L0_attn_all.items() if k in ('w_qkv', 'w_out', 'fc_code')}
    del _L0_attn_all

    def _L0_xattn_setup():
        import jax, jax.numpy as jnp
        import numpy as np
        B, S, E, NH = (2, 256, 128, 4)
        HD = E // NH

        def _mlstm_head(q, k, v, ig, fg, eps=1e-06):
            s, dh = q.shape
            log_f = jax.nn.log_sigmoid(fg)
            cs = jnp.concatenate([jnp.zeros((1, 1), log_f.dtype), jnp.cumsum(log_f, axis=0)], axis=0)
            neg = jnp.asarray(-0.7 * jnp.finfo(cs.dtype).max, cs.dtype)
            log_d = jnp.where(jnp.tri(s, dtype=bool), (cs - cs.T)[1:, 1:] + ig.T, neg)
            m = jnp.max(log_d, axis=-1, keepdims=True)
            d = jnp.exp(log_d - m)
            c = q @ (k.T / jnp.sqrt(dh)) * d
            n = jnp.maximum(jnp.sum(c, axis=-1, keepdims=True), jnp.exp(-m))
            return c / (n + eps) @ v
        key = jax.random.key(seed)
        ks = jax.random.split(key, 8)
        return {'q': jax.random.normal(ks[0], (B, S, E), jnp.float32), 'k': jax.random.normal(ks[1], (B, S, E), jnp.float32), 'v': jax.random.normal(ks[2], (B, S, E), jnp.float32), 'igate_kernel': jax.random.normal(ks[3], (3 * E, NH), jnp.float32) * 0.02, 'igate_bias': jax.random.normal(ks[4], (NH,), jnp.float32) * 0.1, 'fgate_kernel': jax.random.normal(ks[5], (3 * E, NH), jnp.float32) * 0.02, 'fgate_bias': jnp.linspace(3.0, 6.0, NH, dtype=jnp.float32), 'rms_scale': jax.random.normal(ks[6], (HD,), jnp.float32) * 0.02}
    _L0_xattn_all = _L0_xattn_setup()
    _L0_xattn_in = {k: v for k, v in _L0_xattn_all.items() if k in ('igate_kernel', 'igate_bias', 'fgate_kernel', 'fgate_bias', 'rms_scale')}
    del _L0_xattn_all

    def _L0_ffn_setup():
        import jax, jax.numpy as jnp
        import numpy as np
        EPS = 1e-06
        LN_EPS = 1e-05

        def _absmean_core(W):
            gamma = jnp.mean(jnp.abs(W)) + EPS
            Ws = W / gamma
            Wq = jnp.sign(Ws) * jnp.minimum(jnp.round(jnp.abs(Ws)), 1.0)
            return (Wq, gamma)

        @jax.custom_vjp
        def absmean(W):
            return _absmean_core(W)[0]

        def _absmean_fwd(W):
            Wq, gamma = _absmean_core(W)
            return (Wq, gamma)

        def _absmean_bwd(gamma, g):
            return (g / gamma,)
        absmean.defvjp(_absmean_fwd, _absmean_bwd)

        def layernorm(x, w, b, eps=LN_EPS):
            mu = jnp.mean(x, axis=-1, keepdims=True)
            var = jnp.mean((x - mu) ** 2, axis=-1, keepdims=True)
            return (x - mu) * jax.lax.rsqrt(var + eps) * w + b
        key = jax.random.key(seed)
        k1, k2, k3 = jax.random.split(key, 3)
        d, h = (128, 512)
        B, T = (8, 256)
        return {'x': jax.random.normal(k1, (B, T, d), jnp.float32), 'W_fc': jax.random.normal(k2, (h, d), jnp.float32), 'ln_w': jnp.ones((h,), jnp.float32), 'ln_b': jnp.zeros((h,), jnp.float32), 'W_proj': jax.random.normal(k3, (d, h), jnp.float32)}
    _L0_ffn_all = _L0_ffn_setup()
    _L0_ffn_in = {k: v for k, v in _L0_ffn_all.items() if k in ('W_fc', 'ln_w', 'ln_b', 'W_proj')}
    del _L0_ffn_all

    def _L1_attn_setup():
        import jax, jax.numpy as jnp
        import numpy as np
        B, T, D, S, K = (8, 512, 128, 64, 3)
        EPS = 1e-05
        key = jax.random.key(seed)
        ks = jax.random.split(key, 10)

        def lin(k, out_d, in_d):
            s = 1.0 / np.sqrt(in_d)
            return jax.random.uniform(k, (out_d, in_d), jnp.float32, -s, s)
        return {'x': jax.random.normal(ks[0], (B, T, D), jnp.float32), 'norm_w': jnp.ones((D,), jnp.float32), 'norm_b': jnp.zeros((D,), jnp.float32), 'in_w': lin(ks[1], 2 * D, D), 'in_b': jnp.zeros((2 * D,), jnp.float32), 'conv_w': jax.random.normal(ks[2], (D, 1, K), jnp.float32) / np.sqrt(K), 'conv_b': jnp.zeros((D,), jnp.float32), 'dt_w': lin(ks[3], S, D), 'dt_b': jnp.zeros((S,), jnp.float32), 'b_w': lin(ks[4], S, D), 'b_b': jnp.zeros((S,), jnp.float32), 'c_w': lin(ks[5], S, D), 'c_b': jnp.zeros((S,), jnp.float32), 'a_log': jax.random.normal(ks[6], (S,), jnp.float32) * 0.02, 'd': jnp.ones((D,), jnp.float32), 'out_w': lin(ks[7], D, D + S), 'out_b': jnp.zeros((D,), jnp.float32)}
    _L1_attn_all = _L1_attn_setup()
    _L1_attn_in = {k: v for k, v in _L1_attn_all.items() if k in ('norm_w', 'norm_b', 'in_w', 'in_b', 'conv_w', 'conv_b', 'dt_w', 'dt_b', 'b_w', 'b_b', 'c_w', 'c_b', 'a_log', 'd', 'out_w', 'out_b')}
    del _L1_attn_all

    def _L1_xattn_setup():
        import jax, jax.numpy as jnp
        import numpy as np
        N, T, D_KQ, E_KQ, D_V, E_V, H = (2, 256, 128, 128, 128, 128, 16)

        def _shifted_causal_mask(T):
            row = jnp.arange(T)[:, None]
            col = jnp.arange(T)[None, :]
            mask = jnp.where(col < row, 0.0, -jnp.inf).astype(jnp.float32)
            return mask.at[0, 0].set(0.0)
        key = jax.random.key(seed)
        ks = jax.random.split(key, 12)

        def lin(k, fan_in, fan_out):
            return jax.random.normal(k, (fan_in, fan_out), jnp.float32) * (1.0 / np.sqrt(fan_in))
        return {'kq': jax.random.normal(ks[0], (N, T, D_KQ), jnp.float32), 'v': jax.random.normal(ks[1], (N, T, D_V), jnp.float32), 'Wk': lin(ks[2], D_KQ, E_KQ), 'bk': jnp.zeros((E_KQ,), jnp.float32), 'Wq': lin(ks[3], D_KQ, E_KQ), 'bq': jnp.zeros((E_KQ,), jnp.float32), 'Wv': lin(ks[4], D_V, E_V), 'bv': jnp.zeros((E_V,), jnp.float32), 'W1': lin(ks[5], E_V, 4 * E_V), 'b1': jnp.zeros((4 * E_V,), jnp.float32), 'W2': lin(ks[6], 4 * E_V, E_V), 'b2': jnp.zeros((E_V,), jnp.float32)}
    _L1_xattn_all = _L1_xattn_setup()
    _L1_xattn_in = {k: v for k, v in _L1_xattn_all.items() if k in ('Wk', 'bk', 'Wq', 'bq', 'Wv', 'bv', 'W1', 'b1', 'W2', 'b2')}
    del _L1_xattn_all

    def _L1_ffn_setup():
        import jax, jax.numpy as jnp
        import numpy as np
        D = 128
        P = 4
        DEPTH = 5
        FAN = 4
        G = (FAN ** (DEPTH + 1) - 1) // 3
        N_NODES = G * FAN
        HID = P * N_NODES
        key = jax.random.key(seed)
        k0, k1, k2, k3 = jax.random.split(key, 4)
        return {'oldx': jax.random.normal(k0, (2, 256, D), dtype=jnp.float32), 'W_in': jax.random.normal(k1, (HID, D), dtype=jnp.float32) * (1.0 / np.sqrt(D)), 'b_in': jax.random.normal(k2, (HID,), dtype=jnp.float32) * (1.0 / np.sqrt(D)), 'W_out': jax.random.normal(k3, (D, HID), dtype=jnp.float32) * (1.0 / np.sqrt((DEPTH + 1) * P))}
    _L1_ffn_all = _L1_ffn_setup()
    _L1_ffn_in = {k: v for k, v in _L1_ffn_all.items() if k in ('W_in', 'b_in', 'W_out')}
    del _L1_ffn_all

    def _L2_attn_setup():
        import jax, jax.numpy as jnp
        import numpy as np
        B, S, D = (4, 256, 128)
        DK, DV = (128, 128)
        key = jax.random.key(seed)
        ks = jax.random.split(key, 5)
        x = jax.random.normal(ks[0], (B, S, D), dtype=jnp.float32)
        scale = 1.0 / np.sqrt(D)
        Wq = jax.random.normal(ks[1], (D, DK), dtype=jnp.float32) * scale
        Wk = jax.random.normal(ks[2], (D, DK), dtype=jnp.float32) * scale
        Wv = jax.random.normal(ks[3], (D, DV), dtype=jnp.float32) * scale
        Wo = jax.random.normal(ks[4], (DV, DV), dtype=jnp.float32) * (1.0 / np.sqrt(DV))
        return {'x': x, 'Wq': Wq, 'Wk': Wk, 'Wv': Wv, 'Wo': Wo}
    _L2_attn_all = _L2_attn_setup()
    _L2_attn_in = {k: v for k, v in _L2_attn_all.items() if k in ('Wq', 'Wk', 'Wv', 'Wo')}
    del _L2_attn_all

    def _L2_xattn_setup():
        import jax, jax.numpy as jnp
        import numpy as np
        EMBED = 128
        HEADS = 16
        HEAD_DIM = EMBED // HEADS
        N, SEQ = (4, 256)
        key = jax.random.key(seed)
        ks = jax.random.split(key, 9)
        values = jax.random.normal(ks[0], (N, SEQ, EMBED), dtype=jnp.float32)
        keys = jax.random.normal(ks[1], (N, SEQ, EMBED), dtype=jnp.float32)
        query = jax.random.normal(ks[2], (N, SEQ, EMBED), dtype=jnp.float32)
        mask = jax.random.randint(ks[3], (N, 1, SEQ, SEQ), 0, 2, dtype=jnp.int32)
        s_h = 1.0 / np.sqrt(HEAD_DIM)
        s_e = 1.0 / np.sqrt(EMBED)
        Wv = jax.random.normal(ks[4], (HEAD_DIM, HEAD_DIM), dtype=jnp.float32) * s_h
        Wk = jax.random.normal(ks[5], (HEAD_DIM, HEAD_DIM), dtype=jnp.float32) * s_h
        Wq = jax.random.normal(ks[6], (HEAD_DIM, HEAD_DIM), dtype=jnp.float32) * s_h
        Wo = jax.random.normal(ks[7], (EMBED, EMBED), dtype=jnp.float32) * s_e
        bo = jax.random.normal(ks[8], (EMBED,), dtype=jnp.float32) * 0.01
        return {'values': values, 'keys': keys, 'query': query, 'mask': mask, 'Wv': Wv, 'Wk': Wk, 'Wq': Wq, 'Wo': Wo, 'bo': bo}
    _L2_xattn_all = _L2_xattn_setup()
    _L2_xattn_in = {k: v for k, v in _L2_xattn_all.items() if k in ('Wv', 'Wk', 'Wq', 'Wo', 'bo')}
    del _L2_xattn_all

    def _L2_ffn_setup():
        import jax, jax.numpy as jnp
        import numpy as np
        D = 128
        H = 256
        E = 8
        TOP_K = 2
        N_SHARED = 1
        B, S = (2, 128)
        key = jax.random.key(seed)
        ks = jax.random.split(key, 12)
        sc = 0.02
        return {'hidden': jax.random.normal(ks[0], (B, S, D), jnp.float32), 'router_w': jax.random.normal(ks[1], (D, E), jnp.float32) * sc, 'router_b': jnp.zeros((E,), jnp.float32), 'sw1': jax.random.normal(ks[2], (D, H), jnp.float32) * sc, 'sb1': jnp.zeros((H,), jnp.float32), 'sw2': jax.random.normal(ks[3], (H, D), jnp.float32) * sc, 'sb2': jnp.zeros((D,), jnp.float32), 'rw1': jax.random.normal(ks[4], (E, D, H), jnp.float32) * sc, 'rb1': jnp.zeros((E, H), jnp.float32), 'rw2': jax.random.normal(ks[5], (E, H, D), jnp.float32) * sc, 'rb2': jnp.zeros((E, D), jnp.float32)}
    _L2_ffn_all = _L2_ffn_setup()
    _L2_ffn_in = {k: v for k, v in _L2_ffn_all.items() if k in ('router_w', 'router_b', 'sw1', 'sb1', 'sw2', 'sb2', 'rw1', 'rb1', 'rw2', 'rb2')}
    del _L2_ffn_all

    def _L3_attn_setup():
        import math
        import jax, jax.numpy as jnp
        import numpy as np
        N_HEAD = 16

        def _reference_tuple_inner(x, W_dq, W_uq, W_dkv, W_uk, W_uv, W_o):
            B, T, C = x.shape
            nh = N_HEAD
            hs = C // nh
            kvl = W_dkv.shape[0]
            k_eff = (W_dq.T @ W_uq.T @ W_uk).reshape(nh, hs, kvl)
            v_eff = (W_uv.T @ W_o.T).reshape(kvl, nh, hs).transpose(1, 0, 2)
            c_kv = x @ W_dkv.T
            q = (x @ W_dq.T @ W_uq.T).reshape(B, T, nh, hs).transpose(0, 2, 1, 3)
            q_lat = jnp.einsum('bhtd,hdl->bhtl', q, k_eff)
            attn = jnp.einsum('bhtl,bsl->bhts', q_lat, c_kv) / math.sqrt(hs)
            causal_mask = jnp.triu(jnp.ones((T, T), bool), k=1)
            attn = jnp.where(causal_mask[None, None], -jnp.inf, attn)
            attn = jax.nn.softmax(attn, axis=-1)
            ctx = jnp.einsum('bhts,bsl->bhtl', attn, c_kv)
            y = jnp.einsum('bhtl,hld->bhtd', ctx, v_eff).transpose(0, 2, 1, 3).reshape(B, T, C)
            return (y, c_kv)
        key = jax.random.key(seed)
        ks = jax.random.split(key, 7)
        B, T, C = (4, 256, 128)
        QL, KVL = (32, 32)
        s = 0.02
        return {'x': jax.random.normal(ks[0], (B, T, C), jnp.float32), 'W_dq': jax.random.normal(ks[1], (QL, C), jnp.float32) * s, 'W_uq': jax.random.normal(ks[2], (C, QL), jnp.float32) * s, 'W_dkv': jax.random.normal(ks[3], (KVL, C), jnp.float32) * s, 'W_uk': jax.random.normal(ks[4], (C, KVL), jnp.float32) * s, 'W_uv': jax.random.normal(ks[5], (C, KVL), jnp.float32) * s, 'W_o': jax.random.normal(ks[6], (C, C), jnp.float32) * s}
    _L3_attn_all = _L3_attn_setup()
    _L3_attn_in = {k: v for k, v in _L3_attn_all.items() if k in ('W_dq', 'W_uq', 'W_dkv', 'W_uk', 'W_uv', 'W_o')}
    del _L3_attn_all

    def _L3_xattn_setup():
        import jax, jax.numpy as jnp
        import numpy as np
        E = 128
        NUM_HEADS = 16
        DK = E // NUM_HEADS
        EPS = 1e-05
        NEG_INF = -jnp.inf

        def layer_norm(x, g, b):
            mu = jnp.mean(x, axis=-1, keepdims=True)
            var = jnp.var(x, axis=-1, keepdims=True)
            return (x - mu) * jax.lax.rsqrt(var + EPS) * g + b

        def self_attn(x, Wq, Wk, Wv):
            Q, K, V = (x @ Wq, x @ Wk, x @ Wv)
            energy = jnp.einsum('bqd,bkd->bqk', Q, K)
            S = energy.shape[-1]
            lengths = jnp.sum(energy[:, 0] != 0, axis=-1)
            kidx = jnp.arange(S)
            pad = kidx[None, None, :] >= lengths[:, None, None]
            causal = kidx[None, :] < kidx[:, None]
            causal = (kidx[None, :] > kidx[:, None])[None]
            energy = jnp.where(pad | causal, NEG_INF, energy)
            score = jax.nn.softmax(energy / np.sqrt(DK), axis=-1)
            return jnp.einsum('bqk,bkd->bqd', score, V)

        def cross_attn(x, context, Wq, Wk, Wv):
            Q = x @ Wq
            K, V = (context @ Wk, context @ Wv)
            energy = jnp.einsum('bqd,bkd->bqk', Q, K)
            Sk = energy.shape[-1]
            lengths = jnp.sum(energy[:, 0] != 0, axis=-1)
            kidx = jnp.arange(Sk)
            pad = kidx[None, None, :] >= lengths[:, None, None]
            energy = jnp.where(pad, NEG_INF, energy)
            score = jax.nn.softmax(energy / np.sqrt(DK), axis=-1)
            return jnp.einsum('bqk,bkd->bqd', score, V)
        key = jax.random.key(seed)
        ks = jax.random.split(key, 12)
        B, S = (8, 256)
        s = 1.0 / np.sqrt(E)
        inp = {'x': jax.random.normal(ks[0], (B, S, E), jnp.float32), 'context': jax.random.normal(ks[1], (B, S, E), jnp.float32), 'Wq1': jax.random.normal(ks[2], (E, E), jnp.float32) * s, 'Wk1': jax.random.normal(ks[3], (E, E), jnp.float32) * s, 'Wv1': jax.random.normal(ks[4], (E, E), jnp.float32) * s, 'Wq2': jax.random.normal(ks[5], (E, E), jnp.float32) * s, 'Wk2': jax.random.normal(ks[6], (E, E), jnp.float32) * s, 'Wv2': jax.random.normal(ks[7], (E, E), jnp.float32) * s, 'fc1_w': jax.random.normal(ks[8], (E, E), jnp.float32) * s, 'fc1_b': jnp.zeros((E,), jnp.float32), 'fc2_w': jax.random.normal(ks[9], (E, E), jnp.float32) * s, 'fc2_b': jnp.zeros((E,), jnp.float32), 'ln1_g': jnp.ones((E,), jnp.float32), 'ln1_b': jnp.zeros((E,), jnp.float32), 'ln2_g': jnp.ones((E,), jnp.float32), 'ln2_b': jnp.zeros((E,), jnp.float32), 'ln3_g': jnp.ones((E,), jnp.float32), 'ln3_b': jnp.zeros((E,), jnp.float32)}
        return inp
    _L3_xattn_all = _L3_xattn_setup()
    _L3_xattn_in = {k: v for k, v in _L3_xattn_all.items() if k in ('Wq1', 'Wk1', 'Wv1', 'Wq2', 'Wk2', 'Wv2', 'fc1_w', 'fc1_b', 'fc2_w', 'fc2_b', 'ln1_g', 'ln1_b', 'ln2_g', 'ln2_b', 'ln3_g', 'ln3_b')}
    del _L3_xattn_all

    def _L3_ffn_setup():
        import jax, jax.numpy as jnp
        import numpy as np
        B, T, C = (2, 256, 128)
        H, D = (16, 64)
        CR = 8
        R = C // CR
        ROPE = D // 2
        NOPE = D - ROPE
        E, K, I, S = (8, 2, 64, 1)
        THETA = 100000.0
        EPS = 1e-05

        def _rmsnorm(x, w):
            rms = jnp.sqrt(jnp.mean(x * x, axis=-1, keepdims=True) + EPS)
            return w * (x / rms)

        def _rope(xh):
            d = xh.shape[-1]
            t = jnp.arange(xh.shape[2], dtype=jnp.float32)
            freqs = 1.0 / THETA ** (jnp.arange(0, d, 2, dtype=jnp.float32) / d)
            ang = jnp.outer(t, freqs)
            cos, sin = (jnp.cos(ang), jnp.sin(ang))
            xr = xh.reshape(xh.shape[:-1] + (d // 2, 2))
            x0, x1 = (xr[..., 0], xr[..., 1])
            rot = jnp.stack([x0 * cos - x1 * sin, x0 * sin + x1 * cos], axis=-1)
            return rot.reshape(xh.shape)

        def _attention(x, Wq, Wkva, Wkvb, Wo):
            b, t, _ = x.shape
            q = (x @ Wq).reshape(b, t, H, D).transpose(0, 2, 1, 3)
            ckv = x @ Wkva
            kv_latent, k_rope = (ckv[:, :, :R], ckv[:, :, R:])
            kv = (kv_latent @ Wkvb).reshape(b, t, H, NOPE).transpose(0, 2, 1, 3)
            k_rope = jnp.broadcast_to(k_rope[:, None, :, :], (b, H, t, ROPE))
            q_nope, q_rope = (q[..., :NOPE], q[..., NOPE:])
            q = jnp.concatenate([q_nope, _rope(q_rope)], axis=-1)
            k = jnp.concatenate([kv, _rope(k_rope)], axis=-1)
            v = jnp.concatenate([kv, jnp.zeros_like(k_rope)], axis=-1)
            att = jnp.einsum('bhqd,bhkd->bhqk', q, k) / jnp.sqrt(jnp.float32(D))
            mask = jnp.tril(jnp.ones((t, t), dtype=bool))
            att = jnp.where(mask, att, jnp.float32(-jnp.inf))
            att = jax.nn.softmax(att, axis=-1)
            y = jnp.einsum('bhqk,bhkd->bhqd', att, v)
            y = y.transpose(0, 2, 1, 3).reshape(b, t, H * D)
            return y @ Wo

        def _experts(x_flat, Wg, Wu, Wd):
            g = jax.nn.silu(jnp.einsum('nc,eci->nei', x_flat, Wg))
            u = jnp.einsum('nc,eci->nei', x_flat, Wu)
            return jnp.einsum('nei,eic->nec', g * u, Wd)

        def _moe(x, Wgate, expert_bias, Wg, Wu, Wd, sWg, sWu, sWd):
            b, t, c = x.shape
            xf = x.reshape(-1, c)
            shared = jnp.mean(_experts(xf, sWg, sWu, sWd), axis=1)
            logits = xf @ Wgate + expert_bias
            probs = jax.nn.softmax(logits, axis=-1)
            topk_p, topk_i = jax.lax.top_k(probs, K)
            topk_p = topk_p / jnp.sum(topk_p, axis=-1, keepdims=True)
            comb = jnp.sum(jax.nn.one_hot(topk_i, E, dtype=xf.dtype) * topk_p[..., None], axis=1)
            routed = jnp.einsum('ne,nec->nc', comb, _experts(xf, Wg, Wu, Wd))
            return (shared + routed).reshape(b, t, c)
        key = jax.random.key(seed)
        ks = jax.random.split(key, 16)
        w = lambda k, shp: jax.random.normal(k, shp, dtype=jnp.float32) * 0.02
        return {'x': jax.random.normal(ks[0], (B, T, C), dtype=jnp.float32), 'w_ln1': jnp.ones((C,), jnp.float32), 'Wq': w(ks[1], (C, H * D)), 'Wkva': w(ks[2], (C, R + ROPE)), 'Wkvb': w(ks[3], (R, H * NOPE)), 'Wo': w(ks[4], (H * D, C)), 'w_ln2': jnp.ones((C,), jnp.float32), 'Wgate': w(ks[5], (C, E)), 'expert_bias': jnp.zeros((E,), jnp.float32), 'Wg': w(ks[6], (E, C, I)), 'Wu': w(ks[7], (E, C, I)), 'Wd': w(ks[8], (E, I, C)), 'sWg': w(ks[9], (S, C, I)), 'sWu': w(ks[10], (S, C, I)), 'sWd': w(ks[11], (S, I, C))}
    _L3_ffn_all = _L3_ffn_setup()
    _L3_ffn_in = {k: v for k, v in _L3_ffn_all.items() if k in ('w_ln1', 'Wq', 'Wkva', 'Wkvb', 'Wo', 'w_ln2', 'Wgate', 'expert_bias', 'Wg', 'Wu', 'Wd', 'sWg', 'sWu', 'sWd')}
    del _L3_ffn_all
    return {'x': x, 'ctx_1024': ctx_1024, 'mask_Bx1xSxS2_ik1': mask_Bx1xSxS2_ik1, 'L0_attn_w_qkv': _L0_attn_in['w_qkv'], 'L0_attn_w_out': _L0_attn_in['w_out'], 'L0_attn_fc_code': _L0_attn_in['fc_code'], 'L0_xattn_igate_kernel': _L0_xattn_in['igate_kernel'], 'L0_xattn_igate_bias': _L0_xattn_in['igate_bias'], 'L0_xattn_fgate_kernel': _L0_xattn_in['fgate_kernel'], 'L0_xattn_fgate_bias': _L0_xattn_in['fgate_bias'], 'L0_xattn_rms_scale': _L0_xattn_in['rms_scale'], 'L0_ffn_W_fc': _L0_ffn_in['W_fc'], 'L0_ffn_ln_w': _L0_ffn_in['ln_w'], 'L0_ffn_ln_b': _L0_ffn_in['ln_b'], 'L0_ffn_W_proj': _L0_ffn_in['W_proj'], 'L1_attn_norm_w': _L1_attn_in['norm_w'], 'L1_attn_norm_b': _L1_attn_in['norm_b'], 'L1_attn_in_w': _L1_attn_in['in_w'], 'L1_attn_in_b': _L1_attn_in['in_b'], 'L1_attn_conv_w': _L1_attn_in['conv_w'], 'L1_attn_conv_b': _L1_attn_in['conv_b'], 'L1_attn_dt_w': _L1_attn_in['dt_w'], 'L1_attn_dt_b': _L1_attn_in['dt_b'], 'L1_attn_b_w': _L1_attn_in['b_w'], 'L1_attn_b_b': _L1_attn_in['b_b'], 'L1_attn_c_w': _L1_attn_in['c_w'], 'L1_attn_c_b': _L1_attn_in['c_b'], 'L1_attn_a_log': _L1_attn_in['a_log'], 'L1_attn_d': _L1_attn_in['d'], 'L1_attn_out_w': _L1_attn_in['out_w'], 'L1_attn_out_b': _L1_attn_in['out_b'], 'L1_xattn_Wk': _L1_xattn_in['Wk'], 'L1_xattn_bk': _L1_xattn_in['bk'], 'L1_xattn_Wq': _L1_xattn_in['Wq'], 'L1_xattn_bq': _L1_xattn_in['bq'], 'L1_xattn_Wv': _L1_xattn_in['Wv'], 'L1_xattn_bv': _L1_xattn_in['bv'], 'L1_xattn_W1': _L1_xattn_in['W1'], 'L1_xattn_b1': _L1_xattn_in['b1'], 'L1_xattn_W2': _L1_xattn_in['W2'], 'L1_xattn_b2': _L1_xattn_in['b2'], 'L1_ffn_W_in': _L1_ffn_in['W_in'], 'L1_ffn_b_in': _L1_ffn_in['b_in'], 'L1_ffn_W_out': _L1_ffn_in['W_out'], 'L2_attn_Wq': _L2_attn_in['Wq'], 'L2_attn_Wk': _L2_attn_in['Wk'], 'L2_attn_Wv': _L2_attn_in['Wv'], 'L2_attn_Wo': _L2_attn_in['Wo'], 'L2_xattn_Wv': _L2_xattn_in['Wv'], 'L2_xattn_Wk': _L2_xattn_in['Wk'], 'L2_xattn_Wq': _L2_xattn_in['Wq'], 'L2_xattn_Wo': _L2_xattn_in['Wo'], 'L2_xattn_bo': _L2_xattn_in['bo'], 'L2_ffn_router_w': _L2_ffn_in['router_w'], 'L2_ffn_router_b': _L2_ffn_in['router_b'], 'L2_ffn_sw1': _L2_ffn_in['sw1'], 'L2_ffn_sb1': _L2_ffn_in['sb1'], 'L2_ffn_sw2': _L2_ffn_in['sw2'], 'L2_ffn_sb2': _L2_ffn_in['sb2'], 'L2_ffn_rw1': _L2_ffn_in['rw1'], 'L2_ffn_rb1': _L2_ffn_in['rb1'], 'L2_ffn_rw2': _L2_ffn_in['rw2'], 'L2_ffn_rb2': _L2_ffn_in['rb2'], 'L3_attn_W_dq': _L3_attn_in['W_dq'], 'L3_attn_W_uq': _L3_attn_in['W_uq'], 'L3_attn_W_dkv': _L3_attn_in['W_dkv'], 'L3_attn_W_uk': _L3_attn_in['W_uk'], 'L3_attn_W_uv': _L3_attn_in['W_uv'], 'L3_attn_W_o': _L3_attn_in['W_o'], 'L3_xattn_Wq1': _L3_xattn_in['Wq1'], 'L3_xattn_Wk1': _L3_xattn_in['Wk1'], 'L3_xattn_Wv1': _L3_xattn_in['Wv1'], 'L3_xattn_Wq2': _L3_xattn_in['Wq2'], 'L3_xattn_Wk2': _L3_xattn_in['Wk2'], 'L3_xattn_Wv2': _L3_xattn_in['Wv2'], 'L3_xattn_fc1_w': _L3_xattn_in['fc1_w'], 'L3_xattn_fc1_b': _L3_xattn_in['fc1_b'], 'L3_xattn_fc2_w': _L3_xattn_in['fc2_w'], 'L3_xattn_fc2_b': _L3_xattn_in['fc2_b'], 'L3_xattn_ln1_g': _L3_xattn_in['ln1_g'], 'L3_xattn_ln1_b': _L3_xattn_in['ln1_b'], 'L3_xattn_ln2_g': _L3_xattn_in['ln2_g'], 'L3_xattn_ln2_b': _L3_xattn_in['ln2_b'], 'L3_xattn_ln3_g': _L3_xattn_in['ln3_g'], 'L3_xattn_ln3_b': _L3_xattn_in['ln3_b'], 'L3_ffn_w_ln1': _L3_ffn_in['w_ln1'], 'L3_ffn_Wq': _L3_ffn_in['Wq'], 'L3_ffn_Wkva': _L3_ffn_in['Wkva'], 'L3_ffn_Wkvb': _L3_ffn_in['Wkvb'], 'L3_ffn_Wo': _L3_ffn_in['Wo'], 'L3_ffn_w_ln2': _L3_ffn_in['w_ln2'], 'L3_ffn_Wgate': _L3_ffn_in['Wgate'], 'L3_ffn_expert_bias': _L3_ffn_in['expert_bias'], 'L3_ffn_Wg': _L3_ffn_in['Wg'], 'L3_ffn_Wu': _L3_ffn_in['Wu'], 'L3_ffn_Wd': _L3_ffn_in['Wd'], 'L3_ffn_sWg': _L3_ffn_in['sWg'], 'L3_ffn_sWu': _L3_ffn_in['sWu'], 'L3_ffn_sWd': _L3_ffn_in['sWd']}

def reference(x, ctx_1024, mask_Bx1xSxS2_ik1, L0_attn_w_qkv, L0_attn_w_out, L0_attn_fc_code, L0_xattn_igate_kernel, L0_xattn_igate_bias, L0_xattn_fgate_kernel, L0_xattn_fgate_bias, L0_xattn_rms_scale, L0_ffn_W_fc, L0_ffn_ln_w, L0_ffn_ln_b, L0_ffn_W_proj, L1_attn_norm_w, L1_attn_norm_b, L1_attn_in_w, L1_attn_in_b, L1_attn_conv_w, L1_attn_conv_b, L1_attn_dt_w, L1_attn_dt_b, L1_attn_b_w, L1_attn_b_b, L1_attn_c_w, L1_attn_c_b, L1_attn_a_log, L1_attn_d, L1_attn_out_w, L1_attn_out_b, L1_xattn_Wk, L1_xattn_bk, L1_xattn_Wq, L1_xattn_bq, L1_xattn_Wv, L1_xattn_bv, L1_xattn_W1, L1_xattn_b1, L1_xattn_W2, L1_xattn_b2, L1_ffn_W_in, L1_ffn_b_in, L1_ffn_W_out, L2_attn_Wq, L2_attn_Wk, L2_attn_Wv, L2_attn_Wo, L2_xattn_Wv, L2_xattn_Wk, L2_xattn_Wq, L2_xattn_Wo, L2_xattn_bo, L2_ffn_router_w, L2_ffn_router_b, L2_ffn_sw1, L2_ffn_sb1, L2_ffn_sw2, L2_ffn_sb2, L2_ffn_rw1, L2_ffn_rb1, L2_ffn_rw2, L2_ffn_rb2, L3_attn_W_dq, L3_attn_W_uq, L3_attn_W_dkv, L3_attn_W_uk, L3_attn_W_uv, L3_attn_W_o, L3_xattn_Wq1, L3_xattn_Wk1, L3_xattn_Wv1, L3_xattn_Wq2, L3_xattn_Wk2, L3_xattn_Wv2, L3_xattn_fc1_w, L3_xattn_fc1_b, L3_xattn_fc2_w, L3_xattn_fc2_b, L3_xattn_ln1_g, L3_xattn_ln1_b, L3_xattn_ln2_g, L3_xattn_ln2_b, L3_xattn_ln3_g, L3_xattn_ln3_b, L3_ffn_w_ln1, L3_ffn_Wq, L3_ffn_Wkva, L3_ffn_Wkvb, L3_ffn_Wo, L3_ffn_w_ln2, L3_ffn_Wgate, L3_ffn_expert_bias, L3_ffn_Wg, L3_ffn_Wu, L3_ffn_Wd, L3_ffn_sWg, L3_ffn_sWu, L3_ffn_sWd):
    import jax
    import jax.numpy as jnp

    def _L0_attn_ref(x, w_qkv, w_out, fc_code):
        import jax, jax.numpy as jnp
        import numpy as np
        B, T, D_MODEL, N_HEADS = (2, 256, 128, 16)
        HEAD_DIM = D_MODEL // N_HEADS
        CODE_SIZE = HEAD_DIM // 4
        Bx, Tx, _ = x.shape
        scale = HEAD_DIM ** (-0.5)
        qkv = x @ w_qkv.T
        qkv = qkv.reshape(Bx, Tx, 3 * N_HEADS, HEAD_DIM).transpose(0, 2, 1, 3)
        q, k, v = (qkv[:, :N_HEADS], qkv[:, N_HEADS:2 * N_HEADS], qkv[:, 2 * N_HEADS:])
        code = fc_code[0]
        q = jnp.einsum('bhtd,hcd->bhtc', q, code) * scale
        k = jnp.einsum('bhtd,hcd->bhtc', k, code) * scale
        q = jax.nn.softmax(q, axis=-1) * scale
        k_exp = jnp.exp(k - jnp.max(k, axis=2, keepdims=True))
        k_exp_cumsum = jnp.cumsum(k_exp, axis=2)
        kv_cumsum = jnp.cumsum(jnp.einsum('bhtc,bhtd->bhtcd', k_exp, v), axis=2)
        kv = kv_cumsum / (k_exp_cumsum[..., None] + 1e-09)
        xo = jnp.einsum('bhtc,bhtcd->bhtd', q, kv)
        xo = xo.transpose(0, 2, 1, 3).reshape(Bx, Tx, D_MODEL)
        return xo @ w_out.T

    def _L0_xattn_ref(q, k, v, igate_kernel, igate_bias, fgate_kernel, fgate_bias, rms_scale):
        import jax, jax.numpy as jnp
        import numpy as np
        B, S, E, NH = (2, 256, 128, 4)
        HD = E // NH

        def _mlstm_head(q, k, v, ig, fg, eps=1e-06):
            s, dh = q.shape
            log_f = jax.nn.log_sigmoid(fg)
            cs = jnp.concatenate([jnp.zeros((1, 1), log_f.dtype), jnp.cumsum(log_f, axis=0)], axis=0)
            neg = jnp.asarray(-0.7 * jnp.finfo(cs.dtype).max, cs.dtype)
            log_d = jnp.where(jnp.tri(s, dtype=bool), (cs - cs.T)[1:, 1:] + ig.T, neg)
            m = jnp.max(log_d, axis=-1, keepdims=True)
            d = jnp.exp(log_d - m)
            c = q @ (k.T / jnp.sqrt(dh)) * d
            n = jnp.maximum(jnp.sum(c, axis=-1, keepdims=True), jnp.exp(-m))
            return c / (n + eps) @ v
        b, s, e = q.shape
        nh = igate_kernel.shape[1]
        hd = e // nh
        gate_in = jnp.concatenate((q, k, v), axis=-1)
        ig = (gate_in @ igate_kernel + igate_bias).swapaxes(-1, -2)[..., None]
        fg = (gate_in @ fgate_kernel + fgate_bias).swapaxes(-1, -2)[..., None]
        qh = q.reshape(b, s, nh, hd).swapaxes(1, 2)
        kh = k.reshape(b, s, nh, hd).swapaxes(1, 2)
        vh = v.reshape(b, s, nh, hd).swapaxes(1, 2)
        h = jax.vmap(jax.vmap(_mlstm_head))(qh, kh, vh, ig, fg)
        var = jnp.mean(jnp.square(h.astype(jnp.float32)), axis=-1, keepdims=True)
        h = (h * jax.lax.rsqrt(var + 1e-06)).astype(h.dtype) * (1.0 + rms_scale)
        return h.swapaxes(1, 2).reshape(b, s, e)

    def _L0_ffn_ref(x, W_fc, ln_w, ln_b, W_proj):
        import jax, jax.numpy as jnp
        import numpy as np
        EPS = 1e-06
        LN_EPS = 1e-05

        def _absmean_core(W):
            gamma = jnp.mean(jnp.abs(W)) + EPS
            Ws = W / gamma
            Wq = jnp.sign(Ws) * jnp.minimum(jnp.round(jnp.abs(Ws)), 1.0)
            return (Wq, gamma)

        @jax.custom_vjp
        def absmean(W):
            return _absmean_core(W)[0]

        def _absmean_fwd(W):
            Wq, gamma = _absmean_core(W)
            return (Wq, gamma)

        def _absmean_bwd(gamma, g):
            return (g / gamma,)
        absmean.defvjp(_absmean_fwd, _absmean_bwd)

        def layernorm(x, w, b, eps=LN_EPS):
            mu = jnp.mean(x, axis=-1, keepdims=True)
            var = jnp.mean((x - mu) ** 2, axis=-1, keepdims=True)
            return (x - mu) * jax.lax.rsqrt(var + eps) * w + b
        h = jnp.einsum('btd,hd->bth', x, absmean(W_fc))
        h = jax.nn.gelu(h, approximate=False)
        h = layernorm(h, ln_w, ln_b)
        return jnp.einsum('bth,dh->btd', h, absmean(W_proj))

    def _L1_attn_ref(x, norm_w, norm_b, in_w, in_b, conv_w, conv_b, dt_w, dt_b, b_w, b_b, c_w, c_b, a_log, d, out_w, out_b):
        import jax, jax.numpy as jnp
        import numpy as np
        B, T, D, S, K = (8, 512, 128, 64, 3)
        EPS = 1e-05
        bsz, tlen, dim = x.shape
        sdim = a_log.shape[0]
        k = conv_w.shape[-1]
        residual = x
        mu = jnp.mean(x, axis=-1, keepdims=True)
        var = jnp.mean(jnp.square(x - mu), axis=-1, keepdims=True)
        xn = (x - mu) * jax.lax.rsqrt(var + EPS) * norm_w + norm_b
        h = xn @ in_w.T + in_b
        x_proj, z = jnp.split(h, 2, axis=-1)
        xc = jax.lax.conv_general_dilated(x_proj.transpose(0, 2, 1), conv_w, (1,), [(k // 2, k // 2)], dimension_numbers=('NCH', 'OIH', 'NCH'), feature_group_count=dim)
        x_conv = jnp.tanh((xc + conv_b[None, :, None]).transpose(0, 2, 1))
        dt = jax.nn.softplus(z @ dt_w.T + dt_b) + 0.0001
        b = jnp.tanh(z @ b_w.T + b_b)
        c = jnp.tanh(z @ c_w.T + c_b)
        a = -jnp.exp(a_log)
        decay = jnp.exp(a * dt)

        def step(state, inp):
            dec_t, b_t = inp
            state = state * dec_t + b_t
            return (state, state)
        _, states = jax.lax.scan(step, jnp.zeros((bsz, sdim), x.dtype), (decay.transpose(1, 0, 2), b.transpose(1, 0, 2)))
        states = states.transpose(1, 0, 2)
        y = c * states
        mix = jnp.concatenate([x_conv * d, y], axis=-1)
        out = mix @ out_w.T + out_b
        return residual + out

    def _L1_xattn_ref(kq, v, Wk, bk, Wq, bq, Wv, bv, W1, b1, W2, b2):
        import jax, jax.numpy as jnp
        import numpy as np
        N, T, D_KQ, E_KQ, D_V, E_V, H = (2, 256, 128, 128, 128, 128, 16)

        def _shifted_causal_mask(T):
            row = jnp.arange(T)[:, None]
            col = jnp.arange(T)[None, :]
            mask = jnp.where(col < row, 0.0, -jnp.inf).astype(jnp.float32)
            return mask.at[0, 0].set(0.0)
        n, T, _ = kq.shape
        hd_kq = E_KQ // H
        hd_v = E_V // H
        k = (kq @ Wk + bk).reshape(n, T, H, hd_kq).transpose(0, 2, 1, 3)
        q = (kq @ Wq + bq).reshape(n, T, H, hd_kq).transpose(0, 2, 1, 3)
        vv = (v @ Wv + bv).reshape(n, T, H, hd_v).transpose(0, 2, 1, 3)
        scores = jnp.einsum('bhqd,bhkd->bhqk', q, k) + _shifted_causal_mask(T)
        attn = jax.nn.softmax(scores, axis=-1)
        out = jnp.einsum('bhqk,bhkd->bhqd', attn, vv)
        out = out.transpose(0, 2, 1, 3).reshape(n, T, E_V)
        h = jax.nn.gelu(out @ W1 + b1, approximate=False)
        return h @ W2 + b2

    def _L1_ffn_ref(oldx, W_in, b_in, W_out):
        import jax, jax.numpy as jnp
        import numpy as np
        D = 128
        P = 4
        DEPTH = 5
        FAN = 4
        G = (FAN ** (DEPTH + 1) - 1) // 3
        N_NODES = G * FAN
        HID = P * N_NODES
        x = oldx.reshape(-1, D)
        B = x.shape[0]
        logits = x @ W_in.T + b_in
        act = jax.nn.gelu(logits, approximate=False)
        act4 = act.reshape(B, P, G, FAN)
        decisions = jnp.argmax(act4, axis=-1)
        current = jnp.zeros((B, P), dtype=jnp.int32)
        nodes = [current]
        platform = 0
        for d in range(DEPTH):
            moves = jnp.take_along_axis(decisions, current[..., None].astype(jnp.int64), axis=2)[..., 0].astype(jnp.int32)
            next_platform = platform + FAN ** d
            current = next_platform + FAN * (current - platform) + moves
            nodes.append(current)
            platform = next_platform
        mask = sum((jax.nn.one_hot(n, G, dtype=act4.dtype) for n in nodes))
        mask = jax.lax.stop_gradient(mask)
        masked = act4 * mask[..., None]
        new_logits = masked.reshape(B, HID) @ W_out.T
        return new_logits.reshape(oldx.shape)

    def _L2_attn_ref(x, Wq, Wk, Wv, Wo):
        import jax, jax.numpy as jnp
        import numpy as np
        B, S, D = (4, 256, 128)
        DK, DV = (128, 128)
        dim_k = Wq.shape[1]
        q = x @ Wq
        k = x @ Wk
        v = x @ Wv
        scores = jnp.einsum('bsd,btd->bst', q, k)
        m_inf = -jnp.finfo(scores.dtype).max
        causal_mask = jnp.triu(jnp.ones((q.shape[1], q.shape[1]), dtype=bool), k=1)
        scores = jnp.where(causal_mask[None, :, :], m_inf, scores)
        attn = jax.nn.softmax(scores * dim_k ** (-0.5), axis=-1)
        out = jnp.einsum('bst,btv->bsv', attn, v) @ Wo
        return out

    def _L2_xattn_ref(values, keys, query, mask, Wv, Wk, Wq, Wo, bo):
        import jax, jax.numpy as jnp
        import numpy as np
        EMBED = 128
        HEADS = 16
        HEAD_DIM = EMBED // HEADS
        N, SEQ = (4, 256)
        n, q_len = (query.shape[0], query.shape[1])
        k_len, v_len = (keys.shape[1], values.shape[1])
        v = values.reshape(n, v_len, HEADS, HEAD_DIM)
        k = keys.reshape(n, k_len, HEADS, HEAD_DIM)
        q = query.reshape(n, q_len, HEADS, HEAD_DIM)
        v = jnp.einsum('nlhd,ed->nlhe', v, Wv)
        k = jnp.einsum('nlhd,ed->nlhe', k, Wk)
        q = jnp.einsum('nlhd,ed->nlhe', q, Wq)
        energy = jnp.einsum('nqhd,nkhd->nhqk', q, k)
        energy = jnp.where(mask == 0, jnp.float32(-1e+20), energy)
        attention = jax.nn.softmax(energy / jnp.sqrt(jnp.float32(EMBED)), axis=3)
        out = jnp.einsum('nhql,nlhd->nqhd', attention, v).reshape(n, q_len, EMBED)
        return out @ Wo.T + bo

    def _L2_ffn_ref(hidden, router_w, router_b, sw1, sb1, sw2, sb2, rw1, rb1, rw2, rb2):
        import jax, jax.numpy as jnp
        import numpy as np
        D = 128
        H = 256
        E = 8
        TOP_K = 2
        N_SHARED = 1
        B, S = (2, 128)
        b, s, d = hidden.shape
        T = b * s
        flat = hidden.reshape(T, d)
        router_logits = flat @ router_w + router_b
        router_probs = jax.nn.softmax(router_logits, axis=-1)
        topk_probs, topk_idx = jax.lax.top_k(router_probs, TOP_K)
        weights = jnp.zeros_like(router_probs).at[jnp.arange(T)[:, None], topk_idx].add(topk_probs)
        sh = jax.nn.gelu(flat @ sw1 + sb1, approximate=False)
        shared_out = (sh @ sw2 + sb2) / N_SHARED
        h1 = jax.nn.gelu(jnp.einsum('td,edh->teh', flat, rw1) + rb1[None], approximate=False)
        expert_out = jnp.einsum('teh,ehd->ted', h1, rw2) + rb2[None]
        mixed = jnp.einsum('ted,te->td', expert_out, weights)
        return (shared_out + mixed).reshape(b, s, d)

    def _L3_attn_ref(x, W_dq, W_uq, W_dkv, W_uk, W_uv, W_o):
        import math
        import jax, jax.numpy as jnp
        import numpy as np
        N_HEAD = 16

        def _reference_tuple_inner(x, W_dq, W_uq, W_dkv, W_uk, W_uv, W_o):
            B, T, C = x.shape
            nh = N_HEAD
            hs = C // nh
            kvl = W_dkv.shape[0]
            k_eff = (W_dq.T @ W_uq.T @ W_uk).reshape(nh, hs, kvl)
            v_eff = (W_uv.T @ W_o.T).reshape(kvl, nh, hs).transpose(1, 0, 2)
            c_kv = x @ W_dkv.T
            q = (x @ W_dq.T @ W_uq.T).reshape(B, T, nh, hs).transpose(0, 2, 1, 3)
            q_lat = jnp.einsum('bhtd,hdl->bhtl', q, k_eff)
            attn = jnp.einsum('bhtl,bsl->bhts', q_lat, c_kv) / math.sqrt(hs)
            causal_mask = jnp.triu(jnp.ones((T, T), bool), k=1)
            attn = jnp.where(causal_mask[None, None], -jnp.inf, attn)
            attn = jax.nn.softmax(attn, axis=-1)
            ctx = jnp.einsum('bhts,bsl->bhtl', attn, c_kv)
            y = jnp.einsum('bhtl,hld->bhtd', ctx, v_eff).transpose(0, 2, 1, 3).reshape(B, T, C)
            return (y, c_kv)
        return _reference_tuple_inner(x, W_dq, W_uq, W_dkv, W_uk, W_uv, W_o)[0]

    def _L3_xattn_ref(x, context, Wq1, Wk1, Wv1, Wq2, Wk2, Wv2, fc1_w, fc1_b, fc2_w, fc2_b, ln1_g, ln1_b, ln2_g, ln2_b, ln3_g, ln3_b):
        import jax, jax.numpy as jnp
        import numpy as np
        E = 128
        NUM_HEADS = 16
        DK = E // NUM_HEADS
        EPS = 1e-05
        NEG_INF = -jnp.inf

        def layer_norm(x, g, b):
            mu = jnp.mean(x, axis=-1, keepdims=True)
            var = jnp.var(x, axis=-1, keepdims=True)
            return (x - mu) * jax.lax.rsqrt(var + EPS) * g + b

        def self_attn(x, Wq, Wk, Wv):
            Q, K, V = (x @ Wq, x @ Wk, x @ Wv)
            energy = jnp.einsum('bqd,bkd->bqk', Q, K)
            S = energy.shape[-1]
            lengths = jnp.sum(energy[:, 0] != 0, axis=-1)
            kidx = jnp.arange(S)
            pad = kidx[None, None, :] >= lengths[:, None, None]
            causal = kidx[None, :] < kidx[:, None]
            causal = (kidx[None, :] > kidx[:, None])[None]
            energy = jnp.where(pad | causal, NEG_INF, energy)
            score = jax.nn.softmax(energy / np.sqrt(DK), axis=-1)
            return jnp.einsum('bqk,bkd->bqd', score, V)

        def cross_attn(x, context, Wq, Wk, Wv):
            Q = x @ Wq
            K, V = (context @ Wk, context @ Wv)
            energy = jnp.einsum('bqd,bkd->bqk', Q, K)
            Sk = energy.shape[-1]
            lengths = jnp.sum(energy[:, 0] != 0, axis=-1)
            kidx = jnp.arange(Sk)
            pad = kidx[None, None, :] >= lengths[:, None, None]
            energy = jnp.where(pad, NEG_INF, energy)
            score = jax.nn.softmax(energy / np.sqrt(DK), axis=-1)
            return jnp.einsum('bqk,bkd->bqd', score, V)
        z = self_attn(x, Wq1, Wk1, Wv1)
        x = layer_norm(x + z, ln1_g, ln1_b)
        z = cross_attn(x, context, Wq2, Wk2, Wv2)
        x = layer_norm(x + z, ln2_g, ln2_b)
        z = jax.nn.relu(x @ fc1_w + fc1_b)
        z = z @ fc2_w + fc2_b
        return layer_norm(x + z, ln3_g, ln3_b)

    def _L3_ffn_ref(x, w_ln1, Wq, Wkva, Wkvb, Wo, w_ln2, Wgate, expert_bias, Wg, Wu, Wd, sWg, sWu, sWd):
        import jax, jax.numpy as jnp
        import numpy as np
        B, T, C = (2, 256, 128)
        H, D = (16, 64)
        CR = 8
        R = C // CR
        ROPE = D // 2
        NOPE = D - ROPE
        E, K, I, S = (8, 2, 64, 1)
        THETA = 100000.0
        EPS = 1e-05

        def _rmsnorm(x, w):
            rms = jnp.sqrt(jnp.mean(x * x, axis=-1, keepdims=True) + EPS)
            return w * (x / rms)

        def _rope(xh):
            d = xh.shape[-1]
            t = jnp.arange(xh.shape[2], dtype=jnp.float32)
            freqs = 1.0 / THETA ** (jnp.arange(0, d, 2, dtype=jnp.float32) / d)
            ang = jnp.outer(t, freqs)
            cos, sin = (jnp.cos(ang), jnp.sin(ang))
            xr = xh.reshape(xh.shape[:-1] + (d // 2, 2))
            x0, x1 = (xr[..., 0], xr[..., 1])
            rot = jnp.stack([x0 * cos - x1 * sin, x0 * sin + x1 * cos], axis=-1)
            return rot.reshape(xh.shape)

        def _attention(x, Wq, Wkva, Wkvb, Wo):
            b, t, _ = x.shape
            q = (x @ Wq).reshape(b, t, H, D).transpose(0, 2, 1, 3)
            ckv = x @ Wkva
            kv_latent, k_rope = (ckv[:, :, :R], ckv[:, :, R:])
            kv = (kv_latent @ Wkvb).reshape(b, t, H, NOPE).transpose(0, 2, 1, 3)
            k_rope = jnp.broadcast_to(k_rope[:, None, :, :], (b, H, t, ROPE))
            q_nope, q_rope = (q[..., :NOPE], q[..., NOPE:])
            q = jnp.concatenate([q_nope, _rope(q_rope)], axis=-1)
            k = jnp.concatenate([kv, _rope(k_rope)], axis=-1)
            v = jnp.concatenate([kv, jnp.zeros_like(k_rope)], axis=-1)
            att = jnp.einsum('bhqd,bhkd->bhqk', q, k) / jnp.sqrt(jnp.float32(D))
            mask = jnp.tril(jnp.ones((t, t), dtype=bool))
            att = jnp.where(mask, att, jnp.float32(-jnp.inf))
            att = jax.nn.softmax(att, axis=-1)
            y = jnp.einsum('bhqk,bhkd->bhqd', att, v)
            y = y.transpose(0, 2, 1, 3).reshape(b, t, H * D)
            return y @ Wo

        def _experts(x_flat, Wg, Wu, Wd):
            g = jax.nn.silu(jnp.einsum('nc,eci->nei', x_flat, Wg))
            u = jnp.einsum('nc,eci->nei', x_flat, Wu)
            return jnp.einsum('nei,eic->nec', g * u, Wd)

        def _moe(x, Wgate, expert_bias, Wg, Wu, Wd, sWg, sWu, sWd):
            b, t, c = x.shape
            xf = x.reshape(-1, c)
            shared = jnp.mean(_experts(xf, sWg, sWu, sWd), axis=1)
            logits = xf @ Wgate + expert_bias
            probs = jax.nn.softmax(logits, axis=-1)
            topk_p, topk_i = jax.lax.top_k(probs, K)
            topk_p = topk_p / jnp.sum(topk_p, axis=-1, keepdims=True)
            comb = jnp.sum(jax.nn.one_hot(topk_i, E, dtype=xf.dtype) * topk_p[..., None], axis=1)
            routed = jnp.einsum('ne,nec->nc', comb, _experts(xf, Wg, Wu, Wd))
            return (shared + routed).reshape(b, t, c)
        x = x + _attention(_rmsnorm(x, w_ln1), Wq, Wkva, Wkvb, Wo)
        residual = x
        xn = _rmsnorm(x, w_ln2)
        x_out = _moe(xn, Wgate, expert_bias, Wg, Wu, Wd, sWg, sWu, sWd)
        return residual + x_out
    x = x + _L0_attn_ref(_layernorm(x, axis=-1), L0_attn_w_qkv, L0_attn_w_out, L0_attn_fc_code)
    x = x + _L0_xattn_ref(_layernorm(x, axis=-1), ctx_1024, ctx_1024, L0_xattn_igate_kernel, L0_xattn_igate_bias, L0_xattn_fgate_kernel, L0_xattn_fgate_bias, L0_xattn_rms_scale)
    x = x + _L0_ffn_ref(_layernorm(x, axis=-1), L0_ffn_W_fc, L0_ffn_ln_w, L0_ffn_ln_b, L0_ffn_W_proj)
    x = x + _L1_attn_ref(_layernorm(x, axis=-1), L1_attn_norm_w, L1_attn_norm_b, L1_attn_in_w, L1_attn_in_b, L1_attn_conv_w, L1_attn_conv_b, L1_attn_dt_w, L1_attn_dt_b, L1_attn_b_w, L1_attn_b_b, L1_attn_c_w, L1_attn_c_b, L1_attn_a_log, L1_attn_d, L1_attn_out_w, L1_attn_out_b)
    x = x + _L1_xattn_ref(_layernorm(x, axis=-1), ctx_1024, L1_xattn_Wk, L1_xattn_bk, L1_xattn_Wq, L1_xattn_bq, L1_xattn_Wv, L1_xattn_bv, L1_xattn_W1, L1_xattn_b1, L1_xattn_W2, L1_xattn_b2)
    x = x + _L1_ffn_ref(_layernorm(x, axis=-1), L1_ffn_W_in, L1_ffn_b_in, L1_ffn_W_out)
    x = x + _L2_attn_ref(_layernorm(x, axis=-1), L2_attn_Wq, L2_attn_Wk, L2_attn_Wv, L2_attn_Wo)
    x = x + _L2_xattn_ref(ctx_1024, ctx_1024, _layernorm(x, axis=-1), mask_Bx1xSxS2_ik1, L2_xattn_Wv, L2_xattn_Wk, L2_xattn_Wq, L2_xattn_Wo, L2_xattn_bo)
    x = x + _L2_ffn_ref(_layernorm(x, axis=-1), L2_ffn_router_w, L2_ffn_router_b, L2_ffn_sw1, L2_ffn_sb1, L2_ffn_sw2, L2_ffn_sb2, L2_ffn_rw1, L2_ffn_rb1, L2_ffn_rw2, L2_ffn_rb2)
    x = x + _L3_attn_ref(_layernorm(x, axis=-1), L3_attn_W_dq, L3_attn_W_uq, L3_attn_W_dkv, L3_attn_W_uk, L3_attn_W_uv, L3_attn_W_o)
    x = x + _L3_xattn_ref(_layernorm(x, axis=-1), ctx_1024, L3_xattn_Wq1, L3_xattn_Wk1, L3_xattn_Wv1, L3_xattn_Wq2, L3_xattn_Wk2, L3_xattn_Wv2, L3_xattn_fc1_w, L3_xattn_fc1_b, L3_xattn_fc2_w, L3_xattn_fc2_b, L3_xattn_ln1_g, L3_xattn_ln1_b, L3_xattn_ln2_g, L3_xattn_ln2_b, L3_xattn_ln3_g, L3_xattn_ln3_b)
    x = x + _L3_ffn_ref(_layernorm(x, axis=-1), L3_ffn_w_ln1, L3_ffn_Wq, L3_ffn_Wkva, L3_ffn_Wkvb, L3_ffn_Wo, L3_ffn_w_ln2, L3_ffn_Wgate, L3_ffn_expert_bias, L3_ffn_Wg, L3_ffn_Wu, L3_ffn_Wd, L3_ffn_sWg, L3_ffn_sWu, L3_ffn_sWd)
    return x

_drawn_inputs = setup_inputs


def setup_inputs(seed=0):
    import zlib

    import numpy as np

    out = dict(_drawn_inputs(seed))
    spreads = {'L0_ffn_ln_w': (1.0, 0.2),
     'L0_ffn_ln_b': (0.0, 0.1),
     'L1_attn_norm_w': (1.0, 0.6),
     'L1_attn_norm_b': (0.0, 0.8),
     'L1_attn_in_b': (0.0, 0.8),
     'L1_attn_conv_b': (0.0, 0.8),
     'L1_attn_dt_b': (0.0, 0.8),
     'L1_attn_b_b': (0.0, 0.8),
     'L1_attn_c_b': (0.0, 0.8),
     'L1_attn_d': (1.0, 0.6),
     'L1_attn_out_b': (0.0, 0.8),
     'L1_xattn_bk': (0.0, 2.0),
     'L1_xattn_bq': (0.0, 0.8),
     'L1_xattn_bv': (0.0, 0.8),
     'L1_xattn_b1': (0.0, 0.8),
     'L1_xattn_b2': (0.0, 0.8),
     'L2_ffn_router_b': (0.0, 0.8),
     'L2_ffn_sb1': (0.0, 0.8),
     'L2_ffn_sb2': (0.0, 0.8),
     'L2_ffn_rb1': (0.0, 0.8),
     'L2_ffn_rb2': (0.0, 0.8),
     'L3_xattn_fc1_b': (0.0, 2.0),
     'L3_xattn_fc2_b': (0.0, 2.0),
     'L3_xattn_ln1_g': (1.0, 0.6),
     'L3_xattn_ln1_b': (0.0, 0.8),
     'L3_xattn_ln2_g': (1.0, 0.6),
     'L3_xattn_ln2_b': (0.0, 0.8),
     'L3_xattn_ln3_g': (1.0, 0.6),
     'L3_xattn_ln3_b': (0.0, 0.8),
     'L3_ffn_w_ln1': (1.0, 0.6),
     'L3_ffn_w_ln2': (1.0, 0.6),
     'L3_ffn_expert_bias': (0.0, 0.8)}
    factors = {'L0_xattn_igate_bias': 64.0,
     'L0_xattn_rms_scale': 2.76,
     'L1_attn_in_w': 3.922,
     'L1_attn_conv_w': 3.939,
     'L1_attn_dt_w': 8.0,
     'L1_attn_b_w': 8.0,
     'L1_attn_c_w': 8.0,
     'L1_attn_a_log': 8.0,
     'L1_attn_out_w': 3.827,
     'L1_xattn_Wk': 3.598,
     'L1_xattn_Wq': 3.783,
     'L2_attn_Wq': 6.078,
     'L2_attn_Wk': 6.228,
     'L2_attn_Wv': 4.271,
     'L2_attn_Wo': 4.199,
     'L2_xattn_Wk': 8.0,
     'L2_xattn_Wq': 8.0,
     'L2_xattn_bo': 47.793,
     'L2_ffn_router_w': 8.0,
     'L2_ffn_sw1': 8.0,
     'L2_ffn_sw2': 8.0,
     'L2_ffn_rw1': 8.0,
     'L2_ffn_rw2': 8.0,
     'L3_attn_W_dq': 8.0,
     'L3_attn_W_uq': 8.0,
     'L3_attn_W_dkv': 8.0,
     'L3_attn_W_uk': 8.0,
     'L3_attn_W_uv': 8.0,
     'L3_attn_W_o': 8.0,
     'L3_ffn_Wq': 8.0,
     'L3_ffn_Wkva': 8.0,
     'L3_ffn_Wkvb': 8.0,
     'L3_ffn_Wo': 8.0,
     'L3_ffn_Wgate': 8.0,
     'L3_ffn_Wg': 8.0,
     'L3_ffn_Wu': 8.0,
     'L3_ffn_Wd': 8.0,
     'L3_ffn_sWg': 8.0,
     'L3_ffn_sWu': 8.0,
     'L3_ffn_sWd': 8.0}
    for name, (base, spread) in spreads.items():
        noise = np.random.default_rng([zlib.crc32(name.encode()), seed]).standard_normal(out[name].shape)
        drawn = base * np.exp(spread * noise) if base else spread * noise
        out[name] = jnp.asarray(drawn.astype(out[name].dtype))
    for name, factor in factors.items():
        out[name] = (out[name] * factor).astype(out[name].dtype)
    return out
```

```python
from contextlib import ExitStack

import numpy as np

import concourse.bass as bass
from concourse import mybir

F32 = mybir.dt.float32
BF16 = mybir.dt.bfloat16
I32 = mybir.dt.int32
U32 = mybir.dt.uint32
ALU = mybir.AluOpType
ACT = mybir.ActivationFunctionType
AX = mybir.AxisListType

P = 128
B = 8
T = 256
D = 128
NT = B * T // P
TILES = 4
COLS = TILES * P
TURNS = NT // TILES
SEQS = TILES * P // T
HALVES = T // P
LN_EPS = 1e-5


class Chain:

    def __init__(self, eng, sem, turn=0, per_turn=0):
        self.eng, self.sem, self.base, self.per_turn, self.n = eng, sem, turn * per_turn, per_turn, 0

    def __call__(self, step):
        self.n += 1
        step.then_inc(self.sem, 1)
        self.eng.wait_ge(self.sem, self.base + self.n)

    def end(self):
        assert self.n == self.per_turn, f"{self.sem} counts {self.n} steps in a turn"


def tiles_of(x, turn, j=None):
    if j is None:
        return x[:, bass.ds(turn * TILES, TILES), :]
    return x[:, bass.ds(turn * TILES + j, 1), :].rearrange("p o d -> p (o d)")


def measure_tokens(nc, g, name, load_next):
    with ExitStack() as ctx:
        used = g.semaphores
        g.semaphores = []
        sem = lambda n: g.semaphore(nc, ctx, name + "_" + n)
        moments_ready, deviation_ready, rstd_ready = sem("moments_ready"), sem("deviation_ready"), sem("rstd_ready")
        with nc.Block() as block:
            @block.sync
            def _(sp):
                load_next(sp)

            @block.gpsimd
            def _(pool):
                for s in used:
                    pool.sem_clear(s)

            @block.vector
            def _(v):
                for n in range(NT):
                    last = v.bn_aggr(g.moments[:, n, :], g.x_stats[:, n, :])
                last.then_inc(moments_ready, 1)
                v.wait_ge(deviation_ready, 1)
                v.reciprocal(g.rstd[:, :], g.rstd[:, :]).then_inc(rstd_ready, 1)

            @block.scalar
            def _(a):
                a.wait_ge(moments_ready, 1)
                a.activation(g.rstd[:, :], g.moments[:, :, 1], ACT.Sqrt, bias=g.eps[:, 0:1]).then_inc(deviation_ready, 1)


def normalise(v, g, t, dst):
    for j in range(TILES):
        n = bass.ds(t * TILES + j, 1)
        last = v.tensor_scalar(dst[:, j, :], tiles_of(g.x, t, j), g.moments[:, n, 0:1].rearrange("p n o -> p (n o)"),
                               g.rstd[:, n], ALU.subtract, ALU.mult)
    return last


def take_stats(v, g, t):
    for j in range(TILES):
        last = v.bn_stats(g.x_stats[:, bass.ds(t * TILES + j, 1), :].rearrange("p n s -> p (n s)"), tiles_of(g.x, t, j))
    return last



def layer0_attention(nc, g, w):
    HEAD, CODES = 8, 2
    SCALE = HEAD ** -0.5
    with ExitStack() as ctx:
        sb = lambda n, s, d=F32: ctx.enter_context(nc.sbuf_tensor("a0_" + n, s, d))
        ps = lambda n, s, d=F32: ctx.enter_context(nc.psum_tensor("a0_" + n, s, d))
        sem = lambda n: g.semaphore(nc, ctx, "a0_" + n)
        code_mix = sb("code_mix", [P, CODES, P])
        w_code = sb("w_code", [P, 2 * CODES, P])
        xn = sb("xn", [P, TILES, D])
        xnT = sb("xnT", [P, COLS])
        key_max = sb("key_max", [P, CODES * SEQS])
        q0 = sb("q0", [P, COLS])
        q_max = sb("q_max", [P, COLS])
        q_exp = sb("q_exp", [P, CODES, COLS])
        q_sum = sb("q_sum", [P, COLS])
        key_exp = sb("key_exp", [P, CODES, COLS])
        kv = sb("kv", [P, CODES, COLS])
        key_cum = sb("key_cum", [P, CODES, COLS])
        kv_cum = sb("kv_cum", [P, CODES, COLS])
        mixT = sb("mixT", [P, COLS])
        ps_t = ps("ps_t", [P, COLS])
        ps_q = ps("ps_q", [P, CODES, COLS])
        ps_k = ps("ps_k", [P, CODES, COLS])
        ps_v = ps("ps_v", [P, COLS])
        ps_o = ps("ps_o", [P, TILES, D])
        steps, mixed, w_made, w_ready = sem("steps"), sem("mixed"), sem("w_made"), sem("w_ready")
        xn_ready, xT_made, xnT_ready = sem("xn_ready"), sem("xT_made"), sem("xnT_ready")
        qkv_made, q0_ready, max_ready = sem("qkv_made"), sem("q0_ready"), sem("max_ready")
        key_ready, qsub_ready, qexp_ready = sem("key_ready"), sem("qsub_ready"), sem("qexp_ready")
        mix_ready, out_made, added = sem("mix_ready"), sem("out_made"), sem("added")
        block = ctx.enter_context(nc.Block())
        BOUNDS = g.seq_starts[:, 0:CODES * COLS]

        @block.vector
        def _(v):
            v.wait_ge(g.loaded["L0_attn"], 16)
            v.wait_ge(g.loaded["shared"], 16)
            for c in range(CODES):
                last = v.tensor_scalar(code_mix[:, c, :], g.head_blocks, w["code"][:, c:c + 1], SCALE,
                                       ALU.mult, ALU.mult)
            last.then_inc(mixed, 1)
            v.wait_ge(g.x_loaded, 16)
            with v.Fori(0, TURNS) as t:
                step = Chain(v, steps, t, 10)
                v.wait_ge(xT_made, t)
                normalise(v, g, t, xn).then_inc(xn_ready, 1)
                v.wait_ge(qkv_made, t + 1)
                v.tensor_reduce(key_max[:, :], ps_k[:, :, :].rearrange("p c (s t) -> p (c s) t", s=SEQS),
                                AX.X, ALU.max, negate=True).then_inc(max_ready, 1)
                v.wait_ge(q0_ready, t + 1)
                step(v.tensor_tensor(q_max[:, :], q0[:, :], ps_q[:, 1, :], ALU.max))
                v.tensor_tensor(q_exp[:, 0, :], q0[:, :], q_max[:, :], ALU.subtract)
                v.tensor_tensor(q_exp[:, 1, :], ps_q[:, 1, :], q_max[:, :], ALU.subtract).then_inc(qsub_ready, 1)
                v.wait_ge(key_ready, t + 1)
                step(v.tensor_tensor(kv[:, :, :], key_exp[:, :, :],
                                     ps_v[:, :].rearrange("p (o t) -> p o t", o=1).broadcast_to([P, CODES, COLS]), ALU.mult))
                flat = lambda a: a[:, :, :].rearrange("p c t -> p (c t)")
                v.tensor_tensor_scan(flat(key_cum), BOUNDS, flat(key_exp), 0.0, ALU.mult, ALU.add)
                step(v.tensor_tensor_scan(flat(kv_cum), BOUNDS, flat(kv), 0.0, ALU.mult, ALU.add))
                step(v.tensor_scalar(flat(key_cum), flat(key_cum), 1e-9, None, ALU.add))
                step(v.reciprocal(flat(key_cum), flat(key_cum)))
                step(v.tensor_tensor(flat(kv_cum), flat(kv_cum), flat(key_cum), ALU.mult))
                v.wait_ge(qexp_ready, t + 1)
                v.tensor_tensor(q_sum[:, :], q_exp[:, 0, :], q_exp[:, 1, :], ALU.add)
                step(v.tensor_tensor(flat(kv_cum), flat(kv_cum), flat(q_exp), ALU.mult))
                step(v.reciprocal(q_sum[:, :], q_sum[:, :]))
                step(v.tensor_tensor(q_max[:, :], kv_cum[:, 0, :], kv_cum[:, 1, :], ALU.add))
                v.wait_ge(out_made, t)
                v.scalar_tensor_tensor(mixT[:, :], q_max[:, :], SCALE, q_sum[:, :], ALU.mult, ALU.mult).then_inc(mix_ready, 1)
                v.wait_ge(out_made, t + 1)
                v.tensor_tensor(tiles_of(g.x, t), tiles_of(g.x, t), ps_o[:, :, :], ALU.add).then_inc(added, 1)
                v.wait_ge(added, t + 1)
                step(take_stats(v, g, t))
                step.end()

        @block.tensor
        def _(pe):
            pe.wait_ge(mixed, 1)
            for i, nat in enumerate((w["wq"], w["wk"])):
                for c in range(CODES):
                    last = pe.matmul(ps_o[:, 2 * i + c, :], nat, code_mix[:, c, :], start=True, stop=True)
            last.then_inc(w_made, 1)
            pe.wait_ge(w_ready, 1)
            with pe.Fori(0, TURNS) as t:
                pe.wait_ge(xn_ready, t + 1)
                pe.wait_ge(xnT_ready, t)
                for j in range(TILES):
                    last = pe.transpose(ps_t[:, j * P:(j + 1) * P], xn[:, j, :], g.ident)
                last.then_inc(xT_made, 1)
                pe.wait_ge(xnT_ready, t + 1)
                pe.wait_ge(mix_ready, t)
                for c in range(CODES):
                    pe.matmul(ps_k[:, c, :], w_code[:, CODES + c, :], xnT[:, :], start=True, stop=True)
                for c in range(CODES):
                    pe.matmul(ps_q[:, c, :], w_code[:, c, :], xnT[:, :], start=True, stop=True)
                pe.matmul(ps_v[:, :], w["wvT"], xnT[:, :], start=True, stop=True).then_inc(qkv_made, 1)
                pe.wait_ge(mix_ready, t + 1)
                pe.wait_ge(added, t)
                for j in range(TILES):
                    last = pe.matmul(ps_o[:, j, :], mixT[:, j * P:(j + 1) * P], w["woT"], start=True, stop=True)
                last.then_inc(out_made, 1)

        @block.scalar
        def _(a):
            a.wait_ge(w_made, 1)
            a.activation(w_code[:, :, :], ps_o[:, :, :], ACT.Copy).then_inc(w_ready, 1)
            with a.Fori(0, TURNS) as t:
                a.wait_ge(xT_made, t + 1)
                a.wait_ge(qkv_made, t)
                a.activation(xnT[:, :], ps_t[:, :], ACT.Copy).then_inc(xnT_ready, 1)
                a.wait_ge(qkv_made, t + 1)
                a.activation(q0[:, :], ps_q[:, 0, :], ACT.Copy).then_inc(q0_ready, 1)
                a.wait_ge(max_ready, t + 1)
                for c in range(CODES):
                    for s in range(SEQS):
                        i = c * SEQS + s
                        last = a.activation(key_exp[:, c, s * T:(s + 1) * T], ps_k[:, c, s * T:(s + 1) * T], ACT.Exp,
                                            bias=key_max[:, i:i + 1])
                last.then_inc(key_ready, 1)
                a.wait_ge(qsub_ready, t + 1)
                a.activation(q_exp[:, :, :], q_exp[:, :, :], ACT.Exp).then_inc(qexp_ready, 1)



def layer0_mlstm(nc, g, w):
    NH, HD = 4, 32
    V1 = HD + 1
    WIDE = T + P
    with ExitStack() as ctx:
        sb = lambda n, s, d=F32: ctx.enter_context(nc.sbuf_tensor("x0_" + n, s, d))
        ps = lambda n, s, d=F32: ctx.enter_context(nc.psum_tensor("x0_" + n, s, d))
        sem = lambda n: g.semaphore(nc, ctx, "x0_" + n)
        v_ones = sb("v_ones", [P, NT, NH, V1])
        xn, xnT = sb("xn", [P, TILES, D]), sb("xnT", [P, COLS])
        f_gate, f_abs, f_log, f_sum = (sb(n, [NH, COLS]) for n in ("f_gate", "f_abs", "f_log", "f_sum"))
        g_rows, m_rows, floor = (sb(n, [NH, COLS]) for n in ("g_rows", "m_rows", "floor"))
        keyT = sb("keyT", [P, COLS])
        cols = sb("cols", [P, TILES, 2, NH])
        decay = sb("decay", [P, NH, WIDE])
        weight = sb("weight", [P, NH, WIDE])
        norm = sb("norm", [P, HALVES, NH])
        heads = sb("heads", [P, NT, NH, HD])
        squares = sb("squares", [P, HALVES, NH, HD])
        power = sb("power", [P, NT, NH])
        rms_row = sb("rms_row", [P, HD])
        ps_t = ps("ps_t", [P, COLS])
        ps_i, ps_f = ps("ps_i", [P, COLS]), ps("ps_f", [P, COLS])
        ps_m = ps("ps_m", [P, NH, T])
        ps_kq = ps("ps_kq", [P, 2, 512])
        ps_o = ps("ps_o", [P, 512])
        out_of = ps_o[:, 0:HALVES * NH * V1].rearrange("p (j h d) -> p j h d", j=HALVES, h=NH)
        cols_ps = ps_t[:, 0:TILES * 2 * NH].rearrange("p (j k h) -> p j k h", j=TILES, k=2)
        steps, v_ready = sem("steps"), sem("v_ready")
        xn_ready, xT_made, xnT_ready, gates_made = sem("xn_ready"), sem("xT_made"), sem("xnT_ready"), sem("gates_made")
        flog_ready, sum_ready, floor_ready = sem("flog_ready"), sem("sum_ready"), sem("floor_ready")
        cols_made, cols_ready = sem("cols_made"), sem("cols_ready")
        max_made, masked, decay_ready = sem("max_made"), sem("masked"), sem("decay_ready")
        kq_made, weighted, out_made, scaled = sem("kq_made"), sem("weighted"), sem("out_made"), sem("scaled")
        power_ready, root_ready, done = sem("power_ready"), sem("root_ready"), sem("done")
        act_steps, key_ready = sem("act_steps"), sem("key_ready")
        block = ctx.enter_context(nc.Block())
        STARTS, FLOOR = g.seq_starts[0:NH, 0:COLS], w["seq_floor"][0:NH, :]

        @block.gpsimd
        def _(pool):
            pool.wait_ge(g.loaded["context"], 32)
            pool.memset(v_ones[:, :, :, :], 1.0).then_inc(v_ready, 1)
            pool.wait_ge(v_ready, 1)
            pool.tensor_copy(v_ones[:, :, :, 0:HD], g.ctx[:, :, :].rearrange("p n (h d) -> p n h d", h=NH)).then_inc(v_ready, 1)
            with pool.Fori(0, TURNS) as t:
                pool.wait_ge(kq_made, t * 4)
                pool.tensor_copy(keyT[:, :], g.ctxT[:, bass.ds(t * COLS, COLS)]).then_inc(key_ready, 1)

        @block.vector
        def _(v):
            v.wait_ge(g.loaded["L0_xattn"], 16)
            with v.Fori(0, TURNS) as t:
                step = Chain(v, steps, t, 15)
                v.wait_ge(xT_made, t)
                normalise(v, g, t, xn).then_inc(xn_ready, 1)
                v.wait_ge(flog_ready, t + 1)
                step(v.scalar_tensor_tensor(f_log[:, :], f_gate[:, :], 0.0, f_log[:, :], ALU.min, ALU.subtract))
                step(v.tensor_tensor_scan(f_sum[:, :], STARTS, f_log[:, :], 0.0, ALU.mult, ALU.add))
                v.wait_ge(gates_made, t + 1)
                step(v.scalar_tensor_tensor(g_rows[:, :], ps_i[0:NH, :], w["ibias"], f_sum[:, :], ALU.add, ALU.subtract))
                step(v.tensor_tensor_scan(m_rows[:, :], FLOOR, g_rows[:, :], -1e30, ALU.add, ALU.max))
                v.tensor_tensor(floor[:, :], f_sum[:, :], m_rows[:, :], ALU.add).then_inc(sum_ready, 1)
                v.wait_ge(cols_made, t + 1)
                v.wait_ge(decay_ready, t * SEQS)
                v.tensor_copy(cols[:, :, :, :], cols_ps).then_inc(cols_ready, 1)
                for s in range(SEQS):
                    n = t * SEQS + s
                    v.wait_ge(max_made, n + 1)
                    diagonal = w["causalT"].rearrange("p (o c) -> p o c", o=1).broadcast_to([P, NH, P])
                    v.tensor_tensor(decay[:, :, 0:P], ps_m[:, :, 0:P], diagonal, ALU.add)
                    v.tensor_copy(decay[:, :, P:T], ps_m[:, :, P:T])
                    v.tensor_tensor(decay[:, :, T:WIDE], ps_m[:, :, P:T], diagonal, ALU.add).then_inc(masked, 1)
                    v.wait_ge(decay_ready, n + 1)
                    for pair in range(NH // 2):
                        v.wait_ge(kq_made, t * 4 + 2 * s + pair + 1)
                        if pair == 0:
                            v.wait_ge(out_made, n)
                        hh = slice(2 * pair, 2 * pair + 2)
                        v.scalar_tensor_tensor(weight[:, hh, :], ps_kq[:, :, 0:WIDE], HD ** -0.5, decay[:, hh, :],
                                               ALU.mult, ALU.mult).then_inc(weighted, 1)
                    v.wait_ge(out_made, n + 1)
                    j0 = s * HALVES
                    at = bass.ds(t * TILES + j0, HALVES)
                    step(v.tensor_tensor(norm[:, :, :], out_of[:, :, :, HD], cols[:, j0:j0 + HALVES, 1, :], ALU.max))
                    step(v.tensor_scalar(norm[:, :, :], norm[:, :, :], 1e-6, None, ALU.add))
                    step(v.reciprocal(norm[:, :, :], norm[:, :, :]))
                    for j in range(HALVES):
                        last = v.tensor_tensor(heads[:, bass.ds(t * TILES + j0 + j, 1), :, :].rearrange("p o h d -> p (o h) d"),
                                               out_of[:, j, :, 0:HD],
                                               norm[:, j, :].rearrange("p (h o) -> p h o", o=1).broadcast_to([P, NH, HD]), ALU.mult)
                    last.then_inc(scaled, 1)
                    v.wait_ge(scaled, n + 1)
                    flat = heads[:, at, :, :].rearrange("p j h d -> p (j h d)")
                    step(v.tensor_tensor(squares[:, :, :, :].rearrange("p j h d -> p (j h d)"), flat, flat, ALU.mult))
                    step(v.tensor_reduce(power[:, at, :].rearrange("p j h -> p (j h)"),
                                         squares[:, :, :, :].rearrange("p j h d -> p (j h) d"), AX.X, ALU.add))
                step(v.tensor_scalar(rms_row[:, :], w["rms"], 1.0, None, ALU.add))
                step.end()
            v.nop().then_inc(power_ready, 1)
            v.wait_ge(root_ready, 1)
            last = Chain(v, done)
            last(v.reciprocal(power[:, :, :], power[:, :, :]))
            flat = lambda a: a[:, :, :, :].rearrange("p n h d -> p (n h) d")
            last(v.tensor_tensor(flat(heads), flat(heads),
                                 power[:, :, :].rearrange("p n (h o) -> p (n h) o", o=1).broadcast_to([P, NT * NH, HD]), ALU.mult))
            last(v.tensor_tensor(flat(heads), flat(heads),
                                 rms_row[:, :].rearrange("p (o d) -> p o d", o=1).broadcast_to([P, NT * NH, HD]), ALU.mult))
            last(v.tensor_tensor(g.x[:, :, :].rearrange("p n d -> p (n d)"), g.x[:, :, :].rearrange("p n d -> p (n d)"),
                                 heads[:, :, :, :].rearrange("p n h d -> p (n h d)"), ALU.add))
            for n in range(NT):
                ins = v.bn_stats(g.x_stats[:, n, :], g.x[:, n, :])
            last(ins)

        @block.tensor
        def _(pe):
            pe.wait_ge(g.loaded["L0_xattn"], 16)
            pe.wait_ge(g.loaded["context"], 32)
            pe.wait_ge(v_ready, 2)
            with pe.Fori(0, TURNS) as t:
                ctxT = keyT[:, :]
                pe.wait_ge(xn_ready, t + 1)
                pe.wait_ge(cols_ready, t)
                for j in range(TILES):
                    last = pe.transpose(ps_t[:, j * P:(j + 1) * P], xn[:, j, :], g.ident)
                last.then_inc(xT_made, 1)
                pe.wait_ge(xnT_ready, t + 1)
                pe.wait_ge(key_ready, t + 1)
                pe.wait_ge(sum_ready, t)
                for out, wx, wk, wv in ((ps_f, "fx", "fk", "fv"), (ps_i, "ix", "ik", "iv")):
                    pe.matmul(out[0:NH, :], w[wx], xnT[:, :], start=True, stop=False)
                    pe.matmul(out[0:NH, :], w[wk], ctxT, start=False, stop=False)
                    last = pe.matmul(out[0:NH, :], w[wv], ctxT, start=False, stop=True)
                last.then_inc(gates_made, 1)
                pe.wait_ge(floor_ready, t + 1)
                for j in range(TILES):
                    for k, rows in enumerate((g_rows, floor)):
                        last = pe.matmul(cols_ps[:, j, k, :], rows[:, j * P:(j + 1) * P], g.ident[0:NH, 0:NH],
                                         start=True, stop=True)
                last.then_inc(cols_made, 1)
                for s in range(SEQS):
                    n = t * SEQS + s
                    pe.wait_ge(masked, n)
                    for h in range(NH):
                        last = pe.matmul(ps_m[:, h, :], w["minus_head"][0:NH, h * P:(h + 1) * P],
                                         m_rows[:, s * T:(s + 1) * T], start=True, stop=True)
                    last.then_inc(max_made, 1)
                    for pair in range(NH // 2):
                        pe.wait_ge(weighted, t * 4 + 2 * s + pair)
                        for i in range(2):
                            rows = slice(HD * (2 * pair + i), HD * (2 * pair + i + 1))
                            key = lambda half: keyT[rows, s * T + half * P:s * T + (half + 1) * P]
                            pe.matmul(ps_kq[:, i, 0:T], key(0), xnT[rows, s * T:(s + 1) * T], start=True, stop=True)
                            last = pe.matmul(ps_kq[:, i, T:WIDE], key(1), xnT[rows, s * T + P:(s + 1) * T], start=True, stop=True)
                        last.then_inc(kq_made, 1)
                    pe.wait_ge(weighted, t * 4 + 2 * s + 2)
                    pe.wait_ge(scaled, n)
                    for h in range(NH):
                        value = lambda half: v_ones[:, bass.ds(t * TILES + s * HALVES + half, 1), h, :].rearrange("p o d -> p (o d)")
                        pe.matmul(out_of[:, 0, h, :], weight[:, h, 0:P], value(0), start=True, stop=True)
                        pe.matmul(out_of[:, 1, h, :], weight[:, h, P:T], value(0), start=True, stop=False)
                        last = pe.matmul(out_of[:, 1, h, :], weight[:, h, T:WIDE], value(1), start=False, stop=True)
                    last.then_inc(out_made, 1)

        @block.scalar
        def _(a):
            a.wait_ge(g.loaded["L0_xattn"], 16)
            with a.Fori(0, TURNS) as t:
                step = Chain(a, act_steps, t, 2)
                a.wait_ge(xT_made, t + 1)
                a.wait_ge(out_made, t * SEQS)
                a.activation(xnT[:, :], ps_t[:, :], ACT.Copy).then_inc(xnT_ready, 1)
                a.wait_ge(gates_made, t + 1)
                a.wait_ge(sum_ready, t)
                a.activation(f_gate[:, :], ps_f[0:NH, :], ACT.Identity, bias=w["fbias"])
                step(a.activation(f_abs[:, :], ps_f[0:NH, :], ACT.Abs, bias=w["fbias"]))
                step(a.activation(f_abs[:, :], f_abs[:, :], ACT.Exp, scale=-1.0))
                a.activation(f_log[:, :], f_abs[:, :], ACT.Ln, bias=1.0).then_inc(flog_ready, 1)
                a.wait_ge(sum_ready, t + 1)
                a.activation(floor[:, :], floor[:, :], ACT.Exp, scale=-1.0).then_inc(floor_ready, 1)
                a.wait_ge(cols_ready, t + 1)
                for s in range(SEQS):
                    a.wait_ge(masked, t * SEQS + s + 1)
                    for h in range(NH):
                        for half, part in enumerate((slice(0, T), slice(T, WIDE))):
                            last = a.activation(decay[:, h, part], decay[:, h, part], ACT.Exp,
                                                bias=cols[:, s * HALVES + half, 0, h:h + 1])
                    last.then_inc(decay_ready, 1)
                step.end()
            a.wait_ge(power_ready, 1)
            a.activation(power[:, :, :], power[:, :, :], ACT.Sqrt, scale=1.0 / HD, bias=w["rms_eps"]).then_inc(root_ready, 1)



def layer0_ternary_ffn(nc, g, w):
    HID = 512
    CHUNKS = HID // P
    with ExitStack() as ctx:
        sb = lambda n, s, d=F32: ctx.enter_context(nc.sbuf_tensor("f0_" + n, s, d))
        ps = lambda n, s, d=F32: ctx.enter_context(nc.psum_tensor("f0_" + n, s, d))
        sem = lambda n: g.semaphore(nc, ctx, "f0_" + n)
        total, gamma = sb("total", [P, 2]), sb("gamma", [P, 2])
        ternary, negative = sb("ternary", [P, 2, HID]), sb("negative", [P, 2, HID])
        xn, xnT = sb("xn", [P, TILES, D]), sb("xnT", [P, COLS])
        hidden = sb("hidden", [P, NT, HID])
        hn = sb("hn", [P, TILES, HID])
        h_stats, h_moments, h_rstd = sb("h_stats", [P, NT, 6]), sb("h_moments", [P, NT, 2]), sb("h_rstd", [P, NT])
        hT = sb("hT", [P, CHUNKS, COLS])
        ps_t = ps("ps_t", [P, COLS])
        ps_h = ps("ps_h", [P, TILES, HID])
        ps_o = ps("ps_o", [P, TILES, D])
        prep, totals_made, w_ready = sem("prep"), sem("totals_made"), sem("w_ready")
        xn_ready, xT_made, xnT_ready, h_made, gelu_ready = (
            sem(n) for n in ("xn_ready", "xT_made", "xnT_ready", "h_made", "gelu_ready"))
        stats_ready, root_ready, rstd_ready = sem("stats_ready"), sem("root_ready"), sem("rstd_ready")
        hn_ready, hT_made, hT_ready, out_made, added = (
            sem(n) for n in ("hn_ready", "hT_made", "hT_ready", "out_made", "added"))
        steps = sem("steps")
        block = ctx.enter_context(nc.Block())

        @block.vector
        def _(v):
            v.wait_ge(g.loaded["L0_ffn"], 16)
            step = Chain(v, prep)
            for i, name in enumerate(("fcT", "projT")):
                last = v.tensor_reduce(total[:, i:i + 1], w[name], AX.X, ALU.add, apply_absolute_value=True)
            step(last)
            v.wait_ge(totals_made, 1)
            step(v.tensor_scalar(gamma[:, :], ps_o[:, 0, 0:2], 1.0 / (P * HID), 1e-6, ALU.mult, ALU.add))
            step(v.tensor_scalar(gamma[:, :], gamma[:, :], 0.5, None, ALU.mult))
            for i, name in enumerate(("fcT", "projT")):
                v.tensor_scalar(ternary[:, i, :], w[name], gamma[:, i:i + 1], None, ALU.is_gt)
                last = v.tensor_scalar(negative[:, i, :], w[name], -1.0, gamma[:, i:i + 1], ALU.mult, ALU.is_gt)
            step(last)
            v.tensor_tensor(ternary[:, :, :], ternary[:, :, :], negative[:, :, :], ALU.subtract).then_inc(w_ready, 1)
            with v.Fori(0, TURNS) as t:
                v.wait_ge(xT_made, t)
                normalise(v, g, t, xn).then_inc(xn_ready, 1)
                v.wait_ge(gelu_ready, t + 1)
                for j in range(TILES):
                    n = bass.ds(t * TILES + j, 1)
                    last = v.bn_stats(h_stats[:, n, :].rearrange("p o s -> p (o s)"),
                                      hidden[:, n, :].rearrange("p o h -> p (o h)"))
                last.then_inc(stats_ready, 1)
            v.wait_ge(stats_ready, TURNS)
            for n in range(NT):
                last = v.bn_aggr(h_moments[:, n, :], h_stats[:, n, :])
            last.then_inc(rstd_ready, 1)
            v.wait_ge(root_ready, 1)
            step(v.reciprocal(h_rstd[:, :], h_rstd[:, :]))
            with v.Fori(0, TURNS) as t:
                v.wait_ge(hT_made, t * CHUNKS)
                for j in range(TILES):
                    n = bass.ds(t * TILES + j, 1)
                    h = hidden[:, n, :].rearrange("p o h -> p (o h)")
                    last = v.tensor_scalar(hn[:, j, :], h, h_moments[:, n, 0:1].rearrange("p o s -> p (o s)"), h_rstd[:, n],
                                           ALU.subtract, ALU.mult)
                last.then_inc(hn_ready, 1)
                v.wait_ge(out_made, t + 1)
                v.tensor_tensor(tiles_of(g.x, t), tiles_of(g.x, t), ps_o[:, :, :], ALU.add).then_inc(added, 1)
                v.wait_ge(added, t + 1)
                take_stats(v, g, t).then_inc(steps, 1)
            v.wait_ge(steps, TURNS)

        @block.tensor
        def _(pe):
            pe.wait_ge(g.loaded["L0_ffn"], 16)
            pe.wait_ge(prep, 1)
            pe.matmul(ps_o[:, 0, 0:2], g.ones, total[:, :], start=True, stop=True).then_inc(totals_made, 1)
            pe.wait_ge(w_ready, 1)
            with pe.Fori(0, TURNS) as t:
                pe.wait_ge(xn_ready, t + 1)
                pe.wait_ge(xnT_ready, t)
                for j in range(TILES):
                    last = pe.transpose(ps_t[:, j * P:(j + 1) * P], xn[:, j, :], g.ident)
                last.then_inc(xT_made, 1)
                pe.wait_ge(xnT_ready, t + 1)
                pe.wait_ge(gelu_ready, t)
                for j in range(TILES):
                    last = pe.matmul(ps_h[:, j, :], xnT[:, j * P:(j + 1) * P], ternary[:, 0, :], start=True, stop=True)
                last.then_inc(h_made, 1)
            pe.wait_ge(gelu_ready, TURNS)
            with pe.Fori(0, TURNS) as t:
                pe.wait_ge(hn_ready, t + 1)
                pe.wait_ge(hT_ready, t * CHUNKS)
                for c in range(CHUNKS):
                    for j in range(TILES):
                        last = pe.transpose(ps_h[:, c, j * P:(j + 1) * P], hn[:, j, c * P:(c + 1) * P], g.ident)
                    last.then_inc(hT_made, 1)
                pe.wait_ge(added, t)
                pe.wait_ge(hT_ready, (t + 1) * CHUNKS)
                for j in range(TILES):
                    for c in range(CHUNKS):
                        last = pe.matmul(ps_o[:, j, :], hT[:, c, j * P:(j + 1) * P], ternary[:, 1, c * P:(c + 1) * P],
                                         start=c == 0, stop=c == CHUNKS - 1)
                last.then_inc(out_made, 1)

        @block.scalar
        def _(a):
            with a.Fori(0, TURNS) as t:
                a.wait_ge(xT_made, t + 1)
                a.wait_ge(h_made, t)
                a.activation(xnT[:, :], ps_t[:, :], ACT.Copy).then_inc(xnT_ready, 1)
                a.wait_ge(h_made, t + 1)
                a.activation(hidden[:, bass.ds(t * TILES, TILES), :], ps_h[:, :, :], ACT.Gelu).then_inc(gelu_ready, 1)
            a.wait_ge(rstd_ready, 1)
            a.activation(h_rstd[:, :], h_moments[:, :, 1], ACT.Sqrt, bias=g.eps).then_inc(root_ready, 1)
            with a.Fori(0, TURNS) as t:
                a.wait_ge(out_made, t)
                for c in range(CHUNKS):
                    a.wait_ge(hT_made, t * CHUNKS + c + 1)
                    a.activation(hT[:, c, :], ps_h[:, c, :], ACT.Identity, scale=w["ln_w"][:, c:c + 1],
                                 bias=w["ln_b"][:, c:c + 1]).then_inc(hT_ready, 1)



def layer1_state_space(nc, g, w):
    S = 64
    PAD = T + 2
    with ExitStack() as ctx:
        sb = lambda n, s, d=F32: ctx.enter_context(nc.sbuf_tensor("a1_" + n, s, d))
        ps = lambda n, s, d=F32: ctx.enter_context(nc.psum_tensor("a1_" + n, s, d))
        sem = lambda n: g.semaphore(nc, ctx, "a1_" + n)
        x1 = sb("x1", [P, NT, D])
        stats, moments, rstd = sb("stats", [P, NT, 6]), sb("moments", [P, NT, 2]), sb("rstd", [P, NT])
        rate, out_d = sb("rate", [S, 3]), sb("out_d", [P, D])
        xn, xnT = sb("xn", [P, TILES, D]), sb("xnT", [P, COLS])
        proj, conv = sb("proj", [P, SEQS, PAD]), sb("conv", [P, SEQS, T])
        zT = sb("zT", [P, COLS])
        pre, absolute, soft, decay, gate_b, gate_c, states = (
            sb(n, [S, COLS]) for n in ("pre", "absolute", "soft", "decay", "gate_b", "gate_c", "states"))
        ps_t, ps_x, ps_z, ps_dt, ps_b, ps_c = (ps(n, [P, COLS]) for n in ("ps_t", "ps_x", "ps_z", "ps_dt", "ps_b", "ps_c"))
        ps_o = ps("ps_o", [P, TILES, D])
        prep, steps, rate_exp, act_steps = sem("prep"), sem("steps"), sem("rate_exp"), sem("act_steps")
        moments_ready, root_ready, x_ready, w_ready = sem("moments_ready"), sem("root_ready"), sem("x_ready"), sem("w_ready")
        xn_ready, xT_made, xnT_ready, xz_made, proj_ready, zT_ready, gates_made = (
            sem(n) for n in ("xn_ready", "xT_made", "xnT_ready", "xz_made", "proj_ready", "zT_ready", "gates_made"))
        soft_ready, dt_ready, decay_ready, tanh_ready, conv_ready, conv_tanh, y_ready, out_made, added, pads = (
            sem(n) for n in ("soft_ready", "dt_ready", "decay_ready", "tanh_ready", "conv_ready", "conv_tanh",
                             "y_ready", "out_made", "added", "pads"))
        block = ctx.enter_context(nc.Block())

        @block.gpsimd
        def _(pool):
            pool.memset(proj[:, :, :], 0.0).then_inc(pads, 1)
            pool.wait_ge(x_ready, 1)
            pool.tensor_tensor(g.x[:, :, :], g.x[:, :, :], x1[:, :, :], ALU.add).then_inc(pads, 1)

        @block.vector
        def _(v):
            v.wait_ge(g.loaded["L1_attn"], 16)
            step = Chain(v, prep)
            for n in range(NT):
                last = v.tensor_scalar(x1[:, n, :], g.x[:, n, :], g.moments[:, n, 0:1], g.rstd[:, n:n + 1],
                                       ALU.subtract, ALU.mult)
            last.then_inc(x_ready, 1)
            v.wait_ge(x_ready, 1)
            for n in range(NT):
                last = v.bn_stats(stats[:, n, :], x1[:, n, :])
            step(last)
            for n in range(NT):
                last = v.bn_aggr(moments[:, n, :], stats[:, n, :])
            last.then_inc(moments_ready, 1)
            v.tensor_scalar(out_d[:, :], w["outT"], w["d"], None, ALU.mult).then_inc(w_ready, 1)
            v.wait_ge(rate_exp, 1)
            v.tensor_scalar(rate[:, 1:2], rate[:, 0:1], -1.0, None, ALU.mult)
            v.tensor_scalar(rate[:, 2:3], rate[:, 0:1], -1e-4, None, ALU.mult).then_inc(w_ready, 1)
            v.wait_ge(root_ready, 1)
            step(v.reciprocal(rstd[:, :], rstd[:, :]))
            v.wait_ge(pads, 2)
            with v.Fori(0, TURNS) as t:
                step = Chain(v, steps, t, 4)
                v.wait_ge(xT_made, t)
                for j in range(TILES):
                    n = bass.ds(t * TILES + j, 1)
                    last = v.tensor_scalar(xn[:, j, :], x1[:, n, :].rearrange("p o d -> p (o d)"),
                                           moments[:, n, 0:1].rearrange("p o s -> p (o s)"), rstd[:, n],
                                           ALU.subtract, ALU.mult)
                last.then_inc(xn_ready, 1)
                v.wait_ge(proj_ready, t + 1)
                v.wait_ge(conv_tanh, t)
                v.wait_ge(out_made, t)
                step(v.tensor_scalar(conv[:, :, :], proj[:, :, 0:T], w["conv_w"][:, 0:1], None, ALU.mult))
                step(v.scalar_tensor_tensor(conv[:, :, :], proj[:, :, 1:T + 1], w["conv_w"][:, 1:2], conv[:, :, :], ALU.mult, ALU.add))
                v.scalar_tensor_tensor(conv[:, :, :], proj[:, :, 2:T + 2], w["conv_w"][:, 2:3], conv[:, :, :],
                                       ALU.mult, ALU.add).then_inc(conv_ready, 1)
                v.wait_ge(soft_ready, t + 1)
                v.scalar_tensor_tensor(soft[:, :], pre[:, :], 0.0, soft[:, :], ALU.max, ALU.add).then_inc(dt_ready, 1)
                v.wait_ge(decay_ready, t + 1)
                v.wait_ge(tanh_ready, t + 1)
                for s in range(SEQS):
                    c = slice(s * T, (s + 1) * T)
                    last = v.tensor_tensor_scan(states[:, c], decay[:, c], gate_b[:, c], 0.0, ALU.mult, ALU.add)
                step(last)
                v.tensor_tensor(states[:, :], states[:, :], gate_c[:, :], ALU.mult).then_inc(y_ready, 1)
                v.wait_ge(out_made, t + 1)
                v.tensor_tensor(tiles_of(g.x, t), tiles_of(g.x, t), ps_o[:, :, :], ALU.add).then_inc(added, 1)
                v.wait_ge(added, t + 1)
                step(take_stats(v, g, t))
                step.end()

        @block.tensor
        def _(pe):
            pe.wait_ge(g.loaded["L1_attn"], 16)
            pe.wait_ge(w_ready, 2)
            with pe.Fori(0, TURNS) as t:
                pe.wait_ge(xn_ready, t + 1)
                pe.wait_ge(xnT_ready, t)
                for j in range(TILES):
                    last = pe.transpose(ps_t[:, j * P:(j + 1) * P], xn[:, j, :], g.ident)
                last.then_inc(xT_made, 1)
                pe.wait_ge(xnT_ready, t + 1)
                pe.wait_ge(zT_ready, t)
                pe.matmul(ps_x[:, :], w["in_xT"], xnT[:, :], start=True, stop=True)
                pe.matmul(ps_z[:, :], w["in_zT"], xnT[:, :], start=True, stop=True).then_inc(xz_made, 1)
                pe.wait_ge(zT_ready, t + 1)
                pe.wait_ge(tanh_ready, t)
                for out, name in ((ps_dt, "dtT"), (ps_b, "bT"), (ps_c, "cT")):
                    last = pe.matmul(out[0:S, :], w[name], zT[:, :], start=True, stop=True)
                last.then_inc(gates_made, 1)
                pe.wait_ge(conv_tanh, t + 1)
                pe.wait_ge(y_ready, t + 1)
                pe.wait_ge(added, t)
                for j in range(TILES):
                    c = slice(j * P, (j + 1) * P)
                    pe.matmul(ps_o[:, j, :], conv[:, :, :].rearrange("p s t -> p (s t)")[:, c], out_d[:, :], start=True, stop=False)
                    pe.matmul(ps_o[:, j, :], states[:, c], w["out_yT"], start=False, stop=False)
                    last = pe.matmul(ps_o[:, j, :], g.ones[0:1, 0:P], w["out_b"], start=False, stop=True)
                last.then_inc(out_made, 1)

        @block.scalar
        def _(a):
            a.wait_ge(g.loaded["L1_attn"], 16)
            a.wait_ge(moments_ready, 1)
            a.activation(rstd[:, :], moments[:, :, 1], ACT.Sqrt, bias=g.eps).then_inc(root_ready, 1)
            a.activation(rate[:, 0:1], w["a_log"], ACT.Exp).then_inc(rate_exp, 1)
            a.wait_ge(w_ready, 2)
            a.wait_ge(pads, 1)
            with a.Fori(0, TURNS) as t:
                step = Chain(a, act_steps, t, 2)
                a.wait_ge(xT_made, t + 1)
                a.wait_ge(xz_made, t)
                a.activation(xnT[:, :], ps_t[:, :], ACT.Identity, scale=w["norm_w"], bias=w["norm_b"]).then_inc(xnT_ready, 1)
                a.wait_ge(xz_made, t + 1)
                a.wait_ge(conv_ready, t)
                a.activation(proj[:, :, 1:T + 1], ps_x[:, :].rearrange("p (s t) -> p s t", s=SEQS), ACT.Identity,
                             bias=w["in_b"][:, 0:1]).then_inc(proj_ready, 1)
                a.wait_ge(gates_made, t)
                a.activation(zT[:, :], ps_z[:, :], ACT.Identity, bias=w["in_b"][:, 1:2]).then_inc(zT_ready, 1)
                a.wait_ge(gates_made, t + 1)
                a.wait_ge(y_ready, t)
                a.activation(pre[:, :], ps_dt[0:S, :], ACT.Identity, bias=w["dt_b"])
                step(a.activation(absolute[:, :], ps_dt[0:S, :], ACT.Abs, bias=w["dt_b"]))
                step(a.activation(absolute[:, :], absolute[:, :], ACT.Exp, scale=-1.0))
                a.activation(soft[:, :], absolute[:, :], ACT.Ln, bias=1.0).then_inc(soft_ready, 1)
                a.wait_ge(dt_ready, t + 1)
                a.activation(decay[:, :], soft[:, :], ACT.Exp, scale=rate[:, 1:2], bias=rate[:, 2:3]).then_inc(decay_ready, 1)
                a.activation(gate_b[:, :], ps_b[0:S, :], ACT.Tanh, bias=w["b_b"])
                a.activation(gate_c[:, :], ps_c[0:S, :], ACT.Tanh, bias=w["c_b"]).then_inc(tanh_ready, 1)
                a.wait_ge(conv_ready, t + 1)
                a.activation(conv[:, :, :], conv[:, :, :], ACT.Tanh, bias=w["conv_b"]).then_inc(conv_tanh, 1)
                step.end()



def attention16(nc, g, w, name, tag, scale, from_x, causal, values_from_x=False, tail=None):
    NH, HD = 16, 8
    PIECES = 3
    SLOTS = ((0, 0), (1, 0), (2, 0), (0, 1), (1, 1), (0, 2))
    STEP = 8
    STACK = STEP * HD
    MAX_ROW = len(SLOTS)
    V1 = 32
    WIDE = T + P if causal else 2 * T
    PAIRS = NH // 2
    HEADS = SEQS * NH
    SIDE = 4
    GROUPS = HEADS // SIDE
    values_x = values_from_x
    uses_context = not (from_x and values_x)
    STACK_DMAS, ROW_DMAS = 2 * len(SLOTS) + 1, PIECES
    with ExitStack() as ctx:
        sb = lambda n, s, d=F32: ctx.enter_context(nc.sbuf_tensor(tag + n, s, d))
        ps = lambda n, s, d=F32: ctx.enter_context(nc.psum_tensor(tag + n, s, d))
        sem = lambda n: g.semaphore(nc, ctx, tag + n)
        xn, xnT = sb("xn", [P, TILES, D]), sb("xnT", [P, COLS])
        srcT = sb("srcT", [P, COLS])
        rest = sb("rest", [P, 2, COLS])
        pieces = sb("pieces", [P, 2, PIECES, COLS], BF16)
        queries, keys = sb("queries", [P, PAIRS, COLS], BF16), sb("keys", [P, PAIRS, COLS], BF16)
        zeros, ones16 = sb("zeros", [P, T], BF16), sb("ones16", [P, T], BF16)
        values = sb("values", [P, TILES, D])
        v_ones = sb("v_ones", [P, TILES, NH, V1])
        minus_max = sb("minus_max", [P, SEQS, HALVES, NH])
        max_rest = sb("max_rest", [NH, SEQS, T])
        max_pieces = sb("max_pieces", [NH, SEQS, PIECES, T], BF16)
        probs = sb("probs", [P, 2 * SIDE, WIDE])
        sumsT = sb("sumsT", [P, NH // SIDE, COLS])
        inverse = sb("inverse", [P, NH])
        mixed = sb("mixed", [P, TILES, NH, HD])
        mixT = sb("mixT", [P, COLS])
        hT = sb("hT", [P, 4, COLS]) if tail == "mlp" else None
        ident16 = sb("ident16", [P, P], BF16)
        if causal:
            masks = sb("masks", [P, 4, P], BF16)
        else:
            mask_int = sb("mask_int", [P, 2, TILES, T], I32)
            masks = sb("masks", [P, 2, TILES, T], BF16)
        ps_t = ps("ps_t", [P, COLS])
        ps_s = ps("ps_s", [P, 4, 512])
        ps_o = ps("ps_o", [P, 2, 512])
        ps_y = ps("ps_y", [P, TILES, D])
        ps_p = ps_y[:, :, :].rearrange("p j d -> p (j d)")
        by_head = ps_p.rearrange("p (h d) -> p h d", h=NH)
        (const_ready, ones_ready, xn_ready, xT_made, xnT_ready, src_ready, q_made, q_ready, k_made, k_ready, v_made,
         v_staged, split, v_ready, scored, reduced, max_made, max_split, st_made, exped, weighed, inverted, normed) = (
            sem(n) for n in ("const_ready", "ones_ready", "xn_ready", "xT_made", "xnT_ready", "src_ready", "q_made",
                             "q_ready", "k_made", "k_ready", "v_made", "v_staged", "split", "v_ready", "scored", "reduced",
                             "max_made", "max_split", "st_made", "exped", "weighed", "inverted", "normed"))
        sumsT_ready, back_made, mixT_made, mixT_ready, y_made, added, steps = (
            sem(n) for n in ("sumsT_ready", "back_made", "mixT_made", "mixT_ready", "y_made", "added", "steps"))
        cleared, ones_stacked, stack_free = sem("cleared"), sem("ones_stacked"), sem("stack_free")
        stacked = [sem(f"stacked{s}") for s in range(SEQS)]
        rows_ready = [sem(f"rows_ready{s}") for s in range(SEQS)]
        if tail == "mlp":
            up_made, gelu_ready = sem("up_made"), sem("gelu_ready")
        if not causal:
            mask_loaded, mask_ready = sem("mask_loaded"), sem("mask_ready")
        block = ctx.enter_context(nc.Block())
        cols = lambda s: slice(s * T, (s + 1) * T)

        def all_turns(eng, turn):
            with eng.Fori(0, TURNS - 1) as t:
                turn(t, True)
            turn(TURNS - 1, False)

        @block.sync
        def _(sp):
            def load_masks(t):
                sp.wait_ge(mask_ready, t)
                for i, which in enumerate((g.mask_qk, g.mask_kq)):
                    sp.dma_start(mask_int[:, i, :, :], which[bass.ds(t * TILES, TILES), :, :].rearrange("n p k -> p n k"))\
                      .then_inc(mask_loaded, 16)

            def stack(t, s):
                sp.wait_ge(split, t + 1)
                sp.dma_start(queries[MAX_ROW::STEP, :, cols(s)], zeros[:, :]).then_inc(stacked[s], 16)
                for slot, of in enumerate(SLOTS):
                    for which, dst in enumerate((queries, keys)):
                        sp.dma_start(dst[slot::STEP, :, cols(s)], pieces[:, which, of[which], cols(s)]).then_inc(stacked[s], 16)

            sp.wait_ge(cleared, 1)
            for k in range(PIECES):
                for s in range(SEQS):
                    sp.dma_start(keys[MAX_ROW + STEP * k::STACK, :, cols(s)], ones16[0:NH, :]).then_inc(ones_stacked, 16)
            if not causal:
                load_masks(0)
            for s in range(SEQS):
                stack(0, s)

            def turn(t, more):
                for s in range(SEQS):
                    sp.wait_ge(max_split, t * SEQS + s + 1)
                    for k in range(PIECES):
                        sp.dma_start(queries[MAX_ROW + STEP * k::STACK, :, cols(s)], max_pieces[:, s, k, :])\
                          .then_inc(rows_ready[s], 16)
                if more:
                    if not causal:
                        load_masks(t + 1)
                    for s in range(SEQS):
                        sp.wait_ge(st_made, t * HEADS + (s + 1) * NH)
                        sp.sem_inc(stack_free, 1)
                        stack(t + 1, s)

            all_turns(sp, turn)

        @block.gpsimd
        def _(pool):
            pool.wait_ge(g.loaded["context"], 32)
            pool.memset(keys[:, :, :], 0.0)
            pool.memset(queries[:, :, :], 0.0)
            pool.memset(zeros[:, :], 0.0)
            pool.memset(ones16[:, :], 1.0).then_inc(cleared, 1)
            pool.memset(v_ones[:, :, :, :], 1.0).then_inc(ones_ready, 1)
            if uses_context:
                with pool.Fori(0, TURNS) as t:
                    pool.wait_ge(v_made if not values_x else k_made, t)
                    pool.tensor_copy(srcT[:, :], g.ctxT[:, bass.ds(t * COLS, COLS)]).then_inc(src_ready, 1)

        @block.vector
        def _(v):
            v.wait_ge(g.loaded[name], 16)
            v.tensor_copy(ident16[:, :], g.ident)
            if causal:
                for i, m in enumerate(causal):
                    last = v.tensor_copy(masks[:, i, :], w[m])
                last.then_inc(const_ready, 1)
            else:
                v.nop().then_inc(const_ready, 1)
            v.wait_ge(ones_ready, 1)

            def split_in_three(step, part, source, left):
                step(v.tensor_copy(part(0), source))
                step(v.tensor_tensor(left, source, part(0), ALU.subtract))
                step(v.tensor_copy(part(1), left))
                return v.tensor_tensor(part(2), left, part(1), ALU.subtract)

            def split_projections(t, step):
                for s in range(SEQS):
                    v.wait_ge(stacked[s], t * STACK_DMAS * 16)
                for which, ready in enumerate((q_ready, k_ready)):
                    v.wait_ge(ready, t + 1)
                    last = split_in_three(step, lambda k: pieces[:, which, k, :], rest[:, which, :], rest[:, which, :])
                    if which == 0:
                        step(last)
                last.then_inc(split, 1)

            def take_values(t, s):
                v.wait_ge(v_staged, t + 1)
                j = s * HALVES
                v.tensor_copy(v_ones[:, j:j + HALVES, :, 0:HD].rearrange("p j h d -> p (j h) d"),
                              values[:, j:j + HALVES, :].rearrange("p j (h d) -> p (j h) d", h=NH)).then_inc(v_ready, 1)

            def make_masks(t):
                v.wait_ge(mask_loaded, (t + 1) * 32)
                v.tensor_scalar(masks[:, :, :, :], mask_int[:, :, :, :], 0.0, -1e20, ALU.is_equal, ALU.mult)\
                    .then_inc(mask_ready, 1)

            first = Chain(v, steps)
            normalise(v, g, 0, xn).then_inc(xn_ready, 1)
            split_projections(0, first)
            for s in range(SEQS):
                take_values(0, s)
            FIRST = first.n

            def turn(t, more):
                step = Chain(v, steps, t, STEPS)
                step.base = step.base + FIRST
                if not causal:
                    make_masks(t)

                def shift_rows(s):
                    v.wait_ge(max_made, t * SEQS + s + 1)
                    v.wait_ge(rows_ready[s], t * ROW_DMAS * 16)
                    rows = ps_t[0:NH, cols(s)]
                    split_in_three(step, lambda k: max_pieces[:, s, k, :], rows, max_rest[:, s, :]).then_inc(max_split, 1)

                for s in range(SEQS):
                    for p in range(PAIRS):
                        v.wait_ge(scored, t * SEQS * PAIRS + s * PAIRS + p + 1)
                        bank = 2 * (p % 2)
                        peaks = minus_max[:, s, :, p:p + PAIRS + 1:PAIRS]
                        if causal:
                            v.tensor_reduce(peaks[:, 0, :], ps_s[:, bank:bank + 2, 0:P], AX.X, ALU.max, negate=True)
                            last = v.tensor_reduce(peaks[:, 1, :], ps_s[:, bank:bank + 2, P:WIDE], AX.X, ALU.max, negate=True)
                        else:
                            last = v.tensor_reduce(peaks.rearrange("p j h -> p h j"),
                                                   ps_s[:, bank:bank + 2, :].rearrange("p h (j k) -> p h j k", j=HALVES),
                                                   AX.X, ALU.max, negate=True)
                        last.then_inc(reduced, 1)
                        if s > 0 and p == 1:
                            shift_rows(s - 1)
                shift_rows(SEQS - 1)
                if more:
                    v.wait_ge(xT_made, t + 1)
                    normalise(v, g, t + 1, xn).then_inc(xn_ready, 1)
                    split_projections(t + 1, step)
                for j in range(TILES):
                    v.wait_ge(back_made, t * TILES + j + 1)
                    v.reciprocal(inverse[:, :], by_head[:, :, HD]).then_inc(inverted, 1)
                    v.wait_ge(inverted, t * TILES + j + 1)
                    if j == 0 and tail:
                        v.wait_ge(mixT_made, t)
                    v.tensor_tensor(mixed[:, j, :, :], by_head[:, :, 0:HD],
                                    inverse[:, :].rearrange("p (h o) -> p h o", o=1).broadcast_to([P, NH, HD]), ALU.mult)\
                        .then_inc(normed, 1)
                    if more and j % HALVES == HALVES - 1:
                        take_values(t + 1, j // HALVES)
                if tail:
                    v.wait_ge(y_made, t + 1)
                    y = ps_y[:, :, :]
                else:
                    v.wait_ge(normed, (t + 1) * TILES)
                    y = mixed[:, :, :, :].rearrange("p n h d -> p n (h d)")
                v.tensor_tensor(tiles_of(g.x, t), tiles_of(g.x, t), y, ALU.add).then_inc(added, 1)
                v.wait_ge(added, t + 1)
                step(take_stats(v, g, t))
                if more:
                    step.end()

            STEPS = 2 * PIECES + 7 + 1
            all_turns(v, turn)

        @block.tensor
        def _(pe):
            pe.wait_ge(g.loaded[name], 16)
            pe.wait_ge(const_ready, 1)
            pe.wait_ge(ones_stacked, PIECES * SEQS * 16)

            def transpose_x(t):
                pe.wait_ge(xn_ready, t + 1)
                for j in range(TILES):
                    last = pe.transpose(ps_t[:, j * P:(j + 1) * P], xn[:, j, :], g.ident)
                last.then_inc(xT_made, 1)

            def project_queries(t):
                pe.wait_ge(xnT_ready, t + 1)
                pe.matmul(ps_p, w["q"], xnT[:, :], start=True, stop=True).then_inc(q_made, 1)

            def project_keys(t):
                if uses_context:
                    pe.wait_ge(src_ready, t + 1)
                pe.matmul(ps_t[:, :], w["k"], (xnT if from_x else srcT)[:, :], start=True, stop=True).then_inc(k_made, 1)

            def project_values(t):
                pe.wait_ge(q_ready, t + 1)
                for j in range(TILES):
                    out = ps_p[:, j * P:(j + 1) * P]
                    last = pe.matmul(out, (xnT if values_x else srcT)[:, j * P:(j + 1) * P], w["v"],
                                     start=True, stop="v_bias" not in w)
                    if "v_bias" in w:
                        last = pe.matmul(out, g.ones[0:1, 0:P], w["v_bias"], start=False, stop=True)
                last.then_inc(v_made, 1)

            transpose_x(0)
            project_queries(0)
            project_keys(0)
            project_values(0)

            def turn(t, more):
                def stack_of(of, h, col, n):
                    row = STACK * (h % 2)
                    return of[row:row + STACK, h // 2, col:col + n]

                def both_heads(banks, products, hidden, p):
                    for n, (a, b, lhs, rhs) in enumerate(products):
                        for i, out in enumerate(banks):
                            h = 2 * p + i
                            pe.matmul(out[:, a:b], lhs(h), rhs(h), start=n == 0, stop=False)
                    for out in banks:
                        for n, (a, b, mask) in enumerate(hidden):
                            last = pe.matmul(out[:, a:b], ident16[:, :], mask, start=False, stop=n == len(hidden) - 1)
                    return last

                def score_pair(s, p):
                    use = s * PAIRS + p
                    if use >= 2:
                        pe.wait_ge(reduced, t * SEQS * PAIRS + use - 1)
                    banks = [ps_s[:, 2 * (p % 2) + i, :] for i in range(2)]
                    q = lambda h, half: stack_of(queries, h, s * T + half * P, P)
                    k = lambda h, n: stack_of(keys, h, s * T, n)
                    if causal:
                        products = [(0, P, 0, P), (P, WIDE, 1, T)]
                        hidden = [(0, P, masks[:, 0, :]), (T, WIDE, masks[:, 1, :])]
                    else:
                        products = [(half * T, (half + 1) * T, half, T) for half in range(HALVES)]
                        hidden = [(half * T, (half + 1) * T, masks[:, 0, s * HALVES + half, :]) for half in range(HALVES)]
                    both_heads(banks, [(a, b, lambda h, x=half: q(h, x), lambda h, n=n: k(h, n)) for a, b, half, n in products],
                               hidden, p).then_inc(scored, 1)

                def turn_maxima(s):
                    pe.wait_ge(reduced, t * SEQS * PAIRS + (s + 1) * PAIRS)
                    for half in range(HALVES):
                        last = pe.matmul(ps_t[0:NH, s * T + half * P:s * T + (half + 1) * P], minus_max[:, s, half, :],
                                         g.ident, start=True, stop=True)
                    last.then_inc(max_made, 1)

                def shifted_pair(m):
                    s, p = divmod(m, PAIRS)
                    if p == 0:
                        pe.wait_ge(rows_ready[s], (t + 1) * ROW_DMAS * 16)
                    if m >= 2:
                        pe.wait_ge(exped, t * HEADS + 2 * (m - 1))
                    banks = [ps_s[:, 2 * (m % 2) + i, :] for i in range(2)]
                    k = lambda h, half: stack_of(keys, h, s * T + half * P, P)
                    q = lambda h, a, n: stack_of(queries, h, s * T + a, n)
                    if causal:
                        products = [(0, T, 0, 0), (T, WIDE, 1, P)]
                        hidden = [(0, P, masks[:, 2, :]), (T, WIDE, masks[:, 3, :])]
                    else:
                        products = [(half * T, (half + 1) * T, half, 0) for half in range(HALVES)]
                        hidden = [(half * T, (half + 1) * T, masks[:, 1, s * HALVES + half, :]) for half in range(HALVES)]
                    both_heads(banks, [(a, b, lambda h, x=half: k(h, x), lambda h, at=at, n=b - a: q(h, at, n))
                                       for a, b, half, at in products], hidden, p).then_inc(st_made, 2)

                def weigh(n):
                    s, group = divmod(n, GROUPS // SEQS)
                    pe.wait_ge(exped, t * HEADS + SIDE * (n + 1))
                    pe.wait_ge(sumsT_ready, t * GROUPS + max(n - 1, 0))
                    if group == 0:
                        pe.wait_ge(v_ready, t * SEQS + s + 1)
                    spans = ((0, T, 0), (P if causal else 0, T, T))
                    for half, (a, b, at) in enumerate(spans):
                        for i in range(SIDE):
                            h = SIDE * group + i
                            last = pe.matmul(ps_o[32 * i:32 * (i + 1), n % 2, a:b], v_ones[:, s * HALVES + half, h, :],
                                             probs[:, (SIDE * n + i) % (2 * SIDE), at:at + b - a], start=half == 0, stop=half == 1)
                    last.then_inc(weighed, 1)

                def turn_back(j):
                    s = j // HALVES
                    pe.wait_ge(sumsT_ready, t * GROUPS + (s + 1) * (GROUPS // SEQS))
                    pe.wait_ge(normed, t * TILES + j)
                    if j == 0:
                        if more:
                            pe.wait_ge(v_staged, t + 2)
                        pe.wait_ge(added, t)
                    for group in range(NH // SIDE):
                        last = pe.transpose(ps_p[:, group * P:(group + 1) * P], sumsT[:, group, j * P:(j + 1) * P], g.ident)
                    last.then_inc(back_made, 1)

                if not causal:
                    pe.wait_ge(mask_ready, t + 1)
                for s in range(SEQS):
                    pe.wait_ge(stacked[s], (t + 1) * STACK_DMAS * 16)
                    for p in range(PAIRS):
                        score_pair(s, p)
                        if s > 0 and p == 1:
                            pe.wait_ge(k_ready, t + 1)
                            turn_maxima(s - 1)
                turn_maxima(SEQS - 1)
                for m in range(HEADS // 2 + 1):
                    if m < HEADS // 2:
                        shifted_pair(m)
                    if m > 0 and m % 2 == 0:
                        weigh(m // 2 - 1)
                    if m in (PAIRS + 2, PAIRS + 4):
                        turn_back((m - PAIRS) // 2 - 1)
                    if more and m == 1:
                        pe.wait_ge(max_split, (t + 1) * SEQS)
                        transpose_x(t + 1)
                    if more and m == 3:
                        pe.wait_ge(added, t)
                        project_queries(t + 1)
                        project_keys(t + 1)
                    if more and m == 4:
                        project_values(t + 1)

                turn_back(2)
                turn_back(3)
                if tail:
                    if more:
                        pe.wait_ge(k_ready, t + 2)
                    pe.wait_ge(max_split, (t + 1) * SEQS)
                    pe.wait_ge(normed, (t + 1) * TILES)
                    for j in range(TILES):
                        last = pe.transpose(ps_t[:, j * P:(j + 1) * P], mixed[:, j, :, :].rearrange("p h d -> p (h d)"), g.ident)
                    last.then_inc(mixT_made, 1)
                    pe.wait_ge(mixT_ready, t + 1)
                    pe.wait_ge(added, t)
                if tail == "linear":
                    for j in range(TILES):
                        pe.matmul(ps_y[:, j, :], mixT[:, j * P:(j + 1) * P], w["out"], start=True, stop=False)
                        last = pe.matmul(ps_y[:, j, :], g.ones[0:1, 0:P], w["out_b"], start=False, stop=True)
                    last.then_inc(y_made, 1)
                if tail == "mlp":
                    for c in range(4):
                        pe.matmul(ps_s[:, c, :], w["w1"][:, c * P:(c + 1) * P], mixT[:, :], start=True, stop=True).then_inc(up_made, 1)
                    pe.wait_ge(gelu_ready, (t + 1) * 4)
                    for j in range(TILES):
                        for c in range(4):
                            pe.matmul(ps_y[:, j, :], hT[:, c, j * P:(j + 1) * P], w["w2"][:, c * P:(c + 1) * P],
                                      start=c == 0, stop=False)
                        last = pe.matmul(ps_y[:, j, :], g.ones[0:1, 0:P], w["out_b"], start=False, stop=True)
                    last.then_inc(y_made, 1)
                if not tail:
                    pe.wait_ge(exped, (t + 1) * HEADS)

            all_turns(pe, turn)

        @block.scalar
        def _(a):
            a.wait_ge(g.loaded[name], 16)

            def take_xT(t):
                a.wait_ge(xT_made, t + 1)
                a.wait_ge(v_made, t)
                a.activation(xnT[:, :], ps_t[:, :], ACT.Copy).then_inc(xnT_ready, 1)

            def take_projections(t):
                a.wait_ge(split, t)
                a.wait_ge(q_made, t + 1)
                a.activation(rest[:, 0, :], ps_p, ACT.Identity, bias=w["q_bias"]).then_inc(q_ready, 1)
                a.wait_ge(k_made, t + 1)
                a.activation(rest[:, 1, :], ps_t[:, :], ACT.Identity, bias=w["k_bias"]).then_inc(k_ready, 1)
                a.wait_ge(v_made, t + 1)
                a.wait_ge(v_ready, t * SEQS)
                a.activation(values[:, :, :].rearrange("p j d -> p (j d)"), ps_p, ACT.Copy).then_inc(v_staged, 1)

            take_xT(0)
            take_projections(0)

            def turn(t, more):
                def take_sums(n):
                    s, group = divmod(n, GROUPS // SEQS)
                    a.wait_ge(weighed, t * GROUPS + n + 1)
                    if n == 0:
                        a.wait_ge(back_made, t * TILES)
                    a.activation(sumsT[:, group, cols(s)], ps_o[:, n % 2, 0:T], ACT.Copy).then_inc(sumsT_ready, 1)

                for i in range(HEADS):
                    a.wait_ge(st_made, t * HEADS + i // 2 * 2 + 2)
                    if i % SIDE == 0:
                        a.wait_ge(weighed, t * GROUPS + max(i // SIDE - 1, 0))
                    a.activation(probs[:, i % (2 * SIDE), :], ps_s[:, i % 4, 0:WIDE], ACT.Exp, scale=scale).then_inc(exped, 1)
                    if i % SIDE == SIDE - 1 and i > SIDE:
                        take_sums(i // SIDE - 1)
                    if more and i == 4:
                        take_xT(t + 1)
                    if more and i == 8:
                        take_projections(t + 1)
                take_sums(GROUPS - 1)
                if tail:
                    a.wait_ge(mixT_made, t + 1)
                    a.activation(mixT[:, :], ps_t[:, :], ACT.Copy).then_inc(mixT_ready, 1)
                if tail == "mlp":
                    for c in range(4):
                        a.wait_ge(up_made, t * 4 + c + 1)
                        a.activation(hT[:, c, :], ps_s[:, c, :], ACT.Gelu, bias=w["b1"][:, c:c + 1]).then_inc(gelu_ready, 1)

            all_turns(a, turn)


def layer1_attention(nc, g, w):
    attention16(nc, g, w, "L1_xattn", "x1_", 1.0, from_x=True, causal=("mask0", "mask1", "mask0T", "mask1T"), tail="mlp")


def layer2_masked_attention(nc, g, w):
    attention16(nc, g, w, "L2_xattn", "x2_", D ** -0.5, from_x=False, causal=None, tail="linear")


def layer3_latent_attention(nc, g, w):
    with ExitStack() as ctx:
        sb = lambda n, s, d=F32: ctx.enter_context(nc.sbuf_tensor("a3_" + n, s, d))
        sem = lambda n: g.semaphore(nc, ctx, "a3_" + n)
        wide, narrow, values = sb("wide", [P, P]), sb("narrow", [32, P]), sb("v_eff", [32, P])
        w_q, w_k, w_v = sb("w_q", [P, P]), sb("w_k", [P, P]), sb("w_v", [P, P])
        first_made, first_ready, second_made, second_ready, third_made, third_ready = (
            sem(n) for n in ("first_made", "first_ready", "second_made", "second_ready", "third_made", "third_ready"))
        with ExitStack() as psums, nc.Block() as block:
            ps_w = psums.enter_context(nc.psum_tensor("a3_ps_w", [P, 4, 512], F32))

            @block.tensor
            def _(pe):
                pe.wait_ge(g.loaded["L3_attn"], 16)
                pe.matmul(ps_w[:, 0, 0:P], w["dq"], w["uqT"], start=True, stop=True)
                pe.matmul(ps_w[:, 1, 0:P], w["uqT_plain"], w["dq_wide"], start=True, stop=True)
                pe.matmul(ps_w[0:32, 2, 0:P], w["uv"], w["oT"], start=True, stop=True).then_inc(first_made, 1)
                pe.wait_ge(first_ready, 1)
                pe.matmul(ps_w[0:32, 3, 0:P], w["uk"], wide[:, :], start=True, stop=True).then_inc(second_made, 1)
                pe.wait_ge(second_ready, 1)
                pe.matmul(ps_w[:, 0, 0:P], w["dkv"], narrow[:, :], start=True, stop=True)
                pe.matmul(ps_w[:, 1, 0:P], w["dkv"], values[:, :], start=True, stop=True).then_inc(third_made, 1)

            @block.vector
            def _(v):
                v.wait_ge(first_made, 1)
                v.tensor_copy(w_q[:, :], ps_w[:, 0, 0:P])
                v.tensor_copy(wide[:, :], ps_w[:, 1, 0:P])
                v.tensor_copy(values[:, :], ps_w[0:32, 2, 0:P]).then_inc(first_ready, 1)
                v.wait_ge(second_made, 1)
                v.tensor_copy(narrow[:, :], ps_w[0:32, 3, 0:P]).then_inc(second_ready, 1)
                v.wait_ge(third_made, 1)
                v.tensor_copy(w_k[:, :], ps_w[:, 0, 0:P])
                v.tensor_copy(w_v[:, :], ps_w[:, 1, 0:P]).then_inc(third_ready, 1)
                v.wait_ge(third_ready, 1)
        weights = dict(w, q=w_q[:, :], k=w_k[:, :], v=w_v[:, :])
        attention16(nc, g, weights, "L3_attn", "a3_", 8 ** -0.5, from_x=True, causal=("mask", "mask", "maskT", "maskT"),
                    values_from_x=True)



def layer2_attention(nc, g, w):
    SCALE = D ** -0.5
    WIDE = T + P
    with ExitStack() as ctx:
        sb = lambda n, s, d=F32: ctx.enter_context(nc.sbuf_tensor("a2_" + n, s, d))
        ps = lambda n, s, d=F32: ctx.enter_context(nc.psum_tensor("a2_" + n, s, d))
        sem = lambda n: g.semaphore(nc, ctx, "a2_" + n)
        w_vo, ident16, mask16 = sb("w_vo", [P, D]), sb("ident16", [P, P], BF16), sb("mask16", [P, P], BF16)
        xn, xnT = sb("xn", [P, TILES, D]), sb("xnT", [P, COLS])
        qk, values = sb("qk", [P, 2, COLS]), sb("values", [P, TILES, D])
        minus_max, sums, inverse = sb("minus_max", [P, TILES]), sb("sums", [P, TILES]), sb("inverse", [P, TILES])
        probs, probsT = sb("probs", [P, TILES, T]), sb("probsT", [P, SEQS, WIDE])
        ps_t, ps_qk, ps_v = ps("ps_t", [P, COLS]), ps("ps_qk", [P, 2, COLS]), ps("ps_v", [P, TILES, D])
        ps_s, ps_pT = ps("ps_s", [P, TILES, T]), ps("ps_pT", [P, SEQS, 512])
        (w_made, w_ready, xn_ready, xT_made, xnT_ready, qkv_made, qk_ready, v_ready, scored, max_ready, exped,
         pT_made, pT_ready, y_made, added, steps) = (
            sem(n) for n in ("w_made", "w_ready", "xn_ready", "xT_made", "xnT_ready", "qkv_made", "qk_ready", "v_ready",
                             "scored", "max_ready", "exped", "pT_made", "pT_ready", "y_made", "added", "steps"))
        block = ctx.enter_context(nc.Block())

        @block.vector
        def _(v):
            v.wait_ge(g.loaded["L2_attn"], 16)
            v.tensor_copy(ident16[:, :], g.ident)
            v.tensor_copy(mask16[:, :], w["mask"])
            v.wait_ge(w_made, 1)
            v.tensor_copy(w_vo[:, :], ps_t[:, 0:D]).then_inc(w_ready, 1)
            with v.Fori(0, TURNS) as t:
                step = Chain(v, steps, t, 3)
                v.wait_ge(xT_made, t)
                normalise(v, g, t, xn).then_inc(xn_ready, 1)
                v.wait_ge(qkv_made, t + 1)
                v.tensor_copy(values[:, :, :], ps_v[:, :, :]).then_inc(v_ready, 1)
                v.wait_ge(scored, t + 1)
                tiles = ps_s[:, :, :].rearrange("p (s j) k -> p s j k", s=SEQS)
                peaks = minus_max[:, :].rearrange("p (s j) -> p s j", s=SEQS)
                v.tensor_reduce(peaks[:, :, 0], tiles[:, :, 0, 0:P], AX.X, ALU.max)
                step(v.tensor_reduce(peaks[:, :, 1], tiles[:, :, 1, :], AX.X, ALU.max))
                v.tensor_scalar(minus_max[:, :], minus_max[:, :], -SCALE, None, ALU.mult).then_inc(max_ready, 1)
                v.wait_ge(exped, t + 1)
                step(v.reciprocal(inverse[:, :], sums[:, :]))
                v.wait_ge(y_made, t + 1)
                for j in range(TILES):
                    last = v.scalar_tensor_tensor(tiles_of(g.x, t, j), ps_v[:, j, :], inverse[:, j:j + 1], tiles_of(g.x, t, j),
                                                  ALU.mult, ALU.add)
                last.then_inc(added, 1)
                v.wait_ge(added, t + 1)
                step(take_stats(v, g, t))
                step.end()

        @block.tensor
        def _(pe):
            pe.wait_ge(g.loaded["L2_attn"], 16)
            pe.matmul(ps_t[:, 0:D], w["wvT"], w["wo"], start=True, stop=True).then_inc(w_made, 1)
            pe.wait_ge(w_ready, 1)
            with pe.Fori(0, TURNS) as t:
                pe.wait_ge(xn_ready, t + 1)
                pe.wait_ge(xnT_ready, t)
                for j in range(TILES):
                    last = pe.transpose(ps_t[:, j * P:(j + 1) * P], xn[:, j, :], g.ident)
                last.then_inc(xT_made, 1)
                pe.wait_ge(xnT_ready, t + 1)
                pe.wait_ge(added, t)
                pe.matmul(ps_qk[:, 0, :], w["wq"], xnT[:, :], start=True, stop=True)
                pe.matmul(ps_qk[:, 1, :], w["wk"], xnT[:, :], start=True, stop=True)
                for j in range(TILES):
                    last = pe.matmul(ps_v[:, j, :], xnT[:, j * P:(j + 1) * P], w_vo[:, :], start=True, stop=True)
                last.then_inc(qkv_made, 1)
                pe.wait_ge(qk_ready, t + 1)
                for s in range(SEQS):
                    for half in range(HALVES):
                        j = s * HALVES + half
                        n = (half + 1) * P
                        pe.matmul(ps_s[:, j, 0:n], qk[:, 0, j * P:(j + 1) * P], qk[:, 1, s * T:s * T + n], start=True, stop=False)
                        last = pe.matmul(ps_s[:, j, n - P:n], ident16[:, :], mask16[:, :], start=False, stop=True)
                last.then_inc(scored, 1)
                pe.wait_ge(exped, t + 1)
                for s in range(SEQS):
                    for at, j, k in ((0, 0, 0), (P, 1, 0), (T, 1, P)):
                        last = pe.transpose(ps_pT[:, s, at:at + P], probs[:, s * HALVES + j, k:k + P], g.ident)
                last.then_inc(pT_made, 1)
                pe.wait_ge(pT_ready, t + 1)
                pe.wait_ge(v_ready, t + 1)
                for s in range(SEQS):
                    j = s * HALVES
                    pe.matmul(ps_v[:, j, :], probsT[:, s, 0:P], values[:, j, :], start=True, stop=True)
                    pe.matmul(ps_v[:, j + 1, :], probsT[:, s, P:T], values[:, j, :], start=True, stop=False)
                    last = pe.matmul(ps_v[:, j + 1, :], probsT[:, s, T:WIDE], values[:, j + 1, :], start=False, stop=True)
                last.then_inc(y_made, 1)

        @block.scalar
        def _(a):
            with a.Fori(0, TURNS) as t:
                a.wait_ge(xT_made, t + 1)
                a.wait_ge(qkv_made, t)
                a.activation(xnT[:, :], ps_t[:, :], ACT.Copy).then_inc(xnT_ready, 1)
                a.wait_ge(qkv_made, t + 1)
                a.activation(qk[:, :, :], ps_qk[:, :, :], ACT.Copy).then_inc(qk_ready, 1)
                a.wait_ge(max_ready, t + 1)
                for j in range(TILES):
                    n = (j % HALVES + 1) * P
                    last = a.activation(probs[:, j, 0:n], ps_s[:, j, 0:n], ACT.Exp, scale=SCALE,
                                        bias=minus_max[:, j:j + 1], accum_out=sums[:, j:j + 1])
                last.then_inc(exped, 1)
                a.wait_ge(pT_made, t + 1)
                a.activation(probsT[:, :, :], ps_pT[:, :, 0:WIDE], ACT.Copy).then_inc(pT_ready, 1)



def top_two(v, step, scratch, probs, top, rest, chosen):
    E = chosen.shape[2]
    v.memset(scratch[:, :], 0.0)
    for j in range(TILES):
        last = v.max(top[:, j, :], probs[:, j, 0:E])
    step(last)
    step(v.memset(top[:, :, 2:8], -1.0))
    v.memset(scratch[:, :], 0.0)
    for j in range(TILES):
        last = v.match_replace(rest[:, j, :], top[:, j, :], probs[:, j, :], -2.0)
    step(last)
    step(v.tensor_tensor(chosen[:, :, :], rest[:, :, 0:E], probs[:, :, 0:E], ALU.not_equal))
    step(v.tensor_tensor(chosen[:, :, :], chosen[:, :, :], probs[:, :, 0:E], ALU.mult))


TOP_TWO_STEPS = 5


def layer2_experts(nc, g, w):
    E, CH = 8, 2
    ITEMS = E + 1
    CHUNKS = ITEMS * CH
    with ExitStack() as ctx:
        sb = lambda n, s, d=F32: ctx.enter_context(nc.sbuf_tensor("f2_" + n, s, d))
        ps = lambda n, s, d=F32: ctx.enter_context(nc.psum_tensor("f2_" + n, s, d))
        sem = lambda n: g.semaphore(nc, ctx, "f2_" + n)
        xn, xnT = sb("xn", [P, TILES, D]), sb("xnT", [P, COLS])
        peak, total, scratch = sb("peak", [P, TILES]), sb("total", [P, TILES]), sb("scratch", [P, 1])
        top, chosen = sb("top", [P, TILES, 8]), sb("chosen", [P, TILES, E])
        probs, rest = sb("probs", [P, TILES, E + 6]), sb("rest", [P, TILES, E + 6])
        chosenT = sb("chosenT", [E, COLS])
        hT = sb("hT", [P, 4, COLS])
        ps_t, ps_r = ps("ps_t", [P, COLS]), ps("ps_r", [P, TILES, E])
        ps_h, ps_y = ps("ps_h", [P, 2, COLS]), ps("ps_y", [P, 2, TILES, D])
        (xn_ready, xT_made, xnT_ready, routed, shifted, exped, chosen_ready, chosenT_made, chosenT_ready,
         up_made, gelu_ready, down_made, added, steps, padded) = (
            sem(n) for n in ("xn_ready", "xT_made", "xnT_ready", "routed", "shifted", "exped", "chosen_ready",
                             "chosenT_made", "chosenT_ready", "up_made", "gelu_ready", "down_made", "added", "steps", "padded"))
        block = ctx.enter_context(nc.Block())
        per_token = lambda a: a[:, :].rearrange("p (j o) -> p j o", o=1).broadcast_to([P, TILES, E])

        @block.vector
        def _(v):
            v.memset(probs[:, :, E:E + 6], -1.0).then_inc(padded, 1)
            v.wait_ge(padded, 1)
            with v.Fori(0, TURNS) as t:
                step = Chain(v, steps, t, TOP_TWO_STEPS + 5)
                v.wait_ge(xT_made, t)
                normalise(v, g, t, xn).then_inc(xn_ready, 1)
                v.wait_ge(routed, t + 1)
                step(v.tensor_reduce(peak[:, :], ps_r[:, :, :], AX.X, ALU.max))
                v.tensor_tensor(probs[:, :, 0:E], ps_r[:, :, :], per_token(peak), ALU.subtract).then_inc(shifted, 1)
                v.wait_ge(exped, t + 1)
                step(v.tensor_reduce(total[:, :], probs[:, :, 0:E], AX.X, ALU.add))
                step(v.reciprocal(total[:, :], total[:, :]))
                step(v.tensor_tensor(probs[:, :, 0:E], probs[:, :, 0:E], per_token(total), ALU.mult))
                top_two(v, step, scratch, probs, top, rest, chosen)
                v.sem_inc(chosen_ready, 1)
                for e in range(ITEMS):
                    v.wait_ge(down_made, t * ITEMS + e + 1)
                    if e > 0:
                        v.wait_ge(added, t * ITEMS + e)
                    if e < E:
                        for j in range(TILES):
                            last = v.scalar_tensor_tensor(tiles_of(g.x, t, j), ps_y[:, e % 2, j, :], chosen[:, j, e:e + 1],
                                                          tiles_of(g.x, t, j), ALU.mult, ALU.add)
                    else:
                        last = v.tensor_tensor(tiles_of(g.x, t), tiles_of(g.x, t), ps_y[:, e % 2, :, :], ALU.add)
                    last.then_inc(added, 1)
                v.wait_ge(added, (t + 1) * ITEMS)
                step(take_stats(v, g, t))
                step.end()

        @block.tensor
        def _(pe):
            pe.wait_ge(g.loaded["L2_ffn"], 16)

            def up(t, i):
                pe.wait_ge(gelu_ready, t * CHUNKS + max(i - 1, 0))
                pe.matmul(ps_h[:, i % 2, :], w["up"][:, i * P:(i + 1) * P], xnT[:, :], start=True, stop=True).then_inc(up_made, 1)

            def down(t, e):
                pe.wait_ge(gelu_ready, t * CHUNKS + CH * (e + 1))
                pe.wait_ge(added, t * ITEMS + max(e - 1, 0))
                if e == E:
                    pe.wait_ge(chosenT_ready, t + 1)
                for j in range(TILES):
                    out = ps_y[:, e % 2, j, :]
                    for c in range(CH):
                        i = CH * e + c
                        last = pe.matmul(out, hT[:, i % 4, j * P:(j + 1) * P], w["down"][:, i * P:(i + 1) * P],
                                         start=c == 0, stop=c == CH - 1 and e < E)
                    if e == E:
                        pe.matmul(out, g.ones[0:1, 0:P], w["shared_b2"], start=False, stop=False)
                        last = pe.matmul(out, chosenT[:, j * P:(j + 1) * P], w["expert_b2"], start=False, stop=True)
                last.then_inc(down_made, 1)

            with pe.Fori(0, TURNS) as t:
                pe.wait_ge(xn_ready, t + 1)
                pe.wait_ge(chosenT_ready, t)
                for j in range(TILES):
                    last = pe.transpose(ps_t[:, j * P:(j + 1) * P], xn[:, j, :], g.ident)
                last.then_inc(xT_made, 1)
                pe.wait_ge(xnT_ready, t + 1)
                pe.wait_ge(shifted, t)
                for j in range(TILES):
                    pe.matmul(ps_r[:, j, :], xnT[:, j * P:(j + 1) * P], w["router"], start=True, stop=False)
                    last = pe.matmul(ps_r[:, j, :], g.ones[0:1, 0:P], w["router_b"], start=False, stop=True)
                last.then_inc(routed, 1)
                for e in range(ITEMS + 1):
                    if e < ITEMS:
                        for c in range(CH):
                            up(t, CH * e + c)
                    if e == 5:
                        pe.wait_ge(chosen_ready, t + 1)
                        for j in range(TILES):
                            last = pe.matmul(ps_t[0:E, j * P:(j + 1) * P], chosen[:, j, :], g.ident, start=True, stop=True)
                        last.then_inc(chosenT_made, 1)
                    if e > 0:
                        down(t, e - 1)

        @block.scalar
        def _(a):
            a.wait_ge(g.loaded["L2_ffn"], 16)
            with a.Fori(0, TURNS) as t:
                a.wait_ge(xT_made, t + 1)
                a.wait_ge(up_made, t * CHUNKS)
                a.activation(xnT[:, :], ps_t[:, :], ACT.Copy).then_inc(xnT_ready, 1)
                a.wait_ge(shifted, t + 1)
                a.activation(probs[:, :, 0:E], probs[:, :, 0:E], ACT.Exp).then_inc(exped, 1)
                for i in range(CHUNKS):
                    a.wait_ge(up_made, t * CHUNKS + i + 1)
                    a.wait_ge(down_made, t * ITEMS + max(i // CH - 1, 0))
                    a.activation(hT[:, i % 4, :], ps_h[:, i % 2, :], ACT.Gelu, bias=w["b1"][:, i:i + 1]).then_inc(gelu_ready, 1)
                    if i == 12:
                        a.wait_ge(chosenT_made, t + 1)
                        a.activation(chosenT[:, :], ps_t[0:E, :], ACT.Copy).then_inc(chosenT_ready, 1)



def layer3_block(nc, g, w):
    SCALE = 8 ** -0.5
    SELF, CROSS = 0, 1
    HIDE = -1e30
    with ExitStack() as ctx:
        sb = lambda n, s, d=F32: ctx.enter_context(nc.sbuf_tensor("x3_" + n, s, d))
        ps = lambda n, s, d=F32: ctx.enter_context(nc.psum_tensor("x3_" + n, s, d))
        sem = lambda n: g.semaphore(nc, ctx, "x3_" + n)
        tokens = sb("tokens", [P, TILES, D])
        tokensT, srcT = sb("tokensT", [P, COLS]), sb("srcT", [P, COLS])
        qk, values = sb("qk", [P, 2, COLS]), sb("values", [P, TILES, D])
        nonzero, count = sb("nonzero", [1, SEQS, T]), sb("count", [1, SEQS])
        counts = sb("counts", [P, SEQS])
        mask = sb("mask", [P, SEQS, HALVES, T])
        scores, probsT = sb("scores", [P, TILES, T]), sb("probsT", [P, SEQS, 512])
        minus_max, sums, inverse = sb("minus_max", [P, TILES]), sb("sums", [P, TILES]), sb("inverse", [P, TILES])
        stats, moments, rstd = sb("stats", [P, TILES, 6]), sb("moments", [P, TILES, 2]), sb("rstd", [P, TILES])
        exponent, scratch, hT = sb("exponent", [P, TILES]), sb("scratch", [P, 1]), sb("hT", [P, COLS])
        ps_t, ps_qk, ps_v = ps("ps_t", [P, COLS]), ps("ps_qk", [P, 2, COLS]), ps("ps_v", [P, TILES, D])
        ps_s, ps_pT = ps("ps_s", [P, TILES, T]), ps("ps_pT", [P, SEQS, 512])
        (tokens_ready, tT_made, tT_ready, src_ready, qkv_made, qk_ready, v_ready, scored, counted, count_made,
         max_ready, exped, pT_made, pT_ready, z_made, var_ready, rstd_ready, h_made, h_ready, y_made, added,
         steps, pool_steps, const_ready) = (
            sem(n) for n in ("tokens_ready", "tT_made", "tT_ready", "src_ready", "qkv_made", "qk_ready", "v_ready",
                             "scored", "counted", "count_made", "max_ready", "exped", "pT_made", "pT_ready", "z_made",
                             "var_ready", "rstd_ready", "h_made", "h_ready", "y_made", "added", "steps", "pool_steps",
                             "const_ready"))
        block = ctx.enter_context(nc.Block())

        @block.gpsimd
        def _(pool):
            pool.wait_ge(g.loaded["context"], 32)
            pool.memset(exponent[:, :], -0.5).then_inc(const_ready, 1)
            pool.wait_ge(const_ready, 1)
            with pool.Fori(0, TURNS) as t:
                step = Chain(pool, pool_steps, t, 3)
                pool.wait_ge(qkv_made, t * 2)
                pool.tensor_copy(srcT[:, :], g.ctxT[:, bass.ds(t * COLS, COLS)]).then_inc(src_ready, 1)
                for k in range(3):
                    pool.wait_ge(var_ready, t * 3 + k + 1)
                    step(pool.tensor_tensor(rstd[:, :], moments[:, :, 1], g.eps.broadcast_to([P, TILES]), ALU.add))
                    pool.tensor_tensor(rstd[:, :], rstd[:, :], exponent[:, :], ALU.pow).then_inc(rstd_ready, 1)
                step.end()

        @block.vector
        def _(v):
            v.wait_ge(g.loaded["L3_xattn"], 16)

            def attend(t, step, which):
                v.wait_ge(qkv_made, t * 2 + which + 1)
                v.tensor_copy(values[:, :, :], ps_v[:, :, :]).then_inc(v_ready, 1)
                v.wait_ge(scored, t * 2 + which + 1)
                first = ps_s[0:1, :, :].rearrange("p (s j) k -> p s j k", s=SEQS)[:, :, 0, :]
                step(v.tensor_scalar(nonzero[:, :, :], first, 0.0, None, ALU.not_equal))
                v.tensor_reduce(count[:, :], nonzero[:, :, :], AX.X, ALU.add).then_inc(counted, 1)
                v.wait_ge(count_made, t * 2 + which + 1)
                step(v.tensor_copy(counts[:, :], ps_t[:, 0:SEQS]))
                for s in range(SEQS):
                    for half in range(HALVES):
                        last = v.tensor_scalar(mask[:, s, half, :], w["key_index"], counts[:, s:s + 1], HIDE, ALU.is_ge, ALU.mult)
                step(last)
                if which == SELF:
                    for s in range(SEQS):
                        last = v.tensor_tensor(mask[:, s, :, :], mask[:, s, :, :],
                                               w["causal"].rearrange("p (j k) -> p j k", j=HALVES), ALU.add)
                    step(last)
                step(v.tensor_tensor(scores[:, :, :], ps_s[:, :, :], mask[:, :, :, :].rearrange("p s j k -> p (s j) k"), ALU.add))
                step(v.tensor_reduce(minus_max[:, :], scores[:, :, :], AX.X, ALU.max))
                v.tensor_scalar(minus_max[:, :], minus_max[:, :], -SCALE, None, ALU.mult).then_inc(max_ready, 1)
                v.wait_ge(exped, t * 2 + which + 1)
                step(v.reciprocal(inverse[:, :], sums[:, :]))
                v.wait_ge(z_made, t * 2 + which + 1)
                for j in range(TILES):
                    last = v.scalar_tensor_tensor(tokens[:, j, :], ps_v[:, j, :], inverse[:, j:j + 1], tokens[:, j, :],
                                                  ALU.mult, ALU.add)
                step(last)

            def layer_norm(t, step, k):
                for j in range(TILES):
                    last = v.bn_stats(stats[:, j, :], tokens[:, j, :])
                step(last)
                v.memset(scratch[:, :], 0.0)
                for j in range(TILES):
                    last = v.bn_aggr(moments[:, j, :], stats[:, j, :])
                last.then_inc(var_ready, 1)
                v.wait_ge(rstd_ready, t * 3 + k + 1)
                for j in range(TILES):
                    last = v.tensor_scalar(tokens[:, j, :], tokens[:, j, :], moments[:, j, 0:1], rstd[:, j:j + 1],
                                           ALU.subtract, ALU.mult)
                step(last)
                spread = lambda m: m.rearrange("p (o d) -> p o d", o=1).broadcast_to([P, TILES, D])
                step(v.tensor_tensor(tokens[:, :, :], tokens[:, :, :], spread(w["gains"][:, k * D:(k + 1) * D]), ALU.mult))
                return v.tensor_tensor(tokens[:, :, :], tokens[:, :, :], spread(w["biases"][:, k * D:(k + 1) * D]), ALU.add)

            with v.Fori(0, TURNS) as t:
                step = Chain(v, steps, t, 27)
                normalise(v, g, t, tokens).then_inc(tokens_ready, 1)
                v.wait_ge(tokens_ready, t * 3 + 1)
                for which in (SELF, CROSS):
                    attend(t, step, which)
                    layer_norm(t, step, which).then_inc(tokens_ready, 1)
                    v.wait_ge(tokens_ready, t * 3 + which + 2)
                v.wait_ge(h_made, t + 1)
                v.tensor_scalar(hT[:, :], ps_qk[:, 0, :], w["fc1_b"], 0.0, ALU.add, ALU.max).then_inc(h_ready, 1)
                v.wait_ge(y_made, t + 1)
                step(v.tensor_tensor(tokens[:, :, :], tokens[:, :, :], ps_v[:, :, :], ALU.add))
                step(layer_norm(t, step, 2))
                v.tensor_tensor(tiles_of(g.x, t), tiles_of(g.x, t), tokens[:, :, :], ALU.add).then_inc(added, 1)
                v.wait_ge(added, t + 1)
                step(take_stats(v, g, t))
                step.end()

        @block.tensor
        def _(pe):
            pe.wait_ge(g.loaded["L3_xattn"], 16)

            def transpose(t, k):
                pe.wait_ge(tokens_ready, t * 3 + k + 1)
                for j in range(TILES):
                    last = pe.transpose(ps_t[:, j * P:(j + 1) * P], tokens[:, j, :], g.ident)
                last.then_inc(tT_made, 1)
                pe.wait_ge(tT_ready, t * 3 + k + 1)

            def attend(t, which):
                keys_from = tokensT if which == SELF else srcT
                pe.matmul(ps_qk[:, 0, :], w["q%d" % which], tokensT[:, :], start=True, stop=True)
                if which == CROSS:
                    pe.wait_ge(src_ready, t + 1)
                pe.matmul(ps_qk[:, 1, :], w["k%d" % which], keys_from[:, :], start=True, stop=True)
                for j in range(TILES):
                    last = pe.matmul(ps_v[:, j, :], keys_from[:, j * P:(j + 1) * P], w["v%d" % which], start=True, stop=True)
                last.then_inc(qkv_made, 1)
                pe.wait_ge(qk_ready, t * 2 + which + 1)
                for j in range(TILES):
                    s = j // HALVES
                    last = pe.matmul(ps_s[:, j, :], qk[:, 0, j * P:(j + 1) * P], qk[:, 1, s * T:(s + 1) * T], start=True, stop=True)
                last.then_inc(scored, 1)
                pe.wait_ge(counted, t * 2 + which + 1)
                pe.matmul(ps_t[:, 0:SEQS], g.ones[0:1, 0:P], count[:, :], start=True, stop=True).then_inc(count_made, 1)
                pe.wait_ge(exped, t * 2 + which + 1)
                for s in range(SEQS):
                    for half in range(HALVES):
                        for q in range(half if which == SELF else 0, HALVES):
                            last = pe.transpose(ps_pT[:, s, half * T + q * P:half * T + (q + 1) * P],
                                                scores[:, s * HALVES + q, half * P:(half + 1) * P], g.ident)
                last.then_inc(pT_made, 1)
                pe.wait_ge(pT_ready, t * 2 + which + 1)
                pe.wait_ge(v_ready, t * 2 + which + 1)
                for s in range(SEQS):
                    for q in range(HALVES):
                        halves = range(q + 1) if which == SELF else range(HALVES)
                        for half in halves:
                            last = pe.matmul(ps_v[:, s * HALVES + q, :], probsT[:, s, half * T + q * P:half * T + (q + 1) * P],
                                             values[:, s * HALVES + half, :], start=half == 0, stop=half == halves[-1])
                last.then_inc(z_made, 1)

            with pe.Fori(0, TURNS) as t:
                for which in (SELF, CROSS):
                    transpose(t, which)
                    attend(t, which)
                transpose(t, 2)
                pe.matmul(ps_qk[:, 0, :], w["fc1"], tokensT[:, :], start=True, stop=True).then_inc(h_made, 1)
                pe.wait_ge(h_ready, t + 1)
                for j in range(TILES):
                    pe.matmul(ps_v[:, j, :], hT[:, j * P:(j + 1) * P], w["fc2"], start=True, stop=False)
                    last = pe.matmul(ps_v[:, j, :], g.ones[0:1, 0:P], w["fc2_b"], start=False, stop=True)
                last.then_inc(y_made, 1)

        @block.scalar
        def _(a):
            with a.Fori(0, TURNS) as t:
                for k in range(3):
                    a.wait_ge(tT_made, t * 3 + k + 1)
                    a.activation(tokensT[:, :], ps_t[:, :], ACT.Copy).then_inc(tT_ready, 1)
                    if k == 2:
                        continue
                    a.wait_ge(qkv_made, t * 2 + k + 1)
                    a.activation(qk[:, :, :], ps_qk[:, :, :], ACT.Copy).then_inc(qk_ready, 1)
                    a.wait_ge(max_ready, t * 2 + k + 1)
                    for j in range(TILES):
                        last = a.activation(scores[:, j, :], scores[:, j, :], ACT.Exp, scale=SCALE,
                                            bias=minus_max[:, j:j + 1], accum_out=sums[:, j:j + 1])
                    last.then_inc(exped, 1)
                    a.wait_ge(pT_made, t * 2 + k + 1)
                    pT = ps_pT[:, :, :].rearrange("p s (h k) -> p s h k", h=HALVES)
                    to = probsT[:, :, :].rearrange("p s (h k) -> p s h k", h=HALVES)
                    if k == SELF:
                        a.activation(to[:, :, 0, :], pT[:, :, 0, :], ACT.Copy)
                        a.activation(to[:, :, 1, P:T], pT[:, :, 1, P:T], ACT.Copy).then_inc(pT_ready, 1)
                    else:
                        a.activation(probsT[:, :, :], ps_pT[:, :, :], ACT.Copy).then_inc(pT_ready, 1)



TREES, FAN, DEPTH = 4, 4, 5
NODES = (FAN ** (DEPTH + 1) - 1) // (FAN - 1)
DENSE = 4
ABOVE = [(FAN ** d - 1) // (FAN - 1) for d in range(DEPTH + 1)]
WIDTHS = [TREES * FAN ** (d + 1) for d in range(DENSE)]
ROW = 2 * FAN * D + FAN


def layer1_trees(nc, g, w):
    Q = TILES * TREES
    CHUNKS = [max(n // P, 1) for n in WIDTHS]
    ROWS = [min(n, P) for n in WIDTHS]
    ALL = sum(CHUNKS)
    LOW = DEPTH + 1 - DENSE
    ITEMS = LOW * TILES
    FOLDED = TREES * FAN // 2
    with ExitStack() as ctx:
        sb = lambda n, s, d=F32: ctx.enter_context(nc.sbuf_tensor("f1_" + n, s, d))
        ps = lambda n, s, d=F32: ctx.enter_context(nc.psum_tensor("f1_" + n, s, d))
        sem = lambda n: g.semaphore(nc, ctx, "f1_" + n)
        xn, xnT = sb("xn", [P, TILES, D]), sb("xnT", [P, COLS])
        act = [sb("act%d" % d, [P, Q, FAN ** d, FAN]) for d in range(DENSE)]
        here = [sb("here%d" % d, [P, Q, FAN ** d]) for d in range(1, DENSE)]
        low_act = sb("low_act", [P, Q, FAN])
        value, rank_of = sb("value", [P, Q, FAN]), sb("rank_of", [P, Q, FAN])
        peak, node = sb("peak", [P, Q]), sb("node", [P, Q])
        index = sb("index", [P, LOW, Q], U32)
        maskedT = sb("maskedT", [P, ALL, P])
        rows = sb("rows", [P, TILES, TREES, ROW])
        product = sb("product", [P, 2, TREES * FAN, D])
        ps_t, ps_in, ps_o = ps("ps_t", [P, COLS]), ps("ps_in", [P, 3, 512]), ps("ps_o", [P, TILES, 512])
        (xn_ready, xT_made, xnT_ready, in_made, act_ready, masked, mT_made, mT_ready, index_ready, dots_ready,
         low_ready, product_ready, dense_summed, summed, added, steps) = (
            sem(n) for n in ("xn_ready", "xT_made", "xnT_ready", "in_made", "act_ready", "masked", "mT_made", "mT_ready",
                             "index_ready", "dots_ready", "low_ready", "product_ready", "dense_summed", "summed", "added",
                             "steps"))
        gathered = g.gathered
        may_gather, rows_used, biased = sem("may_gather"), sem("rows_used"), sem("biased")
        block = ctx.enter_context(nc.Block())
        spread = lambda a, n: a.rearrange("p (q o) -> p q o", o=1).broadcast_to([P, Q, n])
        level_at = [2 * 512 + sum(WIDTHS[:d]) for d in range(DENSE - 1)] + [0]
        ps_flat = ps_in[:, :, :].rearrange("p b n -> p (b n)")
        chunks = [(d, ROWS[d], c * P) for d in (3, 2, 1, 0) for c in range(CHUNKS[d])]

        @block.gpsimd
        def _(pool):
            with pool.Fori(0, TURNS) as t:
                for n in range(ITEMS):
                    low, j = divmod(n, TILES)
                    pool.wait_ge(index_ready, t * ITEMS + max(n + 1, TILES))
                    pool.sem_inc(may_gather, 1)
                    if low > 0:
                        pool.wait_ge(rows_used, t * ITEMS + n - TILES + 1)
                        pool.sem_inc(may_gather, 1)
                    for tree in range(TREES):
                        pool.indirect_dma_start(
                            rows[:, j, tree, :], None, g.tree_table,
                            bass.IndirectOffsetOnAxis(index[:, low, j * TREES + tree:j * TREES + tree + 1], 0),
                        ).then_inc(gathered[j], 16)

        @block.vector
        def _(v):
            v.wait_ge(g.loaded["L1_ffn"], 16)

            def descend(step, values, q=slice(0, Q), first=False):
                n = q.stop - q.start
                to_children = peak[:, q].rearrange("p (q o) -> p q o", o=1).broadcast_to([P, n, FAN])
                ranks = w["ranks"].rearrange("p (q f) -> p q f", f=FAN)[:, 0:n, :]
                step(v.tensor_reduce(peak[:, q], values, AX.X, ALU.max))
                step(v.tensor_tensor(rank_of[:, q, :], values, to_children, ALU.is_equal))
                step(v.tensor_tensor(rank_of[:, q, :], rank_of[:, q, :], ranks, ALU.mult))
                if first:
                    v.memset(node[:, :], float(FAN))
                else:
                    v.tensor_scalar(node[:, q], node[:, q], float(FAN), float(FAN), ALU.mult, ALU.add)
                step(v.tensor_reduce(peak[:, q], rank_of[:, q, :], AX.X, ALU.max))
                return v.tensor_tensor(node[:, q], node[:, q], peak[:, q], ALU.subtract)

            with v.Fori(0, TURNS) as t:
                step = Chain(v, steps, t, 60)
                v.wait_ge(xT_made, t)
                normalise(v, g, t, xn).then_inc(xn_ready, 1)
                for j in range(TILES):
                    v.wait_ge(in_made, t * TILES + j + 1)
                    if j == 0:
                        v.wait_ge(dense_summed, t)
                    for d in range(DENSE):
                        at = slice(level_at[d], level_at[d] + WIDTHS[d])
                        last = v.tensor_tensor(act[d][:, j * TREES:(j + 1) * TREES, :, :].rearrange("p q c f -> p (q c f)"),
                                               ps_flat[:, at], w["bias"][:, at], ALU.add)
                    last.then_inc(biased, 1)
                v.wait_ge(act_ready, (t + 1) * TILES)
                step(descend(step, act[0][:, :, 0, :], first=True))
                for d in range(1, DENSE):
                    above = here[d - 2][:, :, :] if d > 1 else None
                    pick = v.tensor_tensor(value[:, :, :], rank_of[:, :, :], spread(peak[:, :], FAN), ALU.is_equal)
                    step(pick)
                    if d == 1:
                        step(v.tensor_copy(here[0][:, :, :], value[:, :, :]))
                    else:
                        n = FAN ** (d - 1)
                        for tile in range(TILES):
                            q = slice(tile * TREES, (tile + 1) * TREES)
                            last = v.tensor_tensor(
                                here[d - 1][:, q, :].rearrange("p q (c f) -> p q c f", f=FAN),
                                above[:, q, :].rearrange("p q (c o) -> p q c o", o=1).broadcast_to([P, TREES, n, FAN]),
                                value[:, q, :].rearrange("p q (o f) -> p q o f", o=1).broadcast_to([P, TREES, n, FAN]), ALU.mult)
                        step(last)
                    m = FAN ** d
                    step(v.tensor_tensor(act[d][:, :, :, :], act[d][:, :, :, :],
                                         here[d - 1][:, :, :].rearrange("p q (c o) -> p q c o", o=1).broadcast_to([P, Q, m, FAN]),
                                         ALU.mult))
                    step(v.tensor_reduce(value[:, :, :], act[d][:, :, :, :].rearrange("p q c f -> p q f c"), AX.X, ALU.add))
                    last = descend(step, value[:, :, :])
                    if d < DENSE - 1:
                        step(last)
                last.then_inc(masked, 1)
                v.wait_ge(masked, t + 1)

                def point(low, q):
                    return v.tensor_tensor(index[:, low, q], node[:, q], w["first_row"][:, low * Q + q.start:low * Q + q.stop], ALU.add)

                def tile_of(n):
                    low, j = divmod(n, TILES)
                    return low, j, slice(j * TREES, (j + 1) * TREES)

                def dots(n):
                    low, j, q = tile_of(n)
                    v.wait_ge(gathered[j], (t * LOW + low + 1) * TREES * 16)
                    for k in range(TREES * FAN):
                        tree, f = divmod(k, FAN)
                        row = rows[:, j, tree, f * D:(f + 1) * D]
                        last = v.tensor_tensor_reduce(row, row, xn[:, j, :], 1.0, 0.0,
                                                      ALU.mult, ALU.add, low_act[:, j * TREES + tree, f:f + 1])
                    step(last)
                    v.tensor_tensor(low_act[:, q, :], low_act[:, q, :], rows[:, j, :, 2 * FAN * D:ROW], ALU.add)\
                        .then_inc(dots_ready, 1)

                def use(n):
                    low, j, q = tile_of(n)
                    v.wait_ge(low_ready, t * ITEMS + n + 1)
                    if low < LOW - 1:
                        step(descend(step, low_act[:, q, :], q))
                        point(low + 1, q).then_inc(index_ready, 1)
                    v.wait_ge(summed, t * ITEMS + max(n - 1, 0))
                    v.tensor_tensor(product[:, n % 2, :, :].rearrange("p (r f) d -> p r f d", f=FAN),
                                    rows[:, j, :, FAN * D:2 * FAN * D].rearrange("p r (f d) -> p r f d", f=FAN),
                                    low_act[:, q, :].rearrange("p r (f o) -> p r f o", o=1)
                                    .broadcast_to([P, TREES, FAN, D]), ALU.mult).then_inc(rows_used, 1)
                    v.wait_ge(rows_used, t * ITEMS + n + 1)
                    v.tensor_tensor(product[:, n % 2, 0:FOLDED, :], product[:, n % 2, 0:FOLDED, :],
                                    product[:, n % 2, FOLDED:2 * FOLDED, :], ALU.add).then_inc(product_ready, 1)

                point(0, slice(0, Q)).then_inc(index_ready, TILES)
                for n in range(ITEMS + 1):
                    if n < ITEMS:
                        dots(n)
                    if n > 0:
                        use(n - 1)
                v.wait_ge(summed, (t + 1) * ITEMS)
                v.tensor_tensor(tiles_of(g.x, t), tiles_of(g.x, t), ps_o[:, :, 0:D], ALU.add).then_inc(added, 1)
                v.wait_ge(added, t + 1)
                step(take_stats(v, g, t))
                step.end()

        @block.tensor
        def _(pe):
            pe.wait_ge(g.loaded["L1_ffn"], 16)
            with pe.Fori(0, TURNS) as t:
                pe.wait_ge(xn_ready, t + 1)
                for j in range(TILES):
                    last = pe.transpose(ps_t[:, j * P:(j + 1) * P], xn[:, j, :], g.ident)
                last.then_inc(xT_made, 1)
                pe.wait_ge(xnT_ready, t + 1)
                for j in range(TILES):
                    if j > 0:
                        pe.wait_ge(biased, t * TILES + j)
                    x = xnT[:, j * P:(j + 1) * P]
                    for at, n in ((0, 512), (512, 512), (1024, sum(WIDTHS[:3]))):
                        last = pe.matmul(ps_flat[:, at:at + n], x, w["in"][:, at:at + n], start=True, stop=True)
                    last.then_inc(in_made, 1)
                pe.wait_ge(masked, t + 1)
                pe.wait_ge(added, t)
                for j in range(TILES):
                    for i, (d, k, at) in enumerate(chunks):
                        flat = act[d][:, j * TREES:(j + 1) * TREES, :, :].rearrange("p q c f -> p (q c f)")
                        last = pe.transpose(ps_flat[0:k, i * P:(i + 1) * P], flat[:, at:at + k], g.ident)
                    last.then_inc(mT_made, 1)
                    pe.wait_ge(mT_ready, t * TILES + j + 1)
                    for i, (d, k, at) in enumerate(chunks):
                        last = pe.matmul(ps_o[:, j, 0:D], maskedT[0:k, i, :], w["out"][0:k, i * P:(i + 1) * P],
                                         start=i == 0, stop=False)
                last.then_inc(dense_summed, 1)
                for n in range(ITEMS):
                    pe.wait_ge(product_ready, t * ITEMS + n + 1)
                    for k in range(FOLDED):
                        last = pe.matmul(ps_o[:, n % TILES, 0:D], g.ident, product[:, n % 2, k, :], start=False,
                                         stop=n >= ITEMS - TILES and k == FOLDED - 1)
                    last.then_inc(summed, 1)

        @block.scalar
        def _(a):
            with a.Fori(0, TURNS) as t:
                a.wait_ge(xT_made, t + 1)
                a.activation(xnT[:, :], ps_t[:, :], ACT.Copy).then_inc(xnT_ready, 1)
                for j in range(TILES):
                    a.wait_ge(biased, t * TILES + j + 1)
                    for d in range(DENSE):
                        part = act[d][:, j * TREES:(j + 1) * TREES, :, :].rearrange("p q c f -> p (q c f)")
                        last = a.activation(part, part, ACT.Gelu)
                    last.then_inc(act_ready, 1)
                for j in range(TILES):
                    a.wait_ge(mT_made, t * TILES + j + 1)
                    full = CHUNKS[3] + CHUNKS[2]
                    a.activation(maskedT[:, 0:full, :].rearrange("p c n -> p (c n)"), ps_flat[:, 0:full * P], ACT.Copy)
                    for i in range(full, ALL):
                        k = chunks[i][1]
                        last = a.activation(maskedT[0:k, i, :], ps_flat[0:k, i * P:(i + 1) * P], ACT.Copy)
                    last.then_inc(mT_ready, 1)
                for n in range(ITEMS):
                    part = low_act[:, n % TILES * TREES:(n % TILES + 1) * TREES, :]
                    a.wait_ge(dots_ready, t * ITEMS + n + 1)
                    a.activation(part, part, ACT.Gelu).then_inc(low_ready, 1)




def layer3_rotary_experts(nc, g, w):
    NH, PLAIN, HD, LATENTS = 16, 32, 64, 16
    PAIRS = NH // 2
    WIDE = T + P
    ITEMS = SEQS * NH
    E, HIDDEN = 8, 64
    EXPERTS = E + 1
    GROUPS = (EXPERTS + 1) // 2
    RING = 3
    with ExitStack() as ctx:
        sb = lambda n, s, d=F32: ctx.enter_context(nc.sbuf_tensor("f3_" + n, s, d))
        ps = lambda n, s, d=F32: ctx.enter_context(nc.psum_tensor("f3_" + n, s, d))
        sem = lambda n: g.semaphore(nc, ctx, "f3_" + n)
        ident16, mask16 = sb("ident16", [P, P], BF16), sb("mask16", [P, P], BF16)
        tokens, scaled, featuresT = sb("tokens", [P, TILES, D]), sb("scaled", [P, TILES, D]), sb("featuresT", [P, COLS])
        stats, moments = sb("stats", [P, TILES, 6]), sb("moments", [P, TILES, 2])
        power, rms, exponent = sb("power", [P, TILES]), sb("rms", [P, TILES]), sb("exponent", [P, TILES])
        scratch = sb("scratch", [P, 2])
        swapped = sb("swapped", [P, 2, COLS])
        latents = sb("latents", [P, COLS])
        queries, w_q = sb("queries", [P, PAIRS, COLS]), sb("w_q", [P, NH, HD])
        values = sb("values", [P, TILES, NH * PLAIN])
        minus_max, sums = sb("minus_max", [P, TILES, NH]), sb("sums", [P, TILES, NH])
        probs, probsT = sb("probs", [P, RING, WIDE]), sb("probsT", [P, 2, WIDE])
        mixed, mixedT = sb("mixed", [P, TILES, NH * PLAIN]), sb("mixedT", [P, TILES, 4, P])
        peak, total = sb("peak", [P, TILES]), sb("total", [P, TILES])
        top, chosen = sb("top", [P, TILES, 8]), sb("chosen", [P, TILES, E])
        odds, rest = sb("odds", [P, TILES, E + 6]), sb("rest", [P, TILES, E + 6])
        gate, hidden = sb("gate", [P, 2, COLS]), sb("hidden", [P, GROUPS, COLS])
        ps_s, ps_pT = ps("ps_s", [P, RING, 512]), ps("ps_pT", [P, 2, 512])
        ps_o, ps_y = ps("ps_o", [P, 2, 512]), ps("ps_y", [P, TILES, D])
        ps_t = ps_s[:, 2, :]
        ps_flat = ps_y[:, :, :].rearrange("p j d -> p (j d)")
        items = [(n // 4, n // 2 % 2, n % 2) for n in range(ITEMS)]
        out_of = lambda p: ps_o[:, p % 2, 0:TILES * 2 * PLAIN].rearrange("p (j i d) -> p j i d", j=TILES, i=2)
        ps_router = ps_o[:, 0, 0:TILES * E].rearrange("p (j e) -> p j e", j=TILES)
        pair_banks = (ps_s[:, 0:2, :], ps_pT[:, :, :])
        down_banks = (ps_y[:, :, :], ps_t.rearrange("p (j d) -> p j d", j=TILES))
        (const_ready, padded, power_ready, rms_ready, scaled_ready, xT_made, features_ready, projected, turned,
         rotated, w_made, w_ready, v_made, v_ready, scored, max_ready, exped, pT_made, pT_ready, pv_made) = (
            sem(n) for n in ("const_ready", "padded", "power_ready", "rms_ready", "scaled_ready", "xT_made",
                             "features_ready", "projected", "turned", "rotated", "w_made", "w_ready", "v_made", "v_ready",
                             "scored", "max_ready", "exped", "pT_made", "pT_ready", "pv_made"))
        (mixed_ready, mT_made, mT_ready, y_made, routed, shifted, odds_ready, gu_made, silu_ready, h_ready,
         down_made, summed, added, steps, pool_steps) = (
            sem(n) for n in ("mixed_ready", "mT_made", "mT_ready", "y_made", "routed", "shifted", "odds_ready", "gu_made",
                             "silu_ready", "h_ready", "down_made", "summed", "added", "steps", "pool_steps"))
        block = ctx.enter_context(nc.Block())
        per_token = lambda a: a[:, :].rearrange("p (j o) -> p j o", o=1).broadcast_to([P, TILES, E])
        by_seq = lambda a: a.rearrange("p (s t) -> p s t", s=SEQS)
        table = lambda m: w[m].rearrange("p (o t) -> p o t", o=1).broadcast_to([P, SEQS, T])
        SWAP = [i ^ 1 for i in range(32)]
        turns_of = [("_k", latents[:, :], ps_pT[:, 0, :])] + [("_q", queries[:, p, :], ps_flat) for p in range(PAIRS)]
        ROT = len(turns_of)
        AHEAD = 2
        experts_of = [[e for e in (2 * q, 2 * q + 1) if e < EXPERTS] for q in range(GROUPS)]

        @block.gpsimd
        def _(pool):
            pool.wait_ge(g.loaded["L3_ffn"], 16)
            pool.memset(exponent[:, :], -0.5).then_inc(const_ready, 1)
            pool.wait_ge(const_ready, 1)
            with pool.Fori(0, TURNS) as t:
                step = Chain(pool, pool_steps, t, ROT + 2)

                def root_mean_square(k):
                    pool.wait_ge(power_ready, t * 2 + k + 1)
                    step(pool.tensor_tensor(rms[:, :], power[:, :], g.eps.broadcast_to([P, TILES]), ALU.add))
                    pool.tensor_tensor(rms[:, :], rms[:, :], exponent[:, :], ALU.pow).then_inc(rms_ready, 1)

                root_mean_square(0)
                for k, (which, dst, _) in enumerate(turns_of):
                    pool.wait_ge(turned, t * ROT + k + 1)
                    part = swapped[:, k % 2, :]
                    step(pool.tensor_tensor(by_seq(part), by_seq(part), table("sin" + which), ALU.mult))
                    pool.tensor_tensor(dst, dst, part, ALU.add).then_inc(rotated, 1)
                root_mean_square(1)
                step.end()

        @block.vector
        def _(v):
            v.wait_ge(g.loaded["L3_ffn"], 16)
            v.tensor_copy(ident16[:, :], g.ident)
            v.tensor_copy(mask16[:, :], w["mask"])
            v.memset(odds[:, :, E:E + 6], -1.0).then_inc(padded, 1)
            v.wait_ge(padded, 1)
            v.memset(w_q[:, :, LATENTS:PLAIN], 0.0)
            v.tensor_copy(w_q[:, :, PLAIN:HD], w["q"].rearrange("p (h d) -> p h d", h=NH)[:, :, PLAIN:HD])
            v.wait_ge(w_made, 4)
            v.tensor_copy(w_q[:, :, 0:LATENTS], ps_o[:, 0, 0:NH * LATENTS].rearrange("p (h r) -> p h r", h=NH)).then_inc(w_ready, 1)

            def scale_tokens(t, step, k, weight):
                for j in range(TILES):
                    last = v.bn_stats(stats[:, j, :], tokens[:, j, :])
                step(last)
                v.memset(scratch[:, k:k + 1], 0.0)
                for j in range(TILES):
                    last = v.bn_aggr(moments[:, j, :], stats[:, j, :])
                step(last)
                step(v.tensor_tensor(power[:, :], moments[:, :, 0], moments[:, :, 0], ALU.mult))
                v.tensor_tensor(power[:, :], power[:, :], moments[:, :, 1], ALU.add).then_inc(power_ready, 1)
                v.wait_ge(rms_ready, t * 2 + k + 1)
                for j in range(TILES):
                    last = v.tensor_scalar(scaled[:, j, :], tokens[:, j, :], rms[:, j:j + 1], None, ALU.mult)
                last.then_inc(scaled_ready, 1)
                v.wait_ge(xT_made, t * 2 + k + 1)
                v.tensor_scalar(featuresT[:, :], ps_t, w[weight], None, ALU.mult).then_inc(features_ready, 1)

            with v.Fori(0, TURNS) as t:
                step = Chain(v, steps, t, 2 * 3 + PAIRS + TOP_TWO_STEPS + 8)
                step(normalise(v, g, t, tokens))
                scale_tokens(t, step, 0, "ln1")

                def rotate(k):
                    which, dst, src = turns_of[k]
                    v.wait_ge(projected, t * ROT + k + 1)
                    v.wait_ge(rotated, t * ROT + max(k - 1, 0))
                    v.tensor_tensor(by_seq(dst), by_seq(src), table("cos" + which), ALU.mult)
                    v.stream_shuffle(swapped[:, k % 2, :], src, SWAP).then_inc(turned, 1)

                def normalise_pair(p):
                    v.wait_ge(pv_made, t * ITEMS + 4 * (p + 1))
                    of_pair = sums[:, :, 2 * p:2 * p + 2]
                    step(v.reciprocal(of_pair, of_pair))
                    v.tensor_tensor(mixed[:, :, 2 * p * PLAIN:(2 * p + 2) * PLAIN].rearrange("p j (i d) -> p j i d", i=2), out_of(p),
                                    of_pair.rearrange("p j (i o) -> p j i o", o=1).broadcast_to([P, TILES, 2, PLAIN]), ALU.mult)\
                        .then_inc(mixed_ready, 1)

                for k in range(AHEAD + 1):
                    rotate(k)
                for i in range(ITEMS + 3):
                    if i < ITEMS:
                        p, s, of_pair = items[i]
                        h, j = 2 * p + of_pair, s * HALVES
                        v.wait_ge(scored, t * ITEMS + i + 1)
                        v.tensor_reduce(minus_max[:, j, h:h + 1], ps_s[:, i % RING, 0:P], AX.X, ALU.max, negate=True)
                        v.tensor_reduce(minus_max[:, j + 1, h:h + 1], ps_s[:, i % RING, P:WIDE], AX.X, ALU.max, negate=True)\
                            .then_inc(max_ready, 1)
                    if 2 <= i < ITEMS + 2:
                        n = i - 2
                        v.wait_ge(pT_made, t * ITEMS + n + 1)
                        v.wait_ge(pv_made, t * ITEMS + max(n - 1, 0))
                        v.tensor_copy(probsT[:, n % 2, :], ps_pT[:, n % 2, 0:WIDE]).then_inc(pT_ready, 1)
                    if i % 4 == 2 and i // 4 + AHEAD < PAIRS:
                        rotate(1 + i // 4 + AHEAD)
                    if i >= 6 and i % 4 == 2:
                        normalise_pair(i // 4 - 1)
                v.wait_ge(y_made, t + 1)
                step(v.tensor_tensor(tokens[:, :, :], tokens[:, :, :], ps_y[:, :, :], ALU.add))
                scale_tokens(t, step, 1, "ln2")
                v.wait_ge(routed, t + 1)
                step(v.tensor_reduce(peak[:, :], ps_router, AX.X, ALU.max))
                v.tensor_tensor(odds[:, :, 0:E], ps_router, per_token(peak), ALU.subtract).then_inc(shifted, 1)
                v.wait_ge(odds_ready, t + 1)
                step(v.tensor_reduce(total[:, :], odds[:, :, 0:E], AX.X, ALU.add))
                step(v.reciprocal(total[:, :], total[:, :]))
                step(v.tensor_tensor(odds[:, :, 0:E], odds[:, :, 0:E], per_token(total), ALU.mult))
                top_two(v, step, scratch, odds, top, rest, chosen)
                step(v.tensor_reduce(peak[:, :], chosen[:, :, :], AX.X, ALU.add))
                step(v.reciprocal(peak[:, :], peak[:, :]))
                v.tensor_tensor(chosen[:, :, :], chosen[:, :, :], per_token(peak), ALU.mult)
                for q in range(GROUPS + 1):
                    if q < GROUPS:
                        rows = HIDDEN * len(experts_of[q])
                        v.wait_ge(silu_ready, t * GROUPS + q + 1)
                        v.tensor_tensor(hidden[0:rows, q, :], gate[0:rows, q % 2, :], pair_banks[q % 2][0:rows, 1, :], ALU.mult)\
                            .then_inc(h_ready, 1)
                    for e in experts_of[q - 1] if q else ():
                        v.wait_ge(down_made, t * EXPERTS + e + 1)
                        v.wait_ge(summed, t * EXPERTS + e)
                        if e < E:
                            for j in range(TILES):
                                last = v.scalar_tensor_tensor(tokens[:, j, :], down_banks[e % 2][:, j, :], chosen[:, j, e:e + 1],
                                                              tokens[:, j, :], ALU.mult, ALU.add)
                        else:
                            last = v.tensor_tensor(tokens[:, :, :], tokens[:, :, :], down_banks[e % 2], ALU.add)
                        last.then_inc(summed, 1)
                v.wait_ge(summed, (t + 1) * EXPERTS)
                v.tensor_tensor(tiles_of(g.x, t), tiles_of(g.x, t), tokens[:, :, :], ALU.add).then_inc(added, 1)
                v.wait_ge(added, t + 1)
                step.end()

        @block.tensor
        def _(pe):
            pe.wait_ge(g.loaded["L3_ffn"], 16)
            pe.wait_ge(padded, 1)
            for j in range(4):
                rows = slice(PLAIN * j, PLAIN * (j + 1))
                for c in range(NH // 4):
                    h = 4 * c + j
                    last = pe.matmul(ps_o[:, 0, h * LATENTS:(h + 1) * LATENTS], w["q_plainT"][rows, c * P:(c + 1) * P],
                                     w["kvbT"][rows, c * LATENTS:(c + 1) * LATENTS], start=True, stop=True)
                last.then_inc(w_made, 1)
                pe.wait_ge(w_made, j + 1)
            pe.wait_ge(w_ready, 1)
            with pe.Fori(0, TURNS) as t:
                def transpose_tokens(k):
                    pe.wait_ge(scaled_ready, t * 2 + k + 1)
                    for j in range(TILES):
                        last = pe.transpose(ps_t[:, j * P:(j + 1) * P], scaled[:, j, :], g.ident)
                    last.then_inc(xT_made, 1)
                    pe.wait_ge(features_ready, t * 2 + k + 1)

                pe.wait_ge(summed, t * EXPERTS)
                transpose_tokens(0)
                pe.matmul(ps_pT[:, 0, :], w["kva"], featuresT[:, :], start=True, stop=True).then_inc(projected, 1)

                def project_pair(p):
                    if p > 0:
                        pe.wait_ge(turned, t * ROT + p + 1)
                    pe.matmul(ps_flat, w_q[:, 2 * p:2 * p + 2, :].rearrange("p h d -> p (h d)"), featuresT[:, :],
                              start=True, stop=True).then_inc(projected, 1)

                for p in range(AHEAD):
                    project_pair(p)
                pe.wait_ge(rotated, t * ROT + 1)
                for j in range(TILES):
                    if j >= 2:
                        pe.wait_ge(v_ready, t * TILES + j - 1)
                    pe.matmul(ps_o[:, j % 2, :], latents[0:LATENTS, j * P:(j + 1) * P], w["kvb"], start=True, stop=True)\
                        .then_inc(v_made, 1)

                def score(i):
                    p, s, of_pair = items[i]
                    if i >= RING:
                        pe.wait_ge(exped, t * ITEMS + i - RING + 1)
                    rows = slice(HD * of_pair, HD * (of_pair + 1))
                    out, at = ps_s[:, i % RING, :], s * T
                    q = lambda half: queries[rows, p, at + half * P:at + (half + 1) * P]
                    k = lambda n: latents[rows, at:at + n]
                    pe.matmul(out[:, 0:P], q(0), k(P), start=True, stop=False)
                    pe.matmul(out[:, 0:P], ident16[:, :], mask16[:, :], start=False, stop=True)
                    pe.matmul(out[:, P:WIDE], q(1), k(T), start=True, stop=False)
                    pe.matmul(out[:, T:WIDE], ident16[:, :], mask16[:, :], start=False, stop=True).then_inc(scored, 1)

                def turn_probs(n):
                    pe.wait_ge(exped, t * ITEMS + n + 1)
                    if n >= 2:
                        pe.wait_ge(pT_ready, t * ITEMS + n - 1)
                    for at in (0, P, T):
                        last = pe.transpose(ps_pT[:, n % 2, at:at + P], probs[:, n % RING, at:at + P], g.ident)
                    last.then_inc(pT_made, 1)

                def weigh(n):
                    p, s, of_pair = items[n]
                    h = 2 * p + of_pair
                    pe.wait_ge(pT_ready, t * ITEMS + n + 1)
                    if n % 4 == 0 and p >= 2:
                        pe.wait_ge(mixed_ready, t * PAIRS + p - 1)
                    val = lambda half: values[:, s * HALVES + half, h * PLAIN:(h + 1) * PLAIN]
                    out = lambda half: out_of(p)[:, s * HALVES + half, of_pair, :]
                    pr = lambda at: probsT[:, n % 2, at:at + P]
                    pe.matmul(out(0), pr(0), val(0), start=True, stop=True)
                    pe.matmul(out(1), pr(P), val(0), start=True, stop=False)
                    pe.matmul(out(1), pr(T), val(1), start=False, stop=True).then_inc(pv_made, 1)

                for i in range(ITEMS + 3):
                    if i < ITEMS:
                        if i % 4 == 0:
                            pe.wait_ge(rotated, t * ROT + i // 4 + 2)
                        score(i)
                        if i % 4 == 1 and i // 4 + AHEAD < PAIRS:
                            project_pair(i // 4 + AHEAD)
                    if 2 <= i < ITEMS + 2:
                        turn_probs(i - 2)
                    if i == 3:
                        pe.wait_ge(v_ready, (t + 1) * TILES)
                    if i >= 3:
                        weigh(i - 3)
                pe.wait_ge(mixed_ready, (t + 1) * PAIRS)
                for j in range(TILES + 1):
                    if j < TILES:
                        if j >= RING:
                            pe.wait_ge(mT_ready, t * TILES + j - RING + 1)
                        for c in range(4):
                            last = pe.transpose(ps_s[:, j % RING, c * P:(c + 1) * P], mixed[:, j, c * P:(c + 1) * P], g.ident)
                        last.then_inc(mT_made, 1)
                    if j > 0:
                        pe.wait_ge(mT_ready, t * TILES + j)
                        for c in range(4):
                            last = pe.matmul(ps_y[:, j - 1, :], mixedT[:, j - 1, c, :], w["o"][:, c * P:(c + 1) * P],
                                             start=c == 0, stop=c == 3)
                last.then_inc(y_made, 1)

                transpose_tokens(1)
                for j in range(TILES):
                    pe.matmul(ps_router[:, j, :], featuresT[:, j * P:(j + 1) * P], w["router"], start=True, stop=False)
                    last = pe.matmul(ps_router[:, j, :], g.ones[0:1, 0:P], w["router_b"], start=False, stop=True)
                last.then_inc(routed, 1)
                for q in range(GROUPS + 1):
                    if q < GROUPS:
                        if q >= 2:
                            pe.wait_ge(h_ready, t * GROUPS + q - 1)
                        rows = HIDDEN * len(experts_of[q])
                        for i, m in enumerate(("gate", "up")):
                            last = pe.matmul(pair_banks[q % 2][0:rows, i, :], w[m][:, q * P:q * P + rows], featuresT[:, :],
                                             start=True, stop=True)
                        last.then_inc(gu_made, 1)
                    for e in experts_of[q - 1] if q else ():
                        pe.wait_ge(h_ready, t * GROUPS + q)
                        if e >= 2:
                            pe.wait_ge(summed, t * EXPERTS + e - 1)
                        rows = slice(HIDDEN * (e % 2), HIDDEN * (e % 2) + HIDDEN)
                        for j in range(TILES):
                            last = pe.matmul(down_banks[e % 2][:, j, :], hidden[rows, e // 2, j * P:(j + 1) * P],
                                             w["down"][rows, e // 2 * P:(e // 2 + 1) * P], start=True, stop=True)
                        last.then_inc(down_made, 1)

        @block.scalar
        def _(a):
            with a.Fori(0, TURNS) as t:
                for j in range(TILES):
                    a.wait_ge(v_made, t * TILES + j + 1)
                    a.activation(values[:, j, :], ps_o[:, j % 2, :], ACT.Copy).then_inc(v_ready, 1)
                for i in range(ITEMS):
                    p, s, of_pair = items[i]
                    h = 2 * p + of_pair
                    a.wait_ge(max_ready, t * ITEMS + i + 1)
                    if i >= RING:
                        a.wait_ge(pT_made, t * ITEMS + i - RING + 1)
                    for half, (at, n) in enumerate(((0, P), (P, T))):
                        last = a.activation(probs[:, i % RING, at:at + n], ps_s[:, i % RING, at:at + n], ACT.Exp,
                                            bias=minus_max[:, s * HALVES + half, h:h + 1],
                                            accum_out=sums[:, s * HALVES + half, h:h + 1])
                    last.then_inc(exped, 1)
                for j in range(TILES):
                    a.wait_ge(mT_made, t * TILES + j + 1)
                    a.activation(mixedT[:, j, :, :].rearrange("p c n -> p (c n)"), ps_s[:, j % RING, :], ACT.Copy).then_inc(mT_ready, 1)
                a.wait_ge(shifted, t + 1)
                a.activation(odds[:, :, 0:E], odds[:, :, 0:E], ACT.Exp).then_inc(odds_ready, 1)
                for q in range(GROUPS):
                    rows = HIDDEN * len(experts_of[q])
                    a.wait_ge(gu_made, t * GROUPS + q + 1)
                    if q >= 2:
                        a.wait_ge(h_ready, t * GROUPS + q - 1)
                    a.activation(gate[0:rows, q % 2, :], pair_banks[q % 2][0:rows, 0, :], ACT.Silu).then_inc(silu_ready, 1)
LAYERS = {
    "L0_attn": layer0_attention, "L0_xattn": layer0_mlstm, "L0_ffn": layer0_ternary_ffn,
    "L1_attn": layer1_state_space, "L1_xattn": layer1_attention, "L1_ffn": layer1_trees,
    "L2_attn": layer2_attention, "L2_xattn": layer2_masked_attention, "L2_ffn": layer2_experts,
    "L3_attn": layer3_latent_attention, "L3_xattn": layer3_block, "L3_ffn": layer3_rotary_experts,
}
LAYER_NAMES = list(LAYERS)



def layouts(a):
    f = np.float32
    col = lambda x: np.asarray(x).reshape(-1, P).T
    row = lambda x: np.broadcast_to(np.asarray(x).reshape(1, -1), (P, np.asarray(x).size))
    i = np.arange(P)
    starts = np.ones((P, 4 * T), f)
    starts[:, ::T] = 0
    out = {}
    out["shared"] = {
        "eps": np.full((P, 1), LN_EPS, f),
        "ones": np.ones((P, P), f),
        "ident": np.eye(P, dtype=f),
        "head_blocks": (i[:, None] // 8 == i[None, :] // 8).astype(f),
        "seq_starts": starts,
    }
    qkv = a["L0_attn_w_qkv"]
    out["L0_attn"] = {
        "wq": qkv[0:P], "wk": qkv[P:2 * P], "wvT": qkv[2 * P:].T, "woT": a["L0_attn_w_out"].T,
        "code": a["L0_attn_fc_code"][0].transpose(0, 2, 1).reshape(P, 2),
    }
    ig, fg = a["L0_xattn_igate_kernel"], a["L0_xattn_fgate_kernel"]
    floor = np.zeros((4, COLS), f)
    floor[:, ::T] = -1e30
    out["L0_xattn"] = {
        "ix": ig[0:P], "ik": ig[P:2 * P], "iv": ig[2 * P:], "fx": fg[0:P], "fk": fg[P:2 * P], "fv": fg[2 * P:],
        "ibias": a["L0_xattn_igate_bias"].reshape(-1, 1), "fbias": a["L0_xattn_fgate_bias"].reshape(-1, 1),
        "rms": row(a["L0_xattn_rms_scale"]), "seq_floor": floor,
        "causalT": np.where(i[:, None] <= i[None, :], 0, -1e30).astype(f),
        "minus_head": -np.repeat(np.eye(4, dtype=f), P, axis=1), "rms_eps": np.full((P, 1), 1e-6, f),
    }
    out["L0_ffn"] = {
        "fcT": a["L0_ffn_W_fc"].T, "projT": a["L0_ffn_W_proj"].reshape(P, 4, P).transpose(2, 1, 0).reshape(P, 512),
        "ln_w": col(a["L0_ffn_ln_w"]), "ln_b": col(a["L0_ffn_ln_b"]),
    }
    in_w, out_w = a["L1_attn_in_w"], a["L1_attn_out_w"]
    one = lambda name: a[name].reshape(-1, 1)
    line = lambda name: a[name].reshape(1, -1)
    out["L1_attn"] = {
        "norm_w": one("L1_attn_norm_w"), "norm_b": one("L1_attn_norm_b"), "in_xT": in_w[0:P].T, "in_zT": in_w[P:].T,
        "in_b": col(a["L1_attn_in_b"]), "conv_w": a["L1_attn_conv_w"][:, 0, :], "conv_b": one("L1_attn_conv_b"),
        "dtT": a["L1_attn_dt_w"].T, "dt_b": one("L1_attn_dt_b"), "bT": a["L1_attn_b_w"].T, "b_b": one("L1_attn_b_b"),
        "cT": a["L1_attn_c_w"].T, "c_b": one("L1_attn_c_b"), "a_log": one("L1_attn_a_log"), "d": one("L1_attn_d"),
        "outT": out_w[:, 0:P].T, "out_yT": out_w[:, P:].T, "out_b": line("L1_attn_out_b"),
    }
    def for_stacks(x):
        x = np.asarray(x)
        return x.reshape(x.shape[0], 8, 2, 8).transpose(0, 2, 3, 1).reshape(x.shape[0], P)

    bias_cols = lambda x: for_stacks(np.asarray(x).reshape(1, -1)).T
    none = np.zeros(P, f)
    q_i, k_i = i[:, None], i[None, :]
    hide = lambda seen: np.where(seen, 0, -1e30).astype(f)
    strict0, strict = (k_i < q_i) | ((q_i == 0) & (k_i == 0)), k_i < q_i
    out["L1_xattn"] = {
        "q": for_stacks(a["L1_xattn_Wq"]), "k": for_stacks(a["L1_xattn_Wk"]), "v": a["L1_xattn_Wv"],
        "q_bias": bias_cols(a["L1_xattn_bq"]), "k_bias": bias_cols(a["L1_xattn_bk"]), "v_bias": line("L1_xattn_bv"),
        "mask0": hide(strict0), "mask1": hide(strict), "mask0T": hide(strict0.T), "mask1T": hide(strict.T),
        "w1": a["L1_xattn_W1"], "b1": col(a["L1_xattn_b1"]),
        "w2": a["L1_xattn_W2"].reshape(4, P, P).transpose(1, 0, 2).reshape(P, 512), "out_b": line("L1_xattn_b2"),
    }

    def diagonal(m):
        full = np.zeros((P, P), f)
        for h in range(16):
            full[8 * h:8 * h + 8, 8 * h:8 * h + 8] = np.asarray(m).T
        return full

    out["L2_xattn"] = {
        "q": for_stacks(diagonal(a["L2_xattn_Wq"])), "k": for_stacks(diagonal(a["L2_xattn_Wk"])), "v": diagonal(a["L2_xattn_Wv"]),
        "q_bias": bias_cols(none), "k_bias": bias_cols(none), "out": a["L2_xattn_Wo"].T, "out_b": line("L2_xattn_bo"),
    }
    causal = k_i <= q_i
    out["L2_attn"] = {
        "wq": a["L2_attn_Wq"], "wk": a["L2_attn_Wk"], "wvT": a["L2_attn_Wv"].T, "wo": a["L2_attn_Wo"], "mask": hide(causal),
    }
    out["L3_attn"] = {
        "dq": a["L3_attn_W_dq"], "uqT": for_stacks(a["L3_attn_W_uq"].T), "uqT_plain": a["L3_attn_W_uq"].T,
        "dq_wide": for_stacks(a["L3_attn_W_dq"]), "uv": a["L3_attn_W_uv"], "oT": a["L3_attn_W_o"].T, "uk": a["L3_attn_W_uk"],
        "dkv": a["L3_attn_W_dkv"], "q_bias": bias_cols(none), "k_bias": bias_cols(none),
        "mask": hide(causal), "maskT": hide(causal.T),
    }
    ups = list(a["L2_ffn_rw1"]) + [a["L2_ffn_sw1"]]
    downs = list(a["L2_ffn_rw2"]) + [a["L2_ffn_sw2"]]
    out["L2_ffn"] = {
        "router": a["L2_ffn_router_w"], "router_b": line("L2_ffn_router_b"), "up": np.concatenate(ups, axis=1),
        "b1": np.concatenate([col(b) for b in list(a["L2_ffn_rb1"]) + [a["L2_ffn_sb1"]]], axis=1),
        "down": np.concatenate([m.reshape(2, P, P).transpose(1, 0, 2).reshape(P, 2 * P) for m in downs], axis=1),
        "shared_b2": line("L2_ffn_sb2"), "expert_b2": a["L2_ffn_rb2"],
    }
    key_index = np.arange(T)
    late = np.where(key_index[None, None, :] <= (np.arange(2)[None, :, None] * P + i[:, None, None]), 0, -1e30).astype(f)
    L3 = lambda n: a["L3_xattn_" + n]
    out["L3_xattn"] = {
        "q0": L3("Wq1"), "k0": L3("Wk1"), "v0": L3("Wv1"), "q1": L3("Wq2"), "k1": L3("Wk2"), "v1": L3("Wv2"),
        "fc1": L3("fc1_w"), "fc1_b": one("L3_xattn_fc1_b"), "fc2": L3("fc2_w"), "fc2_b": line("L3_xattn_fc2_b"),
        "gains": np.concatenate([row(L3("ln%d_g" % k)) for k in (1, 2, 3)], axis=1),
        "biases": np.concatenate([row(L3("ln%d_b" % k)) for k in (1, 2, 3)], axis=1),
        "key_index": row(key_index.astype(f)), "causal": late.reshape(P, 2 * T),
    }
    w_in = a["L1_ffn_W_in"].reshape(TREES, NODES, FAN, D)
    w_out = a["L1_ffn_W_out"].T.reshape(TREES, NODES, FAN, D)
    b_in = a["L1_ffn_b_in"].reshape(TREES, NODES, FAN)
    level = lambda m, d: m[:, ABOVE[d]:ABOVE[d] + FAN ** d].reshape(WIDTHS[d], -1)
    outs = []
    for d in (3, 2, 1, 0):
        m = level(w_out, d)
        for c in range(0, len(m), P):
            part = np.zeros((P, D), f)
            part[:len(m[c:c + P])] = m[c:c + P]
            outs.append(part)
    order = (3, 0, 1, 2)
    first_row = np.concatenate([np.tile(np.arange(TREES) * NODES + ABOVE[d], TILES) for d in range(DENSE, DEPTH + 1)])
    out["L1_ffn"] = {
        "in": np.concatenate([level(w_in, d).T for d in order], axis=1),
        "bias": row(np.concatenate([level(b_in, d).T for d in order], axis=1)),
        "out": np.concatenate(outs, axis=1), "ranks": row(np.tile(np.arange(FAN, 0, -1).astype(f), TILES * TREES)),
        "first_row": row(first_row.astype(f)),
    }
    kva, kvb = a["L3_ffn_Wkva"], a["L3_ffn_Wkvb"]
    latent, rope = kvb.shape[0], 32
    kva_wide = np.zeros((P, 2, 64), f)
    kva_wide[:, :, 0:latent], kva_wide[:, :, 32:64] = kva[:, None, 0:latent], kva[:, None, latent:]
    q_plainT = a["L3_ffn_Wq"].reshape(P, 4, 4, 64)[..., 0:32].transpose(2, 3, 1, 0)
    kvbT = kvb.reshape(latent, 4, 4, 32).transpose(2, 3, 1, 0)
    freqs = (1.0 / np.float32(100000.0) ** (np.arange(0, rope, 2, dtype=f) / rope)).astype(f)
    angle = np.outer(np.arange(T, dtype=f), freqs).astype(f).T
    cos, sin = np.ones((64, T), f), np.zeros((64, T), f)
    cos[32:] = np.repeat(np.cos(angle), 2, axis=0)
    sin[32:] = np.repeat(np.sin(angle), 2, axis=0) * np.tile([[-1], [1]], (rope // 2, 1))
    pairs = lambda m: np.concatenate(list(m), axis=1)
    L3f = lambda n: a["L3_ffn_" + n]
    downs3 = np.zeros((5, 2, 64, P), f)
    downs3.reshape(10, 64, P)[0:9] = list(L3f("Wd")) + list(L3f("sWd"))
    out["L3_ffn"] = {
        "q": L3f("Wq"), "kva": kva_wide.reshape(P, P), "kvb": kvb,
        "q_plainT": q_plainT.reshape(P, 4 * P), "kvbT": kvbT.reshape(P, 4 * latent),
        "cos_k": np.tile(cos, (2, 1)), "sin_k": np.tile(sin, (2, 1)),
        "cos_q": np.tile(cos, (2, 1)) / 8, "sin_q": np.tile(sin, (2, 1)) / 8, "mask": hide(causal),
        "o": L3f("Wo").reshape(16, 64, P)[:, 0:32].reshape(4, P, P).transpose(1, 0, 2).reshape(P, 512),
        "ln1": one("L3_ffn_w_ln1"), "ln2": one("L3_ffn_w_ln2"), "router": L3f("Wgate"), "router_b": line("L3_ffn_expert_bias"),
        "gate": pairs(list(L3f("Wg")) + list(L3f("sWg"))), "up": pairs(list(L3f("Wu")) + list(L3f("sWu"))),
        "down": downs3.reshape(5, P, P).transpose(1, 0, 2).reshape(P, 5 * P),
    }
    return out


def packed(parts):
    where, cols, at = {}, [], 0
    for name, p in parts.items():
        p = np.asarray(p)
        full = np.zeros((P, p.shape[1]), p.dtype)
        full[:p.shape[0]] = p
        where[name] = (p.shape[0], at, p.shape[1])
        cols.append(full)
        at += p.shape[1]
    return np.ascontiguousarray(np.concatenate(cols, axis=1)), where


def arrays_of(inputs, names):
    a = {k: np.asarray(v) for k, v in inputs.items()}
    arrays, where = {}, {}
    for name, parts in layouts(a).items():
        if name == "shared" or name in names:
            arrays["w_" + name], where[name] = packed(parts)
    ctx = a["ctx_1024"].reshape(NT, P, D)
    arrays["ctx"] = np.ascontiguousarray(ctx)
    arrays["ctxT"] = np.ascontiguousarray(ctx.reshape(NT * P, D).T)
    arrays["tree_table"] = np.ascontiguousarray(np.concatenate([
        a["L1_ffn_W_in"].reshape(TREES * NODES, FAN * D), a["L1_ffn_W_out"].T.reshape(TREES * NODES, FAN * D),
        a["L1_ffn_b_in"].reshape(TREES * NODES, FAN)], axis=1))
    mask = a["mask_Bx1xSxS2_ik1"].reshape(B, T, T)
    arrays["mask_qk"] = np.ascontiguousarray(mask.reshape(NT, P, T))
    arrays["mask_kq"] = np.ascontiguousarray(mask.transpose(0, 2, 1).reshape(NT, P, T))
    arrays["x"] = np.ascontiguousarray(a["x"].reshape(NT, P, D))
    return arrays, where


def program(nc, arrays, where, names):
    dram = {k: nc.dram_tensor(k, v.shape, mybir.dt.from_np(v.dtype), kind="ExternalInput").ap() for k, v in arrays.items()}
    out = nc.dram_tensor("out", (NT, P, D), F32, kind="ExternalOutput").ap()
    build(nc, dram, where, out, names)


class Shared:

    def __init__(self):
        self.semaphores = []

    def semaphore(self, nc, ctx, name):
        s = ctx.enter_context(nc.semaphore(name))
        self.semaphores.append(s)
        return s


def build(nc, dram, where, out, names):
    with ExitStack() as ctx:
        g = Shared()
        g.x = ctx.enter_context(nc.sbuf_tensor("x_tokens", [P, NT, D], F32))
        g.x_loaded = ctx.enter_context(nc.semaphore("x_loaded"))
        g.gathered = [ctx.enter_context(nc.semaphore(f"gathered{j}")) for j in range(TILES)]
        first_stats = ctx.enter_context(nc.semaphore("first_stats"))
        stored = ctx.enter_context(nc.semaphore("stored"))
        tiles, g.loaded, weights = {}, {}, {}
        width = lambda name: dram["w_" + name].shape[1]
        slots = [ctx.enter_context(nc.sbuf_tensor(f"weights{k}", [P, max(map(width, names[k::2]), default=1)], F32))
                 for k in range(2)]
        shared_sb = ctx.enter_context(nc.sbuf_tensor("shared_sb", [P, width("shared")], F32))
        for name, parts in where.items():
            tiles[name] = shared_sb if name == "shared" else slots[names.index(name) % 2]
            g.loaded[name] = ctx.enter_context(nc.semaphore("loaded_" + name))
            weights[name] = {k: tiles[name][0:r, c:c + n] for k, (r, c, n) in parts.items()}
        g.ident, g.head_blocks, g.seq_starts = (weights["shared"][k] for k in ("ident", "head_blocks", "seq_starts"))
        g.eps, g.ones = weights["shared"]["eps"], weights["shared"]["ones"]
        g.x_stats = ctx.enter_context(nc.sbuf_tensor("x_stats", [P, NT, 6], F32))
        g.moments = ctx.enter_context(nc.sbuf_tensor("moments", [P, NT, 2], F32))
        g.rstd = ctx.enter_context(nc.sbuf_tensor("rstd", [P, NT], F32))
        g.tree_table = dram["tree_table"]
        g.mask_qk, g.mask_kq = dram["mask_qk"], dram["mask_kq"]
        g.ctx = ctx.enter_context(nc.sbuf_tensor("ctx_tokens", [P, NT, D], F32))
        g.ctxT = ctx.enter_context(nc.sbuf_tensor("ctx_features", [P, NT * P], F32))
        g.loaded["context"] = ctx.enter_context(nc.semaphore("loaded_context"))
        def load(sp, name):
            sp.dma_start(tiles[name][:, 0:width(name)], dram["w_" + name]).then_inc(g.loaded[name], 16)

        with nc.Block() as block:
            @block.sync
            def _(sp):
                sp.dma_start(tiles["shared"][:, :], dram["w_shared"]).then_inc(g.loaded["shared"], 16)
                sp.dma_start(g.x[:, :, :], dram["x"].rearrange("n p d -> p n d")).then_inc(g.x_loaded, 16)
                sp.dma_start(g.ctx[:, :, :], dram["ctx"].rearrange("n p d -> p n d")).then_inc(g.loaded["context"], 16)
                sp.dma_start(g.ctxT[:, :], dram["ctxT"]).then_inc(g.loaded["context"], 16)
                load(sp, names[0])

            @block.vector
            def _(v):
                v.wait_ge(g.x_loaded, 16)
                for n in range(NT):
                    last = v.bn_stats(g.x_stats[:, n, :], g.x[:, n, :])
                last.then_inc(first_stats, 1)
                v.wait_ge(first_stats, 1)

            @block.scalar
            def _(a):
                a.wait_ge(g.loaded["shared"], 16)

        for i, name in enumerate(names):
            measure_tokens(nc, g, name, lambda sp: load(sp, names[i + 1]) if i + 1 < len(names) else None)
            LAYERS[name](nc, g, weights[name])
        with nc.Block() as block:
            @block.sync
            def _(sp):
                sp.dma_start(out.rearrange("n p d -> p n d"), g.x[:, :, :]).then_inc(stored, 16)
                sp.wait_ge(stored, 16)


def result(out):
    return out.reshape(B, T, D)


def kernel(**inputs):
    import concourse.bacc as bacc
    from concourse.bass_utils import run_bass_kernel_spmd

    nc = bacc.Bacc("TRN2", target_bir_lowering=False, num_devices=1)
    arrays, where = arrays_of(inputs, LAYER_NAMES)
    program(nc, arrays, where, LAYER_NAMES)
    r = run_bass_kernel_spmd(nc, [arrays], core_ids=[0])
    return result(r.results[0]["out"])
```
